# Optimizing a Trainium2 kernel written in Bass

```python
import numpy as np
import jax
import jax.numpy as jnp

def _softmax(x, axis=-1):
    return jax.nn.softmax(x, axis=axis)

def _gelu(x):
    return jax.nn.gelu(x, approximate=True)

def _silu(x):
    return jax.nn.silu(x)

def _sigmoid(x):
    return jax.nn.sigmoid(x)

def _layernorm(x, axis=-1, eps=1e-05):
    m = jnp.mean(x, axis=axis, keepdims=True)
    v = jnp.var(x, axis=axis, keepdims=True)
    return (x - m) / jnp.sqrt(v + eps)

def _scatter_add(tgt, idx, src, axis=0):
    return tgt.at[idx].add(src)

def _segment_sum(src, seg, n):
    return jax.ops.segment_sum(src, seg, n)
kernel_name = 'mk_lm_tower_d1_tok_ids1024_r4_4f51e9'

def setup_inputs(seed: int=0):
    np.random.seed(seed)
    _w = jnp.asarray

    def _rec_inputs():
        import jax
        import jax.numpy as jnp
        _rk = jax.random.key(seed)
        x = jax.random.randint(jax.random.fold_in(_rk, 1), (8, 256), 0, 200, jnp.int32)
        return x
    x = _rec_inputs()

    def _L0_tok_setup():
        import jax, jax.numpy as jnp
        import numpy as np
        NUM_LEVELS = 32
        SCALE = 0.15
        OPEN_TOKENS = jnp.array([40, 91, 123], dtype=jnp.int32)
        CLOSE_TOKENS = jnp.array([41, 93, 125], dtype=jnp.int32)

        def _compute_levels(token_ids, num_levels):
            is_open = (token_ids[..., None] == OPEN_TOKENS).any(-1)
            is_close = (token_ids[..., None] == CLOSE_TOKENS).any(-1)
            delta = is_open.astype(jnp.int32) - is_close.astype(jnp.int32)

            def step(lvl, d):
                lvl = jnp.clip(lvl + d, 0, num_levels - 1)
                return (lvl, lvl)
            init = jnp.zeros(token_ids.shape[0], dtype=jnp.int32)
            _, levels = jax.lax.scan(step, init, delta.T)
            return levels.T
        key = jax.random.key(seed)
        k1, k2 = jax.random.split(key)
        token_ids = jax.random.randint(k1, (8, 2048), 0, 200, dtype=jnp.int32)
        level_emb = jax.random.normal(k2, (NUM_LEVELS, 256), dtype=jnp.float32)
        return {'token_ids': token_ids, 'level_emb': level_emb}
    _L0_tok_all = _L0_tok_setup()
    _L0_tok_in = {k: v for k, v in _L0_tok_all.items() if k in ('level_emb',)}
    del _L0_tok_all

    def _L0_attn_setup():
        import jax, jax.numpy as jnp
        import numpy as np
        import math
        D_MODEL = 256
        NUM_HEADS = 16
        D_K = D_MODEL // NUM_HEADS
        MAX_LEN = 512
        B, S = (2, 256)
        key = jax.random.key(seed)
        ks = jax.random.split(key, 10)
        lin_scale = 1.0 / math.sqrt(D_MODEL)
        Wq = jax.random.uniform(ks[0], (D_MODEL, D_MODEL), jnp.float32, -lin_scale, lin_scale)
        Wk = jax.random.uniform(ks[1], (D_MODEL, D_MODEL), jnp.float32, -lin_scale, lin_scale)
        Wv = jax.random.uniform(ks[2], (D_MODEL, D_MODEL), jnp.float32, -lin_scale, lin_scale)
        Wo = jax.random.uniform(ks[3], (D_MODEL, D_MODEL), jnp.float32, -lin_scale, lin_scale)
        bq = jnp.zeros((D_MODEL,), jnp.float32)
        bk = jnp.zeros((D_MODEL,), jnp.float32)
        bv = jnp.zeros((D_MODEL,), jnp.float32)
        bo = jnp.zeros((D_MODEL,), jnp.float32)
        er_bound = math.sqrt(6.0 / (MAX_LEN + D_K))
        Er = jax.random.uniform(ks[4], (MAX_LEN, D_K), jnp.float32, -er_bound, er_bound)
        x = jax.random.normal(ks[5], (B, S, D_MODEL), jnp.float32)
        return {'x': x, 'Wq': Wq, 'bq': bq, 'Wk': Wk, 'bk': bk, 'Wv': Wv, 'bv': bv, 'Wo': Wo, 'bo': bo, 'Er': Er}
    _L0_attn_all = _L0_attn_setup()
    _L0_attn_in = {k: v for k, v in _L0_attn_all.items() if k in ('Wq', 'bq', 'Wk', 'bk', 'Wv', 'bv', 'Wo', 'bo', 'Er')}
    del _L0_attn_all

    def _L0_ffn_setup():
        import jax, jax.numpy as jnp
        import numpy as np
        D_MODEL = 256
        N_HEADS = 16
        D_HEAD = D_MODEL // N_HEADS
        N_EXPERTS = 8
        TOP_K = 2
        D_FF = 512
        EPS = 1e-06

        def rmsnorm(x, w):
            return x * jax.lax.rsqrt(jnp.mean(x * x, axis=-1, keepdims=True) + EPS) * w

        def swiglu(x, w_gate, w_up, w_down):
            return jax.nn.silu(x @ w_gate) * (x @ w_up) @ w_down
        key = jax.random.key(seed)
        ks = jax.random.split(key, 16)
        s = 0.02
        B, S = (2, 512)
        return {'X': jax.random.normal(ks[0], (B, S, D_MODEL), dtype=jnp.float32), 'norm1_w': jnp.ones((D_MODEL,), jnp.float32), 'norm2_w': jnp.ones((D_MODEL,), jnp.float32), 'wq': jax.random.normal(ks[1], (D_MODEL, D_MODEL), jnp.float32) * s, 'wk': jax.random.normal(ks[2], (D_MODEL, D_MODEL), jnp.float32) * s, 'wv': jax.random.normal(ks[3], (D_MODEL, D_MODEL), jnp.float32) * s, 'wo': jax.random.normal(ks[4], (D_MODEL, D_MODEL), jnp.float32) * s, 'router_w': jax.random.normal(ks[5], (D_MODEL, N_EXPERTS), jnp.float32) * s, 'sh_gate': jax.random.normal(ks[6], (D_MODEL, D_FF), jnp.float32) * s, 'sh_up': jax.random.normal(ks[7], (D_MODEL, D_FF), jnp.float32) * s, 'sh_down': jax.random.normal(ks[8], (D_FF, D_MODEL), jnp.float32) * s, 'e_gate': jax.random.normal(ks[9], (N_EXPERTS, D_MODEL, D_FF), jnp.float32) * s, 'e_up': jax.random.normal(ks[10], (N_EXPERTS, D_MODEL, D_FF), jnp.float32) * s, 'e_down': jax.random.normal(ks[11], (N_EXPERTS, D_FF, D_MODEL), jnp.float32) * s}
    _L0_ffn_all = _L0_ffn_setup()
    _L0_ffn_in = {k: v for k, v in _L0_ffn_all.items() if k in ('norm1_w', 'norm2_w', 'wq', 'wk', 'wv', 'wo', 'router_w', 'sh_gate', 'sh_up', 'sh_down', 'e_gate', 'e_up', 'e_down')}
    del _L0_ffn_all
    return {'x': x, 'L0_tok_level_emb': _L0_tok_in['level_emb'], 'L0_attn_Wq': _L0_attn_in['Wq'], 'L0_attn_bq': _L0_attn_in['bq'], 'L0_attn_Wk': _L0_attn_in['Wk'], 'L0_attn_bk': _L0_attn_in['bk'], 'L0_attn_Wv': _L0_attn_in['Wv'], 'L0_attn_bv': _L0_attn_in['bv'], 'L0_attn_Wo': _L0_attn_in['Wo'], 'L0_attn_bo': _L0_attn_in['bo'], 'L0_attn_Er': _L0_attn_in['Er'], 'L0_ffn_norm1_w': _L0_ffn_in['norm1_w'], 'L0_ffn_norm2_w': _L0_ffn_in['norm2_w'], 'L0_ffn_wq': _L0_ffn_in['wq'], 'L0_ffn_wk': _L0_ffn_in['wk'], 'L0_ffn_wv': _L0_ffn_in['wv'], 'L0_ffn_wo': _L0_ffn_in['wo'], 'L0_ffn_router_w': _L0_ffn_in['router_w'], 'L0_ffn_sh_gate': _L0_ffn_in['sh_gate'], 'L0_ffn_sh_up': _L0_ffn_in['sh_up'], 'L0_ffn_sh_down': _L0_ffn_in['sh_down'], 'L0_ffn_e_gate': _L0_ffn_in['e_gate'], 'L0_ffn_e_up': _L0_ffn_in['e_up'], 'L0_ffn_e_down': _L0_ffn_in['e_down']}

def reference(x, L0_tok_level_emb, L0_attn_Wq, L0_attn_bq, L0_attn_Wk, L0_attn_bk, L0_attn_Wv, L0_attn_bv, L0_attn_Wo, L0_attn_bo, L0_attn_Er, L0_ffn_norm1_w, L0_ffn_norm2_w, L0_ffn_wq, L0_ffn_wk, L0_ffn_wv, L0_ffn_wo, L0_ffn_router_w, L0_ffn_sh_gate, L0_ffn_sh_up, L0_ffn_sh_down, L0_ffn_e_gate, L0_ffn_e_up, L0_ffn_e_down):
    import jax
    import jax.numpy as jnp

    def _L0_tok_ref(token_ids, level_emb):
        import jax, jax.numpy as jnp
        import numpy as np
        NUM_LEVELS = 32
        SCALE = 0.15
        OPEN_TOKENS = jnp.array([40, 91, 123], dtype=jnp.int32)
        CLOSE_TOKENS = jnp.array([41, 93, 125], dtype=jnp.int32)

        def _compute_levels(token_ids, num_levels):
            is_open = (token_ids[..., None] == OPEN_TOKENS).any(-1)
            is_close = (token_ids[..., None] == CLOSE_TOKENS).any(-1)
            delta = is_open.astype(jnp.int32) - is_close.astype(jnp.int32)

            def step(lvl, d):
                lvl = jnp.clip(lvl + d, 0, num_levels - 1)
                return (lvl, lvl)
            init = jnp.zeros(token_ids.shape[0], dtype=jnp.int32)
            _, levels = jax.lax.scan(step, init, delta.T)
            return levels.T
        levels = _compute_levels(token_ids, NUM_LEVELS)
        hierarchy_pos = level_emb[levels]
        return hierarchy_pos * SCALE

    def _L0_attn_ref(x, Wq, bq, Wk, bk, Wv, bv, Wo, bo, Er):
        import jax, jax.numpy as jnp
        import numpy as np
        import math
        D_MODEL = 256
        NUM_HEADS = 16
        D_K = D_MODEL // NUM_HEADS
        MAX_LEN = 512
        B, S = (2, 256)
        Bsz, Slen, Dm = x.shape
        H, dk = (NUM_HEADS, D_K)

        def proj(W, b):
            y = jnp.einsum('bsd,ed->bse', x, W) + b
            return y.reshape(Bsz, Slen, H, dk).transpose(0, 2, 1, 3)
        Q = proj(Wq, bq)
        K = proj(Wk, bk)
        V = proj(Wv, bv)
        AC = jnp.einsum('bhid,bhjd->bhij', Q, K)
        rel_pos = jnp.arange(Slen - 1, -Slen, -1)
        idx = rel_pos + (Slen - 1)
        Er_emb = Er[idx]
        BD_full = jnp.einsum('bhid,md->bhim', Q, Er_emb)
        i_idx = jnp.arange(Slen)[:, None]
        m_idx = Slen - 1 - i_idx + jnp.arange(Slen)[None, :]
        BD = BD_full[:, :, i_idx, m_idx]
        scores = (AC + BD) / math.sqrt(dk)
        attn = jax.nn.softmax(scores, axis=-1)
        out = jnp.einsum('bhij,bhjd->bhid', attn, V)
        out = out.transpose(0, 2, 1, 3).reshape(Bsz, Slen, Dm)
        return jnp.einsum('bsd,ed->bse', out, Wo) + bo

    def _L0_ffn_ref(X, norm1_w, norm2_w, wq, wk, wv, wo, router_w, sh_gate, sh_up, sh_down, e_gate, e_up, e_down):
        import jax, jax.numpy as jnp
        import numpy as np
        D_MODEL = 256
        N_HEADS = 16
        D_HEAD = D_MODEL // N_HEADS
        N_EXPERTS = 8
        TOP_K = 2
        D_FF = 512
        EPS = 1e-06

        def rmsnorm(x, w):
            return x * jax.lax.rsqrt(jnp.mean(x * x, axis=-1, keepdims=True) + EPS) * w

        def swiglu(x, w_gate, w_up, w_down):
            return jax.nn.silu(x @ w_gate) * (x @ w_up) @ w_down
        B, S, d = X.shape
        scale = 1.0 / jnp.sqrt(jnp.asarray(D_HEAD, X.dtype))
        h = rmsnorm(X, norm1_w)
        q = (h @ wq).reshape(B, S, N_HEADS, D_HEAD)
        k = (h @ wk).reshape(B, S, N_HEADS, D_HEAD)
        v = (h @ wv).reshape(B, S, N_HEADS, D_HEAD)
        scores = jnp.einsum('bshd,bthd->bhst', q, k) * scale
        attn = jax.nn.softmax(scores, axis=-1)
        ctx = jnp.einsum('bhst,bthd->bshd', attn, v).reshape(B, S, d)
        X = X + ctx @ wo
        h2 = rmsnorm(X, norm2_w).reshape(B * S, d)
        logits = h2 @ router_w
        probs = jax.nn.softmax(logits, axis=-1)
        topw, topi = jax.lax.top_k(probs, TOP_K)
        topw = jax.nn.softmax(topw, axis=-1)
        combine = jnp.sum(jax.nn.one_hot(topi, N_EXPERTS, dtype=h2.dtype) * topw[..., None], axis=1)
        shared = swiglu(h2, sh_gate, sh_up, sh_down)
        gate = jnp.einsum('td,edf->etf', h2, e_gate)
        up = jnp.einsum('td,edf->etf', h2, e_up)
        eout = jnp.einsum('etf,efd->etd', jax.nn.silu(gate) * up, e_down)
        spec = jnp.einsum('etd,te->td', eout, combine)
        moe_out = (shared + spec).reshape(B, S, d)
        return X + moe_out
    h = _L0_tok_ref(x, L0_tok_level_emb)
    h = h + _L0_attn_ref(_layernorm(h, axis=-1), L0_attn_Wq, L0_attn_bq, L0_attn_Wk, L0_attn_bk, L0_attn_Wv, L0_attn_bv, L0_attn_Wo, L0_attn_bo, L0_attn_Er)
    h = h + _L0_ffn_ref(_layernorm(h, axis=-1), L0_ffn_norm1_w, L0_ffn_norm2_w, L0_ffn_wq, L0_ffn_wk, L0_ffn_wv, L0_ffn_wo, L0_ffn_router_w, L0_ffn_sh_gate, L0_ffn_sh_up, L0_ffn_sh_down, L0_ffn_e_gate, L0_ffn_e_up, L0_ffn_e_down)
    return h

_drawn_inputs = setup_inputs


def setup_inputs(seed=0):
    import zlib

    import numpy as np

    out = dict(_drawn_inputs(seed))
    spreads = {'L0_attn_bq': (0.0, 0.329),
     'L0_attn_bk': (0.0, 2.0),
     'L0_attn_bv': (0.0, 0.1),
     'L0_attn_bo': (0.0, 0.1),
     'L0_ffn_norm1_w': (1.0, 0.6),
     'L0_ffn_norm2_w': (1.0, 0.6)}
    factors = {'L0_attn_Er': 8.0,
     'L0_ffn_wq': 8.0,
     'L0_ffn_wk': 8.0,
     'L0_ffn_router_w': 4.582,
     'L0_ffn_e_gate': 3.769,
     'L0_ffn_e_up': 3.645,
     'L0_ffn_e_down': 3.78,
     'L0_ffn_sh_gate': 2.856,
     'L0_ffn_sh_down': 2.745}
    for name, (base, spread) in spreads.items():
        noise = np.random.default_rng([zlib.crc32(name.encode()), seed]).standard_normal(out[name].shape)
        drawn = base * np.exp(spread * noise) if base else spread * noise
        out[name] = jnp.asarray(drawn.astype(out[name].dtype))
    for name, factor in factors.items():
        out[name] = (out[name] * factor).astype(out[name].dtype)
    return out
```

```python
import concourse.bass as bass
from concourse import mybir
from contextlib import ExitStack

F32 = mybir.dt.float32
F32R = mybir.dt.float32r
BF16 = mybir.dt.bfloat16
I32 = mybir.dt.int32
U32 = mybir.dt.uint32
ALU = mybir.AluOpType
ACT = mybir.ActivationFunctionType
AX = mybir.AxisListType

B, S, D = 8, 256, 256
T = B * S
H, DK = 16, 16
L = 32
E, F = 8, 512
P = 128
NT = T // P
DC = D // P
FC = F // P
QK_SCALE = 1.0 / DK ** 0.5
EMB_SCALE = 0.15
LN_EPS, RMS_EPS = 1e-5, 1e-6

LEFT = (0, 0, 1, 0, 2, 1)
RIGHT = (0, 1, 0, 2, 0, 1)
SLOTS = len(LEFT)
KP = SLOTS * DK
L3 = 3 * L

BP = 2
NPAIR = B // BP
QI = 16
STEPS = P // QI
COLS = BP * H * QI
PADV = 32
NG = H // 4


class Shared:
    pass


def names(n):
    return [str(i) for i in range(n)]


class Chain:

    def __init__(self, eng, sem):
        self.eng, self.sem, self.base, self.k, self.trip, self.per = eng, sem, 0, 0, None, 0

    def enter(self, trip, per):
        self.base, self.k, self.trip, self.per = self.base + self.k, 0, trip, per

    def leave(self, trips):
        assert self.k == self.per, self.k
        self.base, self.k, self.trip = self.base + trips * self.per, 0, None

    def __call__(self, ins, apart=None):
        ins.then_inc(self.sem, 1)
        self.k += 1
        done = self.base + self.k
        self.eng.wait_ge(self.sem, done if self.trip is None else self.trip * self.per + done)
        if apart is not None:
            self.eng.sem_inc(apart)


def build_program(nc, a, outs):
    ctx = ExitStack()
    with ctx:
        def sem(name):
            return ctx.enter_context(nc.semaphore(name))

        def kept(name, shape, dt):
            return ctx.enter_context(nc.sbuf_tensor(name, shape, dt))

        g = Shared()
        g.sem = sem
        g.ps = ctx.enter_context(nc.psum_tensor("ps", [P, 8, 512], F32))
        g.identF = kept("identF", [P, P], F32)
        g.identB = kept("identB", [P, P], BF16)
        g.negIB = kept("negIB", [P, P], BF16)
        g.qd = nc.dram_tensor("qk_parts", [2, 3, D, T], BF16, kind="Internal").ap()
        g.HS = kept("HS", [P, NT, D], F32)
        g.V2 = kept("V2", [P, NT, H, DK], F32)
        g.H2T = g.V2[:].rearrange("p t h d -> p (t h d)").rearrange("p (c t) -> p c t", c=DC)
        g.comb = kept("comb", [P, NT, E + 1], F32)
        with ExitStack() as mid:
            g.OT = mid.enter_context(nc.sbuf_tensor("OT", [P, NT, NG, P], F32))
            g.XS = mid.enter_context(nc.sbuf_tensor("XS", [P, NT, D], F32))
            with ExitStack() as low:
                def lo(name, shape, dt):
                    return low.enter_context(nc.sbuf_tensor(name, shape, dt))
                g.WoT = lo("WoT", [P, DC, D], F32)
                g.R3 = lo("R3", [L3, D], BF16)
                g.OH3 = lo("OH3", [L3, (NPAIR + 1) * BP * S], BF16)
                g.ErT = lo("ErT", [KP, 2 * S], BF16)
                g.QT = lo("QT", [L, H, KP], BF16)
                g.ACP = lo("ACP", [L, H, L3], BF16)
                g.V3 = lo("V3", [L3, D], BF16)
                tables(nc, g, a)
                level_attention(nc, g)
                project(nc, g, a)
            full_attention(nc, g)
            route(nc, g, a)
        experts(nc, g, a, outs)


def tables(nc, g, a):
    sem, ps = g.sem, g.ps
    s_in = [sem("in_" + n) for n in ("tok", "tab", "w", "er", "id")]
    s_dve, s_act, s_pool = sem("tab_dve"), sem("tab_act"), sem("tab_pool")
    s_lv, s_lvp, s_ln, s_xt, s_xtc, s_proj, s_sp, s_qkT, s_qkTc, s_ac, s_er, s_erT, s_idb, s_rs = (
        sem("tab_" + n) for n in "levels levelsB norm xT xTc proj split qkT qkTc ac er erT idb rstd".split())
    with ExitStack() as c:
        def sb(n, sh, dt):
            return c.enter_context(nc.sbuf_tensor("t_" + n, sh, dt))
        tok, tokf = sb("tok", [B, S], I32), sb("tokf", [B, S], F32)
        acc, Dl, nD, rD, zer, lev = (sb(n, [B, S], F32) for n in ("acc", "Dl", "nD", "rD", "zer", "lev"))
        sel, lvl = sb("sel", [B, B, L3], F32), sb("lvl", [L3, 1], F32)
        emb, xt, bo = sb("emb", [L, D], F32), sb("xt", [L, D], F32), sb("bo", [L, D], F32)
        st, mv, half = sb("st", [L, 6], F32), sb("mv", [L, 4], F32), sb("half", [L, 1], F32)
        xT = sb("xT", [P, DC, L], F32)
        W = sb("W", [P, 3, DC, D], F32)
        bias, tab = sb("bias", [L, 3, D], F32), sb("tab", [L, 3, D], F32)
        r1, r2 = sb("r1", [L, 3, D], F32), sb("r2", [L, 3, D], F32)
        parts = [sb("part" + i, [L, 3, D], BF16) for i in names(3)]
        KT = sb("KT", [L, H, KP], BF16)
        qkT = sb("qkT", [KP, 2, H, L], BF16)
        er, e1, e2 = sb("er", [P, 4, DK], F32), sb("e1", [P, 4, DK], F32), sb("e2", [P, 4, DK], F32)
        eparts = [sb("epart" + i, [P, 4, DK], BF16) for i in names(3)]
        EP = sb("EP", [P, 4, SLOTS, DK], BF16)
        ac, a1, a2 = sb("ac", [L, H, L], F32), sb("a1", [L, H, L], F32), sb("a2", [L, H, L], F32)
        rr, rr1, rr2 = sb("rr", [L, D], F32), sb("rr1", [L, D], F32), sb("rr2", [L, D], F32)
        psf = ps[:].rearrange("p a b -> p (a b)")
        with nc.Block() as block:
            @block.sync
            def _(sp):
                sp.dma_start(tok[:], a["x"]).then_inc(s_in[0], 16)
                sp.dma_start(sel[:], a["sel"]).then_inc(s_in[0], 16)
                sp.dma_start(lvl[:], a["lvl"]).then_inc(s_in[0], 16)
                sp.dma_start(er[:], a["er"]).then_inc(s_in[3], 16)
                sp.dma_start(g.WoT[:], a["WoT"]).then_inc(s_in[2], 16)
                sp.wait_ge(s_in[2], 64)

            @block.scalar
            def _(act):
                act.dma_start(emb[:], a["emb"]).then_inc(s_in[1], 16)
                act.dma_start(g.identF[:], a["ident"]).then_inc(s_in[4], 16)
                act.dma_start(bo[:], a["bo"]).then_inc(s_in[1], 16)
                act.dma_start(bias[:], a["bias"]).then_inc(s_in[1], 16)
                for n, w in enumerate((a["WqT"], a["WkT"], a["WvT"])):
                    act.dma_start(W[:, n], w).then_inc(s_in[2], 16)

            @block.gpsimd
            def _(pool):
                nc.gpsimd.memset(half[:], -0.5).then_inc(s_pool, 1)
                pool.wait_ge(s_pool, 1)
                pool.wait_ge(s_ln, 1)
                nc.gpsimd.tensor_tensor(mv[:, 3:4], mv[:, 2:3], half[:], ALU.pow).then_inc(s_rs, 1)

            @block.vector
            def _(dve):
                do = Chain(dve, s_dve)
                V = nc.vector
                do(V.memset(zer[:], 0.0))
                dve.wait_ge(s_in[0], 48)
                do(V.tensor_copy(tokf[:], tok[:]))
                do(V.tensor_scalar(acc[:], tokf[:], 41.0, None, ALU.is_equal))
                for close in (93.0, 125.0):
                    do(V.scalar_tensor_tensor(acc[:], tokf[:], close, acc[:], ALU.is_equal, ALU.add))
                do(V.scalar_tensor_tensor(acc[:], tokf[:], 40.0, acc[:], ALU.is_equal, ALU.subtract))
                for opened in (91.0, 123.0):
                    do(V.scalar_tensor_tensor(acc[:], tokf[:], opened, acc[:], ALU.is_equal, ALU.add))
                do(V.tensor_tensor_scan(Dl[:], acc[:], zer[:], 0.0, ALU.add, ALU.add))
                do(V.tensor_scalar(nD[:], Dl[:], -1.0, None, ALU.mult))
                do(V.tensor_scalar(rD[:], Dl[:], -1.0, float(L - 1), ALU.mult, ALU.add))
                do(V.tensor_tensor_scan(acc[:], nD[:], rD[:], 0.0, ALU.max, ALU.min))
                V.tensor_tensor(lev[:], acc[:], Dl[:], ALU.add).then_inc(s_lv, 1)
                dve.wait_ge(s_in[1], 48)
                dve.wait_ge(s_in[4], 16)
                do(V.tensor_scalar(emb[:], emb[:], EMB_SCALE, None, ALU.mult))
                do(V.bn_stats(st[:], emb[:]))
                do(V.bn_aggr(mv[:, 0:2], st[:]))
                V.tensor_scalar(mv[:, 2:3], mv[:, 1:2], LN_EPS, None, ALU.add).then_inc(s_ln, 1)
                V.tensor_copy(g.identB[:], g.identF[:]).then_inc(s_idb, 1)
                V.tensor_scalar(g.negIB[:], g.identF[:], -1.0, None, ALU.mult).then_inc(s_idb, 1)
                dve.wait_ge(s_rs, 1)
                V.tensor_scalar(xt[:], emb[:], mv[:, 0:1], mv[:, 3:4], ALU.subtract, ALU.mult).then_inc(s_ln, 1)
                do(V.memset(g.OH3[:, T:], 0.0))
                for q in range(4):
                    dve.wait_ge(s_lvp, q + 1)
                    do(V.tensor_scalar(g.OH3[:, q * 512:(q + 1) * 512], ps[0:L3, q, :], lvl[:, 0:1], None, ALU.is_equal))

                def split(src, r, rr_, out):
                    do(V.tensor_copy(out[0], src))
                    do(V.tensor_tensor(r, src, out[0], ALU.subtract))
                    do(V.tensor_copy(out[1], r))
                    do(V.tensor_tensor(rr_, r, out[1], ALU.subtract))
                    do(V.tensor_copy(out[2], rr_))

                dve.wait_ge(s_in[3], 16)
                split(er[:], e1[:], e2[:], [x[:] for x in eparts])
                for n in range(SLOTS):
                    do(V.tensor_copy(EP[:, :, n], eparts[RIGHT[n]][:]))
                V.memset(zer[0:1, 0:1], 0.0).then_inc(s_er, 1)
                do(V.tensor_tensor(rr[:], emb[:], bo[:], ALU.add))
                split(rr[:], rr1[:], rr2[:], [g.R3[n * L:(n + 1) * L] for n in range(3)])
                dve.wait_ge(s_xt, 1)
                V.tensor_copy(xT[:], psf[:, 2048:2048 + DC * L].rearrange("p (c l) -> p c l", c=DC)).then_inc(s_xtc, 1)
                for n in range(3):
                    dve.wait_ge(s_proj, n + 1)
                    do(V.tensor_tensor(tab[:, n], ps[0:L, 5 + n % 2, 0:D], bias[:, n], ALU.add))
                    V.memset(zer[0:1, 0:1], 0.0).then_inc(s_sp, 1)
                split(tab[:], r1[:], r2[:], [x[:] for x in parts])
                heads = [[x[:, n].rearrange("p (h d) -> p h d", h=H) for x in parts] for n in range(2)]
                for n in range(SLOTS):
                    at = slice(n * DK, (n + 1) * DK)
                    do(V.tensor_copy(g.QT[:, :, at], heads[0][LEFT[n]]))
                    do(V.tensor_copy(KT[:, :, at], heads[1][RIGHT[n]]))
                V.memset(zer[0:1, 0:1], 0.0).then_inc(s_sp, 1)
                for n in range(3):
                    do(V.tensor_copy(g.V3[n * L:(n + 1) * L], parts[n][:, 2]))
                dve.wait_ge(s_erT, 1)
                do(V.tensor_copy(g.ErT[:], ps[0:KP, 0].bitcast(BF16)[:, 0:512]))
                dve.wait_ge(s_qkT, 1)
                for n in range(2):
                    do(V.tensor_copy(qkT[:, n].rearrange("p h l -> p (h l)"), ps[0:KP, 1 + n].bitcast(BF16)[:, 0:512]))
                V.memset(zer[0:1, 0:1], 0.0).then_inc(s_qkTc, 1)
                dve.wait_ge(s_ac, 1)
                do(V.tensor_copy(ac[:], ps[0:L, 3].rearrange("p (h l) -> p h l", h=H)))
                split(ac[:], a1[:], a2[:], [g.ACP[:, :, n * L:(n + 1) * L] for n in range(3)])

            @block.tensor
            def _(pe):
                mm = nc.tensor.matmul
                pe.wait_ge(s_lv, 1)
                for b in range(B):
                    last = mm(ps[0:L3, b // 2, (b % 2) * S:(b % 2 + 1) * S], sel[:, b], lev[:], start=True, stop=True)
                    if b % 2:
                        last.then_inc(s_lvp, 1)
                pe.wait_ge(s_ln, 2)
                pe.wait_ge(s_in[4], 16)
                for n in range(DC):
                    last = nc.tensor.transpose(psf[:, 2048 + n * L:2048 + (n + 1) * L], xt[:, n * P:(n + 1) * P], g.identF[0:L, 0:L])
                last.then_inc(s_xt, 1)
                pe.wait_ge(s_xtc, 1)
                pe.wait_ge(s_in[2], 64)
                for n in range(3):
                    if n >= 2:
                        pe.wait_ge(s_sp, n - 1)
                    for c_ in range(DC):
                        last = mm(ps[0:L, 5 + n % 2, 0:D], xT[:, c_], W[:, n, c_], start=c_ == 0, stop=c_ == DC - 1)
                    last.then_inc(s_proj, 1)
                pe.wait_ge(s_er, 1)
                pe.wait_ge(s_idb, 2)
                for n in range(4):
                    last = nc.tensor.transpose(ps[0:KP, 0].bitcast(BF16)[:, n * P:(n + 1) * P], EP[:, n].rearrange("p s d -> p (s d)"), g.identB[:])
                last.then_inc(s_erT, 1)
                pe.wait_ge(s_sp, 4)
                for n, t in enumerate((g.QT, KT)):
                    for h in range(H):
                        last = nc.tensor.transpose(ps[0:KP, 1 + n].bitcast(BF16)[:, h * L:(h + 1) * L], t[:, h], g.identB[0:L, 0:L])
                last.then_inc(s_qkT, 1)
                pe.wait_ge(s_qkTc, 1)
                for h in range(H):
                    last = mm(ps[0:L, 3, h * L:(h + 1) * L], qkT[:, 0, h], qkT[:, 1, h], start=True, stop=True)
                last.then_inc(s_ac, 1)


def level_attention(nc, g):
    sem, ps = g.sem, g.ps
    (s_built, s_evac, s_mx, s_tr, s_m, s_ready, s_exp, s_qp, s_qb, s_ap, s_ab, s_vp, s_vs, s_pv, s_ot, s_ms, s_apart) = (
        sem("la_" + n) for n in ("built evac halfmax turned max ready exp q_made q_kept a_made a_kept "
                                 "v_made v_kept pv out init apart").split())
    NS = 2 * STEPS
    UN = H // 2
    with ExitStack() as c:
        def sb(n, sh, dt):
            return c.enter_context(nc.sbuf_tensor("la_" + n, sh, dt))
        QB = sb("QB", [KP, 2, BP, H, P], BF16)
        AQ = sb("AQ", [L3, 2, BP, H, P], BF16)
        SA = sb("SA", [P, 2, COLS], BF16)
        SM = sb("SM", [P, 2, COLS], BF16)
        m = sb("m", [P, 2, 4], BF16)
        PT = sb("PT", [P, 2, 2, BP * H, P], F32)
        Vs = sb("Vs", [P, BP, 2, H, PADV], F32)
        OHq = g.OH3[0:L].rearrange("p (q b f i) -> p q b f i", b=BP, f=2, i=P)
        XT = ps[:, 4].bitcast(BF16)[:, 0:512]
        with nc.Block() as block:
            @block.gpsimd
            def _(pool):
                nc.gpsimd.memset(Vs[:, :, :, :, DK:PADV], 0.0).then_inc(s_ms, 1)
                pool.wait_ge(s_ms, 1)
                nc.gpsimd.memset(Vs[:, :, :, :, DK:DK + 1], 1.0).then_inc(s_ms, 1)

            @block.tensor
            def _(pe):
                mm = nc.tensor.matmul

                def make_unit(pair, half, u, made):
                    pe.wait_ge(s_qb, made + 1)
                    pe.sem_inc(s_apart)
                    rhs = OHq[:, bass.ds(pair, 1), :, half, :]
                    for k in range(2):
                        last = mm(ps[0:KP, 6, k * BP * P:(k + 1) * BP * P], g.QT[:, 2 * u + k], rhs, start=True, stop=True)
                    last.then_inc(s_qp, 1)
                    pe.wait_ge(s_ab, made + 1)
                    pe.sem_inc(s_apart)
                    for k in range(2):
                        last = mm(ps[0:L3, 7, k * BP * P:(k + 1) * BP * P], g.ACP[:, 2 * u + k], rhs, start=True, stop=True)
                    last.then_inc(s_ap, 1)

                def build(pair, n):
                    half, k = divmod(n, STEPS)
                    q0 = k * QI
                    if n >= 2:
                        pe.wait_ge(s_exp, pair * NS + n - 1)
                    for jh in range(2):
                        bank = ps[:, 2 * (n % 2) + jh]
                        for b in range(BP):
                            mm(bank[:, b * H * QI:(b + 1) * H * QI], g.OH3[:, bass.ds(pair * (BP * S) + b * S + jh * P, P)],
                               AQ[:, half, b, :, q0:q0 + QI], start=b == 0, stop=False, skip_group_check=True)
                        cols = bank.rearrange("p (h i) -> p h i", i=QI)
                        q = QB[:, half].rearrange("p b h i -> p (b h) i")
                        for i in range(QI):
                            w0 = S - (half * P + q0 + i) + jh * P
                            last = mm(cols[:, :, i], g.ErT[:, w0:w0 + P], q[:, :, q0 + i], start=False, stop=False,
                                      skip_group_check=True)
                    last.then_inc(s_built, 1)

                def turn(pair, n):
                    pe.wait_ge(s_mx, pair * NS + n + 1)
                    for q in range(4):
                        last = nc.tensor.transpose(XT[:, q * P:(q + 1) * P], SM[:, n % 2, q * P:(q + 1) * P], g.identB[:])
                    last.then_inc(s_tr, 1)

                def subtract_max(pair, n):
                    pe.wait_ge(s_m, pair * NS + n + 1)
                    for jh in range(2):
                        for q in range(4):
                            last = mm(ps[:, 2 * (n % 2) + jh, q * P:(q + 1) * P], m[:, n % 2, q:q + 1].to_broadcast([P, P]), g.negIB[:],
                                      start=False, stop=True, skip_group_check=True)
                    last.then_inc(s_ready, 1)

                def make_values(pair, b):
                    pe.wait_ge(s_vs, pair * BP + b + 1)
                    pe.wait_ge(s_ot, pair * 4 + 1)
                    for jh in range(2):
                        last = mm(ps[:, 5, jh * D:(jh + 1) * D], g.OH3[:, bass.ds(pair * (BP * S) + b * S + jh * P, P)], g.V3[:],
                                  start=True, stop=True)
                    last.then_inc(s_vp, 1)

                def weigh_values(pair, half, b):
                    pe.wait_ge(s_exp, pair * NS + (half + 1) * STEPS)
                    pe.wait_ge(s_vs, pair * BP + BP + 1)
                    pe.wait_ge(s_ot, pair * 4 + half * 2 + b + 1)
                    for grp in range(NG):
                        for jh in range(2):
                            for k in range(4):
                                h = 4 * grp + k
                                last = mm(ps[32 * k:32 * k + PADV, 5, grp * P:(grp + 1) * P], Vs[:, b, jh, h],
                                          PT[:, half, jh, b * H + h], start=jh == 0, stop=jh == 1, skip_group_check=True)
                    last.then_inc(s_pv, 1)

                pe.wait_ge(s_ms, 2)
                for u in range(UN):
                    make_unit(0, 0, u, u)
                with pe.Fori(0, NPAIR) as pair:
                    for n in range(NS):
                        half, k = divmod(n, STEPS)
                        if n == 0:
                            pe.wait_ge(s_qb, pair * (2 * UN) + UN + 1)
                            pe.wait_ge(s_ab, pair * (2 * UN) + UN + 1)
                            build(pair, 0)
                        if k < UN - 1:
                            for u in ((0, 1) if k == 0 else (k + 1,)):
                                make_unit(pair + half, 1 - half, u, pair * (2 * UN) + UN + half * UN + u)
                        if n + 1 < NS:
                            if k == STEPS - 1:
                                pe.wait_ge(s_qb, pair * (2 * UN) + 2 * UN + 1)
                                pe.wait_ge(s_ab, pair * (2 * UN) + 2 * UN + 1)
                            build(pair, n + 1)
                        turn(pair, n)
                        if n < BP:
                            make_values(pair, n)
                        if n in (STEPS + 1, STEPS + 4):
                            weigh_values(pair, 0, n == STEPS + 4)
                        subtract_max(pair, n)
                    for b in range(BP):
                        weigh_values(pair, 1, b)

            @block.scalar
            def _(act):
                def keep_unit(half, u, made):
                    act.wait_ge(s_ap, made)
                    nc.scalar.activation(AQ[:, half, :, 2 * u:2 * u + 2], ps[0:L3, 7].rearrange("p (h b i) -> p b h i", h=2, b=BP),
                                         ACT.Copy).then_inc(s_ab, 1)

                def copy_half(pair, n):
                    act.wait_ge(s_built, pair * NS + n + 1)
                    nc.scalar.activation(SA[:, n % 2], ps[:, 2 * (n % 2)], ACT.Copy).then_inc(s_evac, 1)

                nc.scalar.activation(AQ[0:1, 0, 0, 0, 0:1], g.identF[0:1, 0:1], ACT.Copy).then_inc(s_ab, 1)
                nc.scalar.activation(Vs[0:1, 0, 0, 0, 0:1], g.identF[0:1, 0:1], ACT.Copy).then_inc(s_vs, 1)
                act.wait_ge(s_vs, 1)
                act.wait_ge(s_ab, 1)
                for u in range(UN):
                    keep_unit(0, u, u + 1)
                with act.Fori(0, NPAIR) as pair:
                    copy_half(pair, 0)
                    for n in range(NS):
                        half, k = divmod(n, STEPS)
                        if k < UN - 1:
                            for u in ((0, 1) if k == 0 else (k + 1,)):
                                keep_unit(1 - half, u, pair * (2 * UN) + UN + half * UN + u + 1)
                        if n + 1 < NS:
                            copy_half(pair, n + 1)
                        if n < BP:
                            act.wait_ge(s_vp, pair * BP + n + 1)
                            nc.scalar.activation(Vs[:, n, :, :, 0:DK], ps[:, 5].rearrange("p (j h d) -> p j h d", j=2, h=H),
                                                 ACT.Copy).then_inc(s_vs, 1)
                        act.wait_ge(s_ready, pair * NS + n + 1)
                        nc.scalar.activation(PT[:, half, :, :, k * QI:(k + 1) * QI],
                                             ps[:, 2 * (n % 2):2 * (n % 2) + 2].rearrange("p j (h i) -> p j h i", i=QI),
                                             ACT.Exp, scale=QK_SCALE).then_inc(s_exp, 1)

            @block.vector
            def _(dve):
                def keep_unit(half, u, made):
                    dve.wait_ge(s_qp, made)
                    nc.vector.tensor_copy(QB[:, half, :, 2 * u:2 * u + 2], ps[0:KP, 6].rearrange("p (h b i) -> p b h i", h=2, b=BP)
                                          ).then_inc(s_qb, 1)

                def keep_out(pair, half, b):
                    dve.wait_ge(s_pv, pair * 4 + half * 2 + b + 1)
                    nc.vector.tensor_copy(g.OT[:, bass.ds(pair * 4 + b * 2 + half, 1)], ps[:, 5].rearrange("p (o g i) -> p o g i", o=1, g=NG)
                                          ).then_inc(s_ot, 1)

                nc.vector.memset(QB[0:1, 0, 0, 0, 0:1], 0.0).then_inc(s_qb, 1)
                nc.vector.memset(g.OT[0:1, 0, 0, 0:1], 0.0).then_inc(s_ot, 1)
                dve.wait_ge(s_qb, 1)
                dve.wait_ge(s_ot, 1)
                for u in range(UN):
                    keep_unit(0, u, u + 1)
                with dve.Fori(0, NPAIR) as pair:
                    for n in range(NS):
                        half, k = divmod(n, STEPS)
                        if k < UN - 1:
                            for u in ((0, 1) if k == 0 else (k + 1,)):
                                keep_unit(1 - half, u, pair * (2 * UN) + UN + half * UN + u + 1)
                        dve.wait_ge(s_evac, pair * NS + n + 1)
                        nc.vector.tensor_tensor(SM[:, n % 2], ps[:, 2 * (n % 2) + 1], SA[:, n % 2], ALU.max).then_inc(s_mx, 1)
                        dve.wait_ge(s_tr, pair * NS + n + 1)
                        nc.vector.reduce_max(m[:, n % 2], XT.rearrange("p (q j) -> p q j", q=4), AX.X).then_inc(s_m, 1)
                        if n in (STEPS + 2, STEPS + 5):
                            keep_out(pair, 0, int(n == STEPS + 5))
                    for b in range(BP):
                        keep_out(pair, 1, b)


GT = 4
GN = NT // GT


def pe_turn_heads(nc, pe, g, s, t):
    pe.wait_ge(s.ots, t + 1)
    for k in range(GT):
        for grp in range(NG):
            last = nc.tensor.transpose(g.ps[:, k, grp * P:(grp + 1) * P], s.OTs[:, k, grp], g.identF[:])
    last.then_inc(s.rows, 1)
    pe.wait_ge(s.at, t + 1)
    for k in range(GT):
        for c in range(DC):
            last = nc.tensor.transpose(g.ps[:, 4 + c, k * P:(k + 1) * P], s.AT[:, k, c * P:(c + 1) * P], g.identF[:])
    last.then_inc(s.att, 1)


def dve_divide_heads(nc, dve, g, s, t):
    nc.vector.tensor_copy(s.OTs[:], g.OT[:, bass.ds(t * GT, GT)]).then_inc(s.ots, 1)
    dve.wait_ge(s.rows, t + 1)
    rows = g.ps[:, 0:4].rearrange("p k (h d) -> p (k h) d", d=PADV)
    nc.vector.reciprocal(s.rec[:], rows[:, :, DK]).then_inc(s.recip, 1)
    dve.wait_ge(s.recip, t + 1)
    nc.vector.tensor_tensor(s.AT[:].rearrange("p k (h d) -> p (k h) d", d=DK), rows[:, :, 0:DK],
                            s.rec[:].unsqueeze(2).to_broadcast([P, GT * H, DK]), ALU.mult).then_inc(s.at, 1)


def head_buffers(g, c, nc, tag):
    def sb(n, sh):
        return c.enter_context(nc.sbuf_tensor(tag + n, sh, F32))
    s = Shared()
    s.OTs, s.AT, s.ATT, s.rec = sb("OTs", [P, GT, NG, P]), sb("AT", [P, GT, D]), sb("ATT", [P, DC, GT * P]), sb("rec", [P, GT * H])
    s.ots, s.rows, s.recip, s.at, s.att, s.attc = (g.sem(tag + n) for n in ("ots", "rows", "recip", "at", "att", "attc"))
    return s


def project(nc, g, a):
    sem, ps = g.sem, g.ps
    (s_h, s_hs, s_var, s_rs, s_x, s_ms, s_r2, s_hn, s_ht, s_htc, s_q, s_hi, s_r1, s_mi, s_lo, s_moved, s_v, s_vk, s_dv, s_half, s_apart) = (
        sem("pj_" + n) for n in ("h hs var rs x ms r2 hn ht htc q hi r1 mid lo moved v vkept dve half apart").split())
    with ExitStack() as c:
        def sb(n, sh, dt):
            return c.enter_context(nc.sbuf_tensor("pj_" + n, sh, dt))
        s = head_buffers(g, c, nc, "pj_")
        st, mv, half = sb("st", [P, GT, 6], F32), sb("mv", [P, GT, 8], F32), sb("half", [P, GT], F32)
        hn, hT = sb("hn", [P, GT, D], F32), sb("hT", [P, DC, GT * P], F32)
        w1 = sb("w1", [P, D], F32)
        W = sb("W", [P, 3, DC, D], F32)
        r1 = sb("r1", [P, 2, DC, GT * P], F32)
        parts = sb("parts", [P, 2, 3, DC, GT * P], BF16)
        qd = g.qd.rearrange("k a (m p) t -> k p a m t", p=P)
        with nc.Block() as block:
            @block.sync
            def _(sp):
                for n, w in enumerate((a["wq"], a["wk"], a["wv"])):
                    sp.dma_start(W[:, n], w).then_inc(s_moved, 16)
                sp.dma_start(w1[:], a["w1"]).then_inc(s_moved, 16)
                with sp.Fori(0, GN) as t:
                    for k in range(2):
                        sp.wait_ge(s_lo, t * 2 + k + 1)
                        for part in range(3):
                            sp.dma_start(qd[k, :, part, :, bass.ds(t * (GT * P), GT * P)], parts[:, k, part]).then_inc(s_moved, 16)
                sp.wait_ge(s_moved, 64 + GN * 96)

            @block.gpsimd
            def _(pool):
                nc.gpsimd.memset(half[:], -0.5).then_inc(s_half, 1)
                pool.wait_ge(s_half, 1)
                with pool.Fori(0, GN) as t:
                    pool.wait_ge(s_var, t + 1)
                    nc.gpsimd.tensor_tensor(mv[:, :, 3], mv[:, :, 2], half[:], ALU.pow).then_inc(s_rs, 1)
                    pool.wait_ge(s_ms, t + 1)
                    nc.gpsimd.tensor_tensor(mv[:, :, 5], mv[:, :, 4], half[:], ALU.pow).then_inc(s_r2, 1)

            @block.tensor
            def _(pe):
                mm = nc.tensor.matmul
                pe.wait_ge(s_moved, 64)
                with pe.Fori(0, GN) as t:
                    pe_turn_heads(nc, pe, g, s, t)
                    pe.wait_ge(s.attc, t + 1)
                    for k in range(GT):
                        out = ps[:, k // 2, (k % 2) * D:(k % 2 + 1) * D]
                        for cc in range(DC):
                            mm(out, s.ATT[:, cc, k * P:(k + 1) * P], g.WoT[:, cc], start=cc == 0, stop=False)
                        last = mm(out, g.OH3[:, bass.ds(t * (GT * P) + k * P, P)], g.R3[:], start=False, stop=True)
                    last.then_inc(s_h, 1)
                    pe.wait_ge(s_hn, GT * (t + 1))
                    for k in range(GT):
                        for cc in range(DC):
                            last = nc.tensor.transpose(ps[:, 2 + cc, k * P:(k + 1) * P], hn[:, k, cc * P:(cc + 1) * P], g.identF[:])
                    last.then_inc(s_ht, 1)
                    pe.wait_ge(s_htc, t + 1)
                    for n in range(2):
                        for m in range(DC):
                            for cc in range(DC):
                                last = mm(ps[:, 4 + 2 * n + m], W[:, n, cc, m * P:(m + 1) * P], hT[:, cc], start=cc == 0, stop=cc == DC - 1)
                        last.then_inc(s_q, 1)
                    for k in range(GT):
                        for cc in range(DC):
                            last = mm(ps[:, k // 2, (k % 2) * D:(k % 2 + 1) * D], hT[:, cc, k * P:(k + 1) * P], W[:, 2, cc], start=cc == 0, stop=cc == DC - 1)
                    last.then_inc(s_v, 1)
                    pe.wait_ge(s_vk, t + 1)
                    pe.wait_ge(s_lo, 2 * t + 2)

            @block.scalar
            def _(act):
                def copy(out, in_):
                    return nc.scalar.activation(out, in_, ACT.Copy)

                with act.Fori(0, GN) as t:
                    act.wait_ge(s.att, t + 1)
                    copy(s.ATT[:], ps[:, 4:6]).then_inc(s.attc, 1)
                    act.wait_ge(s_h, t + 1)
                    copy(g.HS[:, bass.ds(t * GT, GT)], ps[:, 0:2].rearrange("p a (k d) -> p (a k) d", d=D)).then_inc(s_hs, 1)
                    act.wait_ge(s_ht, t + 1)
                    copy(hT[:], ps[:, 2:4]).then_inc(s_htc, 1)
                    act.wait_ge(s_moved, t * 96 + 64)
                    for n in range(2):
                        act.wait_ge(s_q, 2 * t + n + 1)
                        copy(parts[:, n, 0], ps[:, 4 + 2 * n:6 + 2 * n]).then_inc(s_hi, 1)
                    act.wait_ge(s_v, t + 1)
                    copy(g.V2[:, bass.ds(t * GT, GT), :, 0:DK], ps[:, 0:2].rearrange("p a (k h d) -> p (a k) h d", h=H, d=DK)).then_inc(s_vk, 1)
                    for n in range(2):
                        act.wait_ge(s_r1, 2 * t + n + 1)
                        copy(parts[:, n, 1], r1[:, n]).then_inc(s_mi, 1)

            @block.vector
            def _(dve):
                V = nc.vector
                do = Chain(dve, s_dv)
                with dve.Fori(0, GN) as t:
                    do.enter(t, 2 + 2 * GT)
                    dve_divide_heads(nc, dve, g, s, t)
                    dve.wait_ge(s_hs, t + 1)
                    for k in range(GT):
                        do(V.bn_stats(st[:, k], g.HS[:, bass.ds(t * GT + k, 1)].rearrange("p o d -> p (o d)")), s_apart)
                        do(V.bn_aggr(mv[:, k, 0:2], st[:, k]))
                    V.tensor_scalar(mv[:, :, 2], mv[:, :, 1], LN_EPS, None, ALU.add).then_inc(s_var, 1)
                    dve.wait_ge(s_rs, t + 1)
                    for k in range(GT):
                        V.tensor_scalar(g.XS[:, bass.ds(t * GT + k, 1)], g.HS[:, bass.ds(t * GT + k, 1)], mv[:, k, 0:1], mv[:, k, 3:4],
                                        ALU.subtract, ALU.mult).then_inc(s_x, 1)
                    do(V.tensor_tensor(mv[:, :, 6], mv[:, :, 3], mv[:, :, 3], ALU.mult))
                    do(V.tensor_tensor(mv[:, :, 6], mv[:, :, 6], mv[:, :, 1], ALU.mult))
                    V.tensor_scalar(mv[:, :, 4], mv[:, :, 6], RMS_EPS, None, ALU.add).then_inc(s_ms, 1)
                    dve.wait_ge(s_x, GT * (t + 1))
                    dve.wait_ge(s_r2, t + 1)
                    for k in range(GT):
                        V.scalar_tensor_tensor(hn[:, k:k + 1], g.XS[:, bass.ds(t * GT + k, 1)], mv[:, k, 5:6], w1[:].unsqueeze(1),
                                               ALU.mult, ALU.mult).then_inc(s_hn, 1)
                    for n in range(2):
                        dve.wait_ge(s_hi, 2 * t + n + 1)
                        V.tensor_tensor(r1[:, n], ps[:, 4 + 2 * n:6 + 2 * n], parts[:, n, 0], ALU.subtract).then_inc(s_r1, 1)
                    for n in range(2):
                        dve.wait_ge(s_mi, 2 * t + n + 1)
                        V.tensor_tensor(parts[:, n, 2], r1[:, n], parts[:, n, 1], ALU.subtract).then_inc(s_lo, 1)
                    do.leave(GN)


def full_attention(nc, g):
    sem, ps = g.sem, g.ps
    (s_sc, s_max, s_lg, s_exp, s_pv, s_ot, s_vs, s_pad) = (sem("fa_" + n) for n in "scores max less exp pv out values pad".split())
    s_ld = [sem("fa_load" + n) for n in names(2)]
    HP = H // 2
    with ExitStack() as c:
        def sb(n, sh, dt):
            return c.enter_context(nc.sbuf_tensor("fa_" + n, sh, dt))
        QK = sb("QK", [KP, 2, 2, H, S], BF16)
        m = sb("m", [P, 2, H, 2], BF16)
        PT = sb("PT", [P, 2, 4, 2, S], F32)
        Vs = sb("Vs", [P, 2, 2, H, PADV], F32)
        src = g.qd.rearrange("k a (h d) t -> k a d h t", d=DK)
        sides = (LEFT, RIGHT)
        with nc.Block() as block:
            @block.sync
            def _(sp):
                def load(b, par):
                    for k in range(2):
                        for n in range(SLOTS):
                            sp.dma_start(QK[n * DK:(n + 1) * DK, par, k], src[k, sides[k][n], :, :, bass.ds(b * S, S)]).then_inc(s_ld[par], 16)

                load(0, 0)
                load(1, 1)
                with sp.Fori(0, B // 2 - 1) as t:
                    for par in range(2):
                        sp.wait_ge(s_lg, (2 * t + par + 1) * HP)
                        load(2 * t + 2 + par, par)

            @block.tensor
            def _(pe):
                mm = nc.tensor.matmul

                def scores(b, par, h):
                    if h >= 2:
                        pe.wait_ge(s_max, b * H + h - 1)
                    for half in range(2):
                        last = mm(ps[:, h % 2, half * S:(half + 1) * S], QK[:, par, 0, h, half * P:(half + 1) * P], QK[:, par, 1, h],
                                  start=True, stop=True)
                    last.then_inc(s_sc, 1)

                def less_max(b, par, hp):
                    if hp >= 2:
                        pe.wait_ge(s_exp, b * HP + hp - 1)
                    pe.wait_ge(s_max, b * H + 2 * hp + 2)
                    for k in range(2):
                        h = 2 * hp + k
                        bank = ps[:, 2 + 2 * (hp % 2) + k]
                        for jh in range(2):
                            mm(bank[:, jh * S:(jh + 1) * S], QK[:, par, 1, h, jh * P:(jh + 1) * P], QK[:, par, 0, h],
                               start=jh == 0, stop=False, skip_group_check=True)
                        for jh in range(2):
                            for half in range(2):
                                at = jh * S + half * P
                                last = mm(bank[:, at:at + P], m[:, par, h, half:half + 1].to_broadcast([P, P]), g.negIB[:],
                                          start=False, stop=True, skip_group_check=True)
                    last.then_inc(s_lg, 1)

                def weigh(b, par, grp):
                    pe.wait_ge(s_exp, b * HP + 2 * grp + 2)
                    if grp % 2 == 0:
                        pe.wait_ge(s_ot, b * 2 + grp // 2 + 1)
                    for jh in range(2):
                        for k in range(4):
                            last = mm(ps[32 * k:32 * k + PADV, 6 + grp // 2, (grp % 2) * S:(grp % 2 + 1) * S],
                                      Vs[:, par, jh, 4 * grp + k], PT[:, grp % 2, k, jh], start=jh == 0, stop=jh == 1, skip_group_check=True)
                    last.then_inc(s_pv, 1)

                pe.wait_ge(s_pad, 2)
                with pe.Fori(0, B // 2) as t:
                    for par in range(2):
                        b = 2 * t + par
                        pe.wait_ge(s_ld[par], t * (2 * SLOTS * 16) + 2 * SLOTS * 16)
                        pe.wait_ge(s_vs, b + 1)
                        for h in range(4):
                            scores(b, par, h)
                        for hp in range(HP):
                            less_max(b, par, hp)
                            for h in (2 * hp + 4, 2 * hp + 5):
                                if h < H:
                                    scores(b, par, h)
                            if hp % 2 == 0 and hp:
                                weigh(b, par, hp // 2 - 1)
                        weigh(b, par, NG - 1)

            @block.gpsimd
            def _(pool):
                nc.gpsimd.memset(Vs[:, :, :, :, DK:PADV], 0.0).then_inc(s_pad, 1)
                pool.wait_ge(s_pad, 1)
                nc.gpsimd.memset(Vs[:, :, :, :, DK:DK + 1], 1.0).then_inc(s_pad, 1)

            @block.scalar
            def _(act):
                with act.Fori(0, B // 2) as t:
                    for par in range(2):
                        b = 2 * t + par
                        nc.scalar.activation(Vs[:, par, :, :, 0:DK], g.V2[:, bass.ds(2 * b, 2)], ACT.Copy).then_inc(s_vs, 1)
                        for hp in range(HP):
                            act.wait_ge(s_lg, b * HP + hp + 1)
                            if hp >= 4:
                                act.wait_ge(s_pv, b * NG + hp // 2 - 1)
                            grp, k = hp // 2, 2 * (hp % 2)
                            nc.scalar.activation(PT[:, grp % 2, k:k + 2], ps[:, 2 + 2 * (hp % 2):4 + 2 * (hp % 2)].rearrange("p k (j i) -> p k j i", j=2),
                                                 ACT.Exp, scale=QK_SCALE).then_inc(s_exp, 1)

            @block.vector
            def _(dve):
                def keep_out(b, x):
                    dve.wait_ge(s_pv, b * NG + 2 * x + 2)
                    nc.vector.tensor_copy(g.OT[:, bass.ds(2 * b, 2), 2 * x:2 * x + 2], ps[:, 6 + x].rearrange("p (g f i) -> p f g i", g=2, f=2)
                                          ).then_inc(s_ot, 1)

                for n in range(2):
                    nc.vector.memset(m[0:1, n, 0, 0:1], 0.0).then_inc(s_ot, 1)
                dve.wait_ge(s_ot, 2)
                with dve.Fori(0, B // 2) as t:
                    for par in range(2):
                        b = 2 * t + par
                        for h in range(H):
                            dve.wait_ge(s_sc, b * H + h + 1)
                            nc.vector.reduce_max(m[:, par, h], ps[:, h % 2].rearrange("p (f j) -> p f j", f=2), AX.X).then_inc(s_max, 1)
                            if h == 13:
                                keep_out(b, 0)
                        keep_out(b, 1)


def route(nc, g, a):
    sem, ps = g.sem, g.ps
    (s_in, s_h, s_x2, s_var, s_r2, s_hn, s_ht, s_htc, s_h2, s_lg, s_d, s_e, s_d2, s_e2, s_dv, s_half, s_done, s_apart) = (
        sem("rt_" + n) for n in "in h x2 var r2 hn ht htc h2 logits diff exp diff2 exp2 dve half done apart".split())
    with ExitStack() as c:
        def sb(n, sh, dt):
            return c.enter_context(nc.sbuf_tensor("rt_" + n, sh, dt))
        s = head_buffers(g, c, nc, "rt_")
        st, mv, half = sb("st", [P, GT, 6], F32), sb("mv", [P, GT, 6], F32), sb("half", [P, GT], F32)
        X2, hn, hT = sb("X2", [P, GT, D], F32), sb("hn", [P, GT, D], F32), sb("hT", [P, DC, GT * P], F32)
        w2, W, rw, iota = sb("w2", [P, D], F32), sb("W", [P, DC, D], F32), sb("rw", [P, DC, E], F32), sb("iota", [P, E], F32)
        lg, v8, ix, es = sb("lg", [P, GT, E], F32), sb("v8", [P, GT, E], F32), sb("ix", [P, GT, E], U32), sb("es", [P, GT, E], F32)
        fx, p, ed, cb = sb("fx", [P, GT, 2], F32), sb("p", [P, GT, 4], F32), sb("ed", [P, GT], F32), sb("cb", [P, GT, 2, E], F32)
        cw = sb("cw", [P, GT, 2], F32)
        with nc.Block() as block:
            @block.sync
            def _(sp):
                for o, i in ((W, a["wo"]), (w2, a["w2"]), (rw, a["rw"]), (iota, a["iota"])):
                    sp.dma_start(o[:], i).then_inc(s_in, 16)

            @block.gpsimd
            def _(pool):
                nc.gpsimd.memset(half[:], -0.5).then_inc(s_half, 1)
                pool.wait_ge(s_half, 1)
                with pool.Fori(0, GN) as t:
                    pool.wait_ge(s_var, t + 1)
                    nc.gpsimd.tensor_tensor(mv[:, :, 4], mv[:, :, 3], half[:], ALU.pow).then_inc(s_r2, 1)

            @block.tensor
            def _(pe):
                mm = nc.tensor.matmul
                pe.wait_ge(s_in, 64)
                with pe.Fori(0, GN) as t:
                    pe_turn_heads(nc, pe, g, s, t)
                    pe.wait_ge(s.attc, t + 1)
                    for k in range(GT):
                        for cc in range(DC):
                            last = mm(ps[:, k // 2, (k % 2) * D:(k % 2 + 1) * D], s.ATT[:, cc, k * P:(k + 1) * P], W[:, cc],
                                      start=cc == 0, stop=cc == DC - 1)
                    last.then_inc(s_h, 1)
                    pe.wait_ge(s_hn, GT * (t + 1))
                    for k in range(GT):
                        for cc in range(DC):
                            last = nc.tensor.transpose(ps[:, 2 + cc, k * P:(k + 1) * P], hn[:, k, cc * P:(cc + 1) * P], g.identF[:])
                    last.then_inc(s_ht, 1)
                    pe.wait_ge(s_htc, t + 1)
                    for k in range(GT):
                        for cc in range(DC):
                            last = mm(ps[:, 6, k * E:(k + 1) * E], hT[:, cc, k * P:(k + 1) * P], rw[:, cc], start=cc == 0, stop=cc == DC - 1)
                    last.then_inc(s_lg, 1)
                    pe.wait_ge(s_done, t + 1)

            @block.scalar
            def _(act):
                act.wait_ge(s_in, 64)
                with act.Fori(0, GN) as t:
                    act.wait_ge(s.att, t + 1)
                    nc.scalar.activation(s.ATT[:], ps[:, 4:6], ACT.Copy).then_inc(s.attc, 1)
                    act.wait_ge(s_ht, t + 1)
                    nc.scalar.activation(hT[:], ps[:, 2:4], ACT.Copy).then_inc(s_htc, 1)
                    act.wait_ge(s_htc, t + 1)
                    nc.scalar.activation(g.H2T[:, :, bass.ds(t * (GT * P), GT * P)], hT[:], ACT.Copy).then_inc(s_h2, 1)
                    act.wait_ge(s_d, t + 1)
                    nc.scalar.activation(es[:], es[:], ACT.Exp).then_inc(s_e, 1)
                    act.wait_ge(s_d2, t + 1)
                    nc.scalar.activation(ed[:], ed[:], ACT.Exp).then_inc(s_e2, 1)

            @block.vector
            def _(dve):
                V = nc.vector
                do = Chain(dve, s_dv)
                dve.wait_ge(s_in, 64)
                do(V.memset(g.comb[:], 1.0))
                with dve.Fori(0, GN) as t:
                    do.enter(t, 11 + 7 * GT)
                    dve_divide_heads(nc, dve, g, s, t)
                    dve.wait_ge(s_h, t + 1)
                    V.tensor_tensor(X2[:], ps[:, 0:2].rearrange("p a (k d) -> p (a k) d", d=D), g.XS[:, bass.ds(t * GT, GT)], ALU.add).then_inc(s_x2, 1)
                    dve.wait_ge(s_x2, t + 1)
                    for k in range(GT):
                        do(V.bn_stats(st[:, k], X2[:, k]), s_apart)
                        do(V.bn_aggr(mv[:, k, 0:2], st[:, k]))
                    do(V.tensor_tensor(mv[:, :, 2], mv[:, :, 0], mv[:, :, 0], ALU.mult))
                    do(V.tensor_tensor(mv[:, :, 2], mv[:, :, 2], mv[:, :, 1], ALU.add))
                    V.tensor_scalar(mv[:, :, 3], mv[:, :, 2], RMS_EPS, None, ALU.add).then_inc(s_var, 1)
                    do(V.tensor_tensor(g.HS[:, bass.ds(t * GT, GT)], g.HS[:, bass.ds(t * GT, GT)], X2[:], ALU.add))
                    dve.wait_ge(s_r2, t + 1)
                    for k in range(GT):
                        V.scalar_tensor_tensor(hn[:, k], X2[:, k], mv[:, k, 4:5], w2[:], ALU.mult, ALU.mult).then_inc(s_hn, 1)
                    dve.wait_ge(s_lg, t + 1)
                    do(V.tensor_copy(lg[:], ps[:, 6, 0:GT * E].rearrange("p (k e) -> p k e", e=E)), s_apart)
                    for k in range(GT):
                        do(V.max(v8[:, k], lg[:, k]), s_apart)
                        do(V.max_index(ix[:, k], v8[:, k], lg[:, k]), s_apart)
                    V.tensor_tensor(es[:], v8[:], v8[:, :, 0:1].to_broadcast([P, GT, E]), ALU.subtract).then_inc(s_d, 1)
                    do(V.tensor_copy(fx[:], ix[:, :, 0:2]))
                    dve.wait_ge(s_e, t + 1)
                    do(V.reduce_sum(p[:, :, 0], es[:], AX.X))
                    do(V.reciprocal(p[:, :, 1], p[:, :, 0]))
                    do(V.tensor_tensor(p[:, :, 2], es[:, :, 1], p[:, :, 1], ALU.mult))
                    V.tensor_tensor(ed[:], p[:, :, 2], p[:, :, 1], ALU.subtract).then_inc(s_d2, 1)
                    dve.wait_ge(s_e2, t + 1)
                    do(V.tensor_scalar(p[:, :, 3], ed[:], 1.0, None, ALU.add))
                    do(V.reciprocal(cw[:, :, 0], p[:, :, 3]))
                    do(V.tensor_tensor(cw[:, :, 1], cw[:, :, 0], ed[:], ALU.mult))
                    for k in range(GT):
                        for n in range(2):
                            do(V.tensor_scalar(cb[:, k, n], iota[:], fx[:, k, n:n + 1], cw[:, k, n:n + 1], ALU.is_equal, ALU.mult))
                        do(V.tensor_tensor(g.comb[:, bass.ds(t * GT + k, 1), 0:E], cb[:, k:k + 1, 0], cb[:, k:k + 1, 1], ALU.add))
                    V.memset(p[:, 0, 0:1], 0.0).then_inc(s_done, 1)
                    dve.wait_ge(s_done, t + 1)
                    do.leave(GN)


def experts(nc, g, a, outs):
    sem, ps = g.sem, g.ps
    s_hid, s_sil, s_act_, s_y, s_acc, s_out = (sem("ex_" + n) for n in "hidden silu act y acc out".split())
    s_w = [sem("ex_w" + n) for n in names(2)]
    NE = E + 1
    with ExitStack() as c:
        def sb(n, sh, dt):
            return c.enter_context(nc.sbuf_tensor("ex_" + n, sh, dt))
        WG, WU, WD = sb("WG", [P, 2, DC, F], F32), sb("WU", [P, 2, DC, F], F32), sb("WD", [P, 2, FC, D], F32)
        sil, hid = sb("sil", [P, 2, 512], F32), sb("hid", [P, 2, FC, 512], F32)
        rounds = [(e, tg) for e in range(NE) for tg in range(4)]
        with nc.Block() as block:
            @block.sync
            def _(sp):
                for e in range(NE):
                    if e >= 2:
                        sp.wait_ge(s_y, 4 * (e - 1))
                    for o, i in ((WG, a["sh_gate"] if e == E else a["e_gate"][e]), (WU, a["sh_up"] if e == E else a["e_up"][e]), (WD, a["sh_down"] if e == E else a["e_down"][e])):
                        sp.dma_start(o[:, e % 2], i.rearrange("(c p) f -> p c f", p=P)).then_inc(s_w[e % 2], 16)
                sp.wait_ge(s_acc, len(rounds))
                sp.dma_start(outs.rearrange("(t p) d -> p t d", p=P), g.HS[:]).then_inc(s_out, 16)
                sp.wait_ge(s_out, 16)

            @block.tensor
            def _(pe):
                mm = nc.tensor.matmul

                def up(r):
                    e, tg = rounds[r]
                    if tg == 0:
                        pe.wait_ge(s_w[e % 2], 48 * (e // 2 + 1))
                    for f in range(FC):
                        n = r * FC + f
                        if n >= 2:
                            pe.wait_ge(s_act_, n - 1)
                        for w, bk in ((WG, 2 * (n % 2)), (WU, 2 * (n % 2) + 1)):
                            for cc in range(DC):
                                last = mm(ps[:, bk], w[:, e % 2, cc, f * P:(f + 1) * P], g.H2T[:, cc, tg * 512:(tg + 1) * 512], start=cc == 0, stop=cc == 1)
                        last.then_inc(s_hid, 1)

                def down(r):
                    e, tg = rounds[r]
                    pe.wait_ge(s_act_, FC * (r + 1))
                    if r >= 2:
                        pe.wait_ge(s_acc, r - 1)
                    for k in range(4):
                        for f in range(FC):
                            last = mm(ps[:, 4 + 2 * (r % 2) + k // 2, (k % 2) * D:(k % 2 + 1) * D], hid[:, r % 2, f, k * P:(k + 1) * P], WD[:, e % 2, f], start=f == 0, stop=f == 3)
                    last.then_inc(s_y, 1)

                for r in range(len(rounds)):
                    up(r)
                    if r:
                        down(r - 1)
                down(len(rounds) - 1)

            @block.scalar
            def _(act):
                for n in range(len(rounds) * FC):
                    act.wait_ge(s_hid, n + 1)
                    if n >= 2:
                        act.wait_ge(s_act_, n - 1)
                    nc.scalar.activation(sil[:, n % 2], ps[:, 2 * (n % 2)], ACT.Silu).then_inc(s_sil, 1)

            @block.vector
            def _(dve):
                def acc(r):
                    e, tg = rounds[r]
                    dve.wait_ge(s_y, r + 1)
                    if r >= 4:
                        dve.wait_ge(s_acc, r - 3)
                    for k in range(4):
                        tile = 4 * tg + k
                        last = nc.vector.scalar_tensor_tensor(g.HS[:, tile], ps[:, 4 + 2 * (r % 2) + k // 2, (k % 2) * D:(k % 2 + 1) * D],
                                                              g.comb[:, tile, e:e + 1], g.HS[:, tile], ALU.mult, ALU.add)
                    last.then_inc(s_acc, 1)

                for r in range(len(rounds)):
                    for f in range(FC):
                        n = r * FC + f
                        dve.wait_ge(s_sil, n + 1)
                        nc.vector.tensor_tensor(hid[:, r % 2, f], ps[:, 2 * (n % 2) + 1], sil[:, n % 2], ALU.mult).then_inc(s_act_, 1)
                    if r:
                        acc(r - 1)
                acc(len(rounds) - 1)


def kernel(**inputs):
    import numpy as np
    import concourse.bacc as bacc
    from concourse.bass_utils import run_bass_kernel_spmd

    def given(name):
        return np.asarray(inputs[name])

    def rows(w):
        return np.ascontiguousarray(w.reshape(DC, P, -1).transpose(1, 0, 2))

    sel = np.zeros((B, B, L3), np.float32)
    sel[np.arange(B), np.arange(B)] = 1
    arrays = dict(
        x=given("x"), sel=sel, lvl=(np.arange(L3) % L).astype(np.float32)[:, None].copy(),
        iota=np.ascontiguousarray(np.broadcast_to(np.arange(E, dtype=np.float32), (P, E))),
        er=np.ascontiguousarray(given("L0_attn_Er")[::-1].reshape(4, P, DK).transpose(1, 0, 2)), emb=given("L0_tok_level_emb"),
        ident=np.eye(P, dtype=np.float32), bo=np.ascontiguousarray(np.broadcast_to(given("L0_attn_bo"), (L, D))),
        bias=np.ascontiguousarray(np.broadcast_to(np.stack([given("L0_attn_b" + k) for k in "qkv"]), (L, 3, D))),
        w1=np.ascontiguousarray(np.broadcast_to(given("L0_ffn_norm1_w"), (P, D))),
        w2=np.ascontiguousarray(np.broadcast_to(given("L0_ffn_norm2_w"), (P, D))),
        **{k + "T": rows(given("L0_attn_" + k).T) for k in ("Wq", "Wk", "Wv", "Wo")},
        **{k: rows(given("L0_ffn_" + k)) for k in ("wq", "wk", "wv", "wo")},
        rw=rows(given("L0_ffn_router_w")),
        **{k: given("L0_ffn_" + k) for k in ("sh_gate", "sh_up", "sh_down", "e_gate", "e_up", "e_down")})
    nc = bacc.Bacc("TRN2", target_bir_lowering=False, num_devices=1)
    aps = {n: nc.dram_tensor("in_" + n, v.shape, mybir.dt.from_np(v.dtype), kind="ExternalInput").ap() for n, v in arrays.items()}
    out = nc.dram_tensor("out", [T, D], F32, kind="ExternalOutput").ap()
    build_program(nc, aps, out)
    r = run_bass_kernel_spmd(nc, [{"in_" + n: v for n, v in arrays.items()}], core_ids=[0])
    return r.results[0]["out"].reshape(B, S, D)
```

```python
import concourse.bass as bass
from concourse import mybir
from contextlib import ExitStack

F32 = mybir.dt.float32
F32R = mybir.dt.float32r
BF16 = mybir.dt.bfloat16
I32 = mybir.dt.int32
U32 = mybir.dt.uint32
ALU = mybir.AluOpType
ACT = mybir.ActivationFunctionType
AX = mybir.AxisListType

B, S, D = 8, 256, 256
T = B * S
H, DK = 16, 16
L = 32
E, F = 8, 512
P = 128
NT = T // P
DC = D // P
FC = F // P
QK_SCALE = 1.0 / DK ** 0.5
EMB_SCALE = 0.15
LN_EPS, RMS_EPS = 1e-5, 1e-6

LEFT = (0, 0, 1, 0, 2, 1)
RIGHT = (0, 1, 0, 2, 0, 1)
SLOTS = len(LEFT)
KP = SLOTS * DK
L3 = 3 * L

BP = 2
NPAIR = B // BP
QI = 16
STEPS = P // QI
COLS = BP * H * QI
PADV = 32
SLOTS_X = (2 * T + E * (P - 1)) // P
NG = H // 4


class Shared:
    pass


def names(n):
    return [str(i) for i in range(n)]


class Chain:

    def __init__(self, eng, sem):
        self.eng, self.sem, self.base, self.k, self.trip, self.per = eng, sem, 0, 0, None, 0

    def enter(self, trip, per):
        self.base, self.k, self.trip, self.per = self.base + self.k, 0, trip, per

    def leave(self, trips):
        assert self.k == self.per, self.k
        self.base, self.k, self.trip = self.base + trips * self.per, 0, None

    def __call__(self, ins, apart=None):
        ins.then_inc(self.sem, 1)
        self.k += 1
        done = self.base + self.k
        self.eng.wait_ge(self.sem, done if self.trip is None else self.trip * self.per + done)
        if apart is not None:
            self.eng.sem_inc(apart)


def build_program(nc, a, outs):
    ctx = ExitStack()
    with ctx:
        def sem(name):
            return ctx.enter_context(nc.semaphore(name))

        def kept(name, shape, dt):
            return ctx.enter_context(nc.sbuf_tensor(name, shape, dt))

        g = Shared()
        g.sem = sem
        g.ps = ctx.enter_context(nc.psum_tensor("ps", [P, 8, 512], F32))
        g.identF = kept("identF", [P, P], F32)
        g.identB = kept("identB", [P, P], BF16)
        g.negIB = kept("negIB", [P, P], BF16)
        g.xs = nc.dram_tensor("expert_in", [SLOTS_X * P, D], F32, kind="Internal").ap()
        g.ys = nc.dram_tensor("expert_out", [SLOTS_X * P, D], F32, kind="Internal").ap()
        g.qd = nc.dram_tensor("qk_parts", [2, 3, D, T], BF16, kind="Internal").ap()
        g.HS = kept("HS", [P, NT, D], F32)
        g.V2 = kept("V2", [P, NT, H, DK], F32)
        g.H2T = g.V2[:].rearrange("p t h d -> p (t h d)").rearrange("p (c t) -> p c t", c=DC)
        g.XS = kept("XS", [P, NT, D], F32)
        g.pick = kept("pick", [P, 2, NT, E], F32)
        g.share = kept("share", [P, NT, 2], F32)
        with ExitStack() as mid:
            g.OT = mid.enter_context(nc.sbuf_tensor("OT", [P, NT, NG, P], F32))
            with ExitStack() as low:
                def lo(name, shape, dt):
                    return low.enter_context(nc.sbuf_tensor(name, shape, dt))
                g.WoT = lo("WoT", [P, DC, D], F32)
                g.R3 = lo("R3", [L3, D], BF16)
                g.OH3 = lo("OH3", [L3, (NPAIR + 1) * BP * S], BF16)
                g.ErT = lo("ErT", [KP, 2 * S], BF16)
                g.QT = lo("QT", [L, H, KP], BF16)
                g.ACP = lo("ACP", [L, H, L3], BF16)
                g.V3 = lo("V3", [L3, D], BF16)
                tables(nc, g, a)
                level_attention(nc, g)
                project(nc, g, a)
            full_attention(nc, g)
            route(nc, g, a)
        experts(nc, g, a, outs)


def tables(nc, g, a):
    sem, ps = g.sem, g.ps
    s_in = [sem("in_" + n) for n in ("tok", "tab", "w", "er", "id")]
    s_dve, s_act, s_pool = sem("tab_dve"), sem("tab_act"), sem("tab_pool")
    s_lv, s_lvp, s_ln, s_xt, s_xtc, s_proj, s_sp, s_qkT, s_qkTc, s_ac, s_er, s_erT, s_idb, s_rs, s_zero, s_zd = (
        sem("tab_" + n) for n in "levels levelsB norm xT xTc proj split qkT qkTc ac er erT idb rstd zero zeroed".split())
    with ExitStack() as c:
        def sb(n, sh, dt):
            return c.enter_context(nc.sbuf_tensor("t_" + n, sh, dt))
        tok, tokf = sb("tok", [B, S], I32), sb("tokf", [B, S], F32)
        acc, Dl, nD, rD, zer, lev = (sb(n, [B, S], F32) for n in ("acc", "Dl", "nD", "rD", "zer", "lev"))
        sel, lvl = sb("sel", [B, B, L3], F32), sb("lvl", [L3, 1], F32)
        emb, xt, bo = sb("emb", [L, D], F32), sb("xt", [L, D], F32), sb("bo", [L, D], F32)
        st, mv, half = sb("st", [L, 6], F32), sb("mv", [L, 4], F32), sb("half", [L, 1], F32)
        xT = sb("xT", [P, DC, L], F32)
        W = sb("W", [P, 3, DC, D], F32)
        zfill = sb("zfill", [P, SLOTS_X // 3 * D], F32)
        bias, tab = sb("bias", [L, 3, D], F32), sb("tab", [L, 3, D], F32)
        r1, r2 = sb("r1", [L, 3, D], F32), sb("r2", [L, 3, D], F32)
        parts = [sb("part" + i, [L, 3, D], BF16) for i in names(3)]
        KT = sb("KT", [L, H, KP], BF16)
        qkT = sb("qkT", [KP, 2, H, L], BF16)
        er, e1, e2 = sb("er", [P, 4, DK], F32), sb("e1", [P, 4, DK], F32), sb("e2", [P, 4, DK], F32)
        eparts = [sb("epart" + i, [P, 4, DK], BF16) for i in names(3)]
        EP = sb("EP", [P, 4, SLOTS, DK], BF16)
        ac, a1, a2 = sb("ac", [L, H, L], F32), sb("a1", [L, H, L], F32), sb("a2", [L, H, L], F32)
        rr, rr1, rr2 = sb("rr", [L, D], F32), sb("rr1", [L, D], F32), sb("rr2", [L, D], F32)
        psf = ps[:].rearrange("p a b -> p (a b)")
        with nc.Block() as block:
            @block.sync
            def _(sp):
                sp.dma_start(tok[:], a["x"]).then_inc(s_in[0], 16)
                sp.dma_start(sel[:], a["sel"]).then_inc(s_in[0], 16)
                sp.dma_start(lvl[:], a["lvl"]).then_inc(s_in[0], 16)
                sp.dma_start(er[:], a["er"]).then_inc(s_in[3], 16)
                sp.dma_start(g.WoT[:], a["WoT"]).then_inc(s_in[2], 16)
                sp.wait_ge(s_zero, 1)
                zrows = g.xs.rearrange("(n p r) d -> n p (r d)", n=3, p=P)
                for n in range(3):
                    sp.dma_start(zrows[n], zfill[:]).then_inc(s_zd, 16)
                sp.wait_ge(s_zd, 48)
                sp.wait_ge(s_in[2], 64)

            @block.scalar
            def _(act):
                act.dma_start(emb[:], a["emb"]).then_inc(s_in[1], 16)
                act.dma_start(g.identF[:], a["ident"]).then_inc(s_in[4], 16)
                act.dma_start(bo[:], a["bo"]).then_inc(s_in[1], 16)
                act.dma_start(bias[:], a["bias"]).then_inc(s_in[1], 16)
                for n, w in enumerate((a["WqT"], a["WkT"], a["WvT"])):
                    act.dma_start(W[:, n], w).then_inc(s_in[2], 16)

            @block.gpsimd
            def _(pool):
                nc.gpsimd.memset(half[:], -0.5).then_inc(s_pool, 1)
                nc.gpsimd.memset(zfill[:], 0.0).then_inc(s_zero, 1)
                pool.wait_ge(s_pool, 1)
                pool.wait_ge(s_ln, 1)
                nc.gpsimd.tensor_tensor(mv[:, 3:4], mv[:, 2:3], half[:], ALU.pow).then_inc(s_rs, 1)

            @block.vector
            def _(dve):
                do = Chain(dve, s_dve)
                V = nc.vector
                do(V.memset(zer[:], 0.0))
                dve.wait_ge(s_in[0], 48)
                do(V.tensor_copy(tokf[:], tok[:]))
                do(V.tensor_scalar(acc[:], tokf[:], 41.0, None, ALU.is_equal))
                for close in (93.0, 125.0):
                    do(V.scalar_tensor_tensor(acc[:], tokf[:], close, acc[:], ALU.is_equal, ALU.add))
                do(V.scalar_tensor_tensor(acc[:], tokf[:], 40.0, acc[:], ALU.is_equal, ALU.subtract))
                for opened in (91.0, 123.0):
                    do(V.scalar_tensor_tensor(acc[:], tokf[:], opened, acc[:], ALU.is_equal, ALU.add))
                do(V.tensor_tensor_scan(Dl[:], acc[:], zer[:], 0.0, ALU.add, ALU.add))
                do(V.tensor_scalar(nD[:], Dl[:], -1.0, None, ALU.mult))
                do(V.tensor_scalar(rD[:], Dl[:], -1.0, float(L - 1), ALU.mult, ALU.add))
                do(V.tensor_tensor_scan(acc[:], nD[:], rD[:], 0.0, ALU.max, ALU.min))
                V.tensor_tensor(lev[:], acc[:], Dl[:], ALU.add).then_inc(s_lv, 1)
                dve.wait_ge(s_in[1], 48)
                dve.wait_ge(s_in[4], 16)
                do(V.tensor_scalar(emb[:], emb[:], EMB_SCALE, None, ALU.mult))
                do(V.bn_stats(st[:], emb[:]))
                do(V.bn_aggr(mv[:, 0:2], st[:]))
                V.tensor_scalar(mv[:, 2:3], mv[:, 1:2], LN_EPS, None, ALU.add).then_inc(s_ln, 1)
                V.tensor_copy(g.identB[:], g.identF[:]).then_inc(s_idb, 1)
                V.tensor_scalar(g.negIB[:], g.identF[:], -1.0, None, ALU.mult).then_inc(s_idb, 1)
                dve.wait_ge(s_rs, 1)
                V.tensor_scalar(xt[:], emb[:], mv[:, 0:1], mv[:, 3:4], ALU.subtract, ALU.mult).then_inc(s_ln, 1)
                do(V.memset(g.OH3[:, T:], 0.0))
                for q in range(4):
                    dve.wait_ge(s_lvp, q + 1)
                    do(V.tensor_scalar(g.OH3[:, q * 512:(q + 1) * 512], ps[0:L3, q, :], lvl[:, 0:1], None, ALU.is_equal))

                def split(src, r, rr_, out):
                    do(V.tensor_copy(out[0], src))
                    do(V.tensor_tensor(r, src, out[0], ALU.subtract))
                    do(V.tensor_copy(out[1], r))
                    do(V.tensor_tensor(rr_, r, out[1], ALU.subtract))
                    do(V.tensor_copy(out[2], rr_))

                dve.wait_ge(s_in[3], 16)
                split(er[:], e1[:], e2[:], [x[:] for x in eparts])
                for n in range(SLOTS):
                    do(V.tensor_copy(EP[:, :, n], eparts[RIGHT[n]][:]))
                V.memset(zer[0:1, 0:1], 0.0).then_inc(s_er, 1)
                do(V.tensor_tensor(rr[:], emb[:], bo[:], ALU.add))
                split(rr[:], rr1[:], rr2[:], [g.R3[n * L:(n + 1) * L] for n in range(3)])
                dve.wait_ge(s_xt, 1)
                V.tensor_copy(xT[:], psf[:, 2048:2048 + DC * L].rearrange("p (c l) -> p c l", c=DC)).then_inc(s_xtc, 1)
                for n in range(3):
                    dve.wait_ge(s_proj, n + 1)
                    do(V.tensor_tensor(tab[:, n], ps[0:L, 5 + n % 2, 0:D], bias[:, n], ALU.add))
                    V.memset(zer[0:1, 0:1], 0.0).then_inc(s_sp, 1)
                split(tab[:], r1[:], r2[:], [x[:] for x in parts])
                heads = [[x[:, n].rearrange("p (h d) -> p h d", h=H) for x in parts] for n in range(2)]
                for n in range(SLOTS):
                    at = slice(n * DK, (n + 1) * DK)
                    do(V.tensor_copy(g.QT[:, :, at], heads[0][LEFT[n]]))
                    do(V.tensor_copy(KT[:, :, at], heads[1][RIGHT[n]]))
                V.memset(zer[0:1, 0:1], 0.0).then_inc(s_sp, 1)
                for n in range(3):
                    do(V.tensor_copy(g.V3[n * L:(n + 1) * L], parts[n][:, 2]))
                dve.wait_ge(s_erT, 1)
                do(V.tensor_copy(g.ErT[:], ps[0:KP, 0].bitcast(BF16)[:, 0:512]))
                dve.wait_ge(s_qkT, 1)
                for n in range(2):
                    do(V.tensor_copy(qkT[:, n].rearrange("p h l -> p (h l)"), ps[0:KP, 1 + n].bitcast(BF16)[:, 0:512]))
                V.memset(zer[0:1, 0:1], 0.0).then_inc(s_qkTc, 1)
                dve.wait_ge(s_ac, 1)
                do(V.tensor_copy(ac[:], ps[0:L, 3].rearrange("p (h l) -> p h l", h=H)))
                split(ac[:], a1[:], a2[:], [g.ACP[:, :, n * L:(n + 1) * L] for n in range(3)])

            @block.tensor
            def _(pe):
                mm = nc.tensor.matmul
                pe.wait_ge(s_lv, 1)
                for b in range(B):
                    last = mm(ps[0:L3, b // 2, (b % 2) * S:(b % 2 + 1) * S], sel[:, b], lev[:], start=True, stop=True)
                    if b % 2:
                        last.then_inc(s_lvp, 1)
                pe.wait_ge(s_ln, 2)
                pe.wait_ge(s_in[4], 16)
                for n in range(DC):
                    last = nc.tensor.transpose(psf[:, 2048 + n * L:2048 + (n + 1) * L], xt[:, n * P:(n + 1) * P], g.identF[0:L, 0:L])
                last.then_inc(s_xt, 1)
                pe.wait_ge(s_xtc, 1)
                pe.wait_ge(s_in[2], 64)
                for n in range(3):
                    if n >= 2:
                        pe.wait_ge(s_sp, n - 1)
                    for c_ in range(DC):
                        last = mm(ps[0:L, 5 + n % 2, 0:D], xT[:, c_], W[:, n, c_], start=c_ == 0, stop=c_ == DC - 1)
                    last.then_inc(s_proj, 1)
                pe.wait_ge(s_er, 1)
                pe.wait_ge(s_idb, 2)
                for n in range(4):
                    last = nc.tensor.transpose(ps[0:KP, 0].bitcast(BF16)[:, n * P:(n + 1) * P], EP[:, n].rearrange("p s d -> p (s d)"), g.identB[:])
                last.then_inc(s_erT, 1)
                pe.wait_ge(s_sp, 4)
                for n, t in enumerate((g.QT, KT)):
                    for h in range(H):
                        last = nc.tensor.transpose(ps[0:KP, 1 + n].bitcast(BF16)[:, h * L:(h + 1) * L], t[:, h], g.identB[0:L, 0:L])
                last.then_inc(s_qkT, 1)
                pe.wait_ge(s_qkTc, 1)
                for h in range(H):
                    last = mm(ps[0:L, 3, h * L:(h + 1) * L], qkT[:, 0, h], qkT[:, 1, h], start=True, stop=True)
                last.then_inc(s_ac, 1)


def level_attention(nc, g):
    sem, ps = g.sem, g.ps
    (s_built, s_evac, s_mx, s_tr, s_m, s_ready, s_exp, s_qp, s_qb, s_ap, s_ab, s_vp, s_vs, s_pv, s_ot, s_ms, s_apart) = (
        sem("la_" + n) for n in ("built evac halfmax turned max ready exp q_made q_kept a_made a_kept "
                                 "v_made v_kept pv out init apart").split())
    NS = 2 * STEPS
    UN = H // 2
    with ExitStack() as c:
        def sb(n, sh, dt):
            return c.enter_context(nc.sbuf_tensor("la_" + n, sh, dt))
        QB = sb("QB", [KP, 2, BP, H, P], BF16)
        AQ = sb("AQ", [L3, 2, BP, H, P], BF16)
        SA = sb("SA", [P, 2, COLS], BF16)
        SM = sb("SM", [P, 2, COLS], BF16)
        m = sb("m", [P, 2, 4], BF16)
        PT = sb("PT", [P, 2, 2, BP * H, P], F32)
        Vs = sb("Vs", [P, BP, 2, H, PADV], F32)
        OHq = g.OH3[0:L].rearrange("p (q b f i) -> p q b f i", b=BP, f=2, i=P)
        XT = ps[:, 4].bitcast(BF16)[:, 0:512]
        with nc.Block() as block:
            @block.gpsimd
            def _(pool):
                nc.gpsimd.memset(Vs[:, :, :, :, DK:PADV], 0.0).then_inc(s_ms, 1)
                pool.wait_ge(s_ms, 1)
                nc.gpsimd.memset(Vs[:, :, :, :, DK:DK + 1], 1.0).then_inc(s_ms, 1)

            @block.tensor
            def _(pe):
                mm = nc.tensor.matmul

                def make_unit(pair, half, u, made):
                    pe.wait_ge(s_qb, made + 1)
                    pe.sem_inc(s_apart)
                    rhs = OHq[:, bass.ds(pair, 1), :, half, :]
                    for k in range(2):
                        last = mm(ps[0:KP, 6, k * BP * P:(k + 1) * BP * P], g.QT[:, 2 * u + k], rhs, start=True, stop=True)
                    last.then_inc(s_qp, 1)
                    pe.wait_ge(s_ab, made + 1)
                    pe.sem_inc(s_apart)
                    for k in range(2):
                        last = mm(ps[0:L3, 7, k * BP * P:(k + 1) * BP * P], g.ACP[:, 2 * u + k], rhs, start=True, stop=True)
                    last.then_inc(s_ap, 1)

                def build(pair, n):
                    half, k = divmod(n, STEPS)
                    q0 = k * QI
                    if n >= 2:
                        pe.wait_ge(s_exp, pair * NS + n - 1)
                    for jh in range(2):
                        bank = ps[:, 2 * (n % 2) + jh]
                        for b in range(BP):
                            mm(bank[:, b * H * QI:(b + 1) * H * QI], g.OH3[:, bass.ds(pair * (BP * S) + b * S + jh * P, P)],
                               AQ[:, half, b, :, q0:q0 + QI], start=b == 0, stop=False, skip_group_check=True)
                        cols = bank.rearrange("p (h i) -> p h i", i=QI)
                        q = QB[:, half].rearrange("p b h i -> p (b h) i")
                        for i in range(QI):
                            w0 = S - (half * P + q0 + i) + jh * P
                            last = mm(cols[:, :, i], g.ErT[:, w0:w0 + P], q[:, :, q0 + i], start=False, stop=False,
                                      skip_group_check=True)
                    last.then_inc(s_built, 1)

                def turn(pair, n):
                    pe.wait_ge(s_mx, pair * NS + n + 1)
                    for q in range(4):
                        last = nc.tensor.transpose(XT[:, q * P:(q + 1) * P], SM[:, n % 2, q * P:(q + 1) * P], g.identB[:])
                    last.then_inc(s_tr, 1)

                def subtract_max(pair, n):
                    pe.wait_ge(s_m, pair * NS + n + 1)
                    for jh in range(2):
                        for q in range(4):
                            last = mm(ps[:, 2 * (n % 2) + jh, q * P:(q + 1) * P], m[:, n % 2, q:q + 1].to_broadcast([P, P]), g.negIB[:],
                                      start=False, stop=True, skip_group_check=True)
                    last.then_inc(s_ready, 1)

                def make_values(pair, b):
                    pe.wait_ge(s_vs, pair * BP + b + 1)
                    pe.wait_ge(s_ot, pair * 4 + 1)
                    for jh in range(2):
                        last = mm(ps[:, 5, jh * D:(jh + 1) * D], g.OH3[:, bass.ds(pair * (BP * S) + b * S + jh * P, P)], g.V3[:],
                                  start=True, stop=True)
                    last.then_inc(s_vp, 1)

                def weigh_values(pair, half, b):
                    pe.wait_ge(s_exp, pair * NS + (half + 1) * STEPS)
                    pe.wait_ge(s_vs, pair * BP + BP + 1)
                    pe.wait_ge(s_ot, pair * 4 + half * 2 + b + 1)
                    for grp in range(NG):
                        for jh in range(2):
                            for k in range(4):
                                h = 4 * grp + k
                                last = mm(ps[32 * k:32 * k + PADV, 5, grp * P:(grp + 1) * P], Vs[:, b, jh, h],
                                          PT[:, half, jh, b * H + h], start=jh == 0, stop=jh == 1, skip_group_check=True)
                    last.then_inc(s_pv, 1)

                pe.wait_ge(s_ms, 2)
                for u in range(UN):
                    make_unit(0, 0, u, u)
                with pe.Fori(0, NPAIR) as pair:
                    for n in range(NS):
                        half, k = divmod(n, STEPS)
                        if n == 0:
                            pe.wait_ge(s_qb, pair * (2 * UN) + UN + 1)
                            pe.wait_ge(s_ab, pair * (2 * UN) + UN + 1)
                            build(pair, 0)
                        if k < UN - 1:
                            for u in ((0, 1) if k == 0 else (k + 1,)):
                                make_unit(pair + half, 1 - half, u, pair * (2 * UN) + UN + half * UN + u)
                        if n + 1 < NS:
                            if k == STEPS - 1:
                                pe.wait_ge(s_qb, pair * (2 * UN) + 2 * UN + 1)
                                pe.wait_ge(s_ab, pair * (2 * UN) + 2 * UN + 1)
                            build(pair, n + 1)
                        turn(pair, n)
                        if n < BP:
                            make_values(pair, n)
                        if n in (STEPS + 1, STEPS + 4):
                            weigh_values(pair, 0, n == STEPS + 4)
                        subtract_max(pair, n)
                    for b in range(BP):
                        weigh_values(pair, 1, b)

            @block.scalar
            def _(act):
                def keep_unit(half, u, made):
                    act.wait_ge(s_ap, made)
                    nc.scalar.activation(AQ[:, half, :, 2 * u:2 * u + 2], ps[0:L3, 7].rearrange("p (h b i) -> p b h i", h=2, b=BP),
                                         ACT.Copy).then_inc(s_ab, 1)

                def copy_half(pair, n):
                    act.wait_ge(s_built, pair * NS + n + 1)
                    nc.scalar.activation(SA[:, n % 2], ps[:, 2 * (n % 2)], ACT.Copy).then_inc(s_evac, 1)

                nc.scalar.activation(AQ[0:1, 0, 0, 0, 0:1], g.identF[0:1, 0:1], ACT.Copy).then_inc(s_ab, 1)
                nc.scalar.activation(Vs[0:1, 0, 0, 0, 0:1], g.identF[0:1, 0:1], ACT.Copy).then_inc(s_vs, 1)
                act.wait_ge(s_vs, 1)
                act.wait_ge(s_ab, 1)
                for u in range(UN):
                    keep_unit(0, u, u + 1)
                with act.Fori(0, NPAIR) as pair:
                    copy_half(pair, 0)
                    for n in range(NS):
                        half, k = divmod(n, STEPS)
                        if k < UN - 1:
                            for u in ((0, 1) if k == 0 else (k + 1,)):
                                keep_unit(1 - half, u, pair * (2 * UN) + UN + half * UN + u + 1)
                        if n + 1 < NS:
                            copy_half(pair, n + 1)
                        if n < BP:
                            act.wait_ge(s_vp, pair * BP + n + 1)
                            nc.scalar.activation(Vs[:, n, :, :, 0:DK], ps[:, 5].rearrange("p (j h d) -> p j h d", j=2, h=H),
                                                 ACT.Copy).then_inc(s_vs, 1)
                        act.wait_ge(s_ready, pair * NS + n + 1)
                        nc.scalar.activation(PT[:, half, :, :, k * QI:(k + 1) * QI],
                                             ps[:, 2 * (n % 2):2 * (n % 2) + 2].rearrange("p j (h i) -> p j h i", i=QI),
                                             ACT.Exp, scale=QK_SCALE).then_inc(s_exp, 1)

            @block.vector
            def _(dve):
                def keep_unit(half, u, made):
                    dve.wait_ge(s_qp, made)
                    nc.vector.tensor_copy(QB[:, half, :, 2 * u:2 * u + 2], ps[0:KP, 6].rearrange("p (h b i) -> p b h i", h=2, b=BP)
                                          ).then_inc(s_qb, 1)

                def keep_out(pair, half, b):
                    dve.wait_ge(s_pv, pair * 4 + half * 2 + b + 1)
                    nc.vector.tensor_copy(g.OT[:, bass.ds(pair * 4 + b * 2 + half, 1)], ps[:, 5].rearrange("p (o g i) -> p o g i", o=1, g=NG)
                                          ).then_inc(s_ot, 1)

                nc.vector.memset(QB[0:1, 0, 0, 0, 0:1], 0.0).then_inc(s_qb, 1)
                nc.vector.memset(g.OT[0:1, 0, 0, 0:1], 0.0).then_inc(s_ot, 1)
                dve.wait_ge(s_qb, 1)
                dve.wait_ge(s_ot, 1)
                for u in range(UN):
                    keep_unit(0, u, u + 1)
                with dve.Fori(0, NPAIR) as pair:
                    for n in range(NS):
                        half, k = divmod(n, STEPS)
                        if k < UN - 1:
                            for u in ((0, 1) if k == 0 else (k + 1,)):
                                keep_unit(1 - half, u, pair * (2 * UN) + UN + half * UN + u + 1)
                        dve.wait_ge(s_evac, pair * NS + n + 1)
                        nc.vector.tensor_tensor(SM[:, n % 2], ps[:, 2 * (n % 2) + 1], SA[:, n % 2], ALU.max).then_inc(s_mx, 1)
                        dve.wait_ge(s_tr, pair * NS + n + 1)
                        nc.vector.reduce_max(m[:, n % 2], XT.rearrange("p (q j) -> p q j", q=4), AX.X).then_inc(s_m, 1)
                        if n in (STEPS + 2, STEPS + 5):
                            keep_out(pair, 0, int(n == STEPS + 5))
                    for b in range(BP):
                        keep_out(pair, 1, b)


GT = 4
GN = NT // GT


def pe_turn_heads(nc, pe, g, s, t):
    pe.wait_ge(s.ots, t + 1)
    for k in range(GT):
        for grp in range(NG):
            last = nc.tensor.transpose(g.ps[:, k, grp * P:(grp + 1) * P], s.OTs[:, k, grp], g.identF[:])
    last.then_inc(s.rows, 1)
    pe.wait_ge(s.at, t + 1)
    for k in range(GT):
        for c in range(DC):
            last = nc.tensor.transpose(g.ps[:, 4 + c, k * P:(k + 1) * P], s.AT[:, k, c * P:(c + 1) * P], g.identF[:])
    last.then_inc(s.att, 1)


def dve_divide_heads(nc, dve, g, s, t):
    nc.vector.tensor_copy(s.OTs[:], g.OT[:, bass.ds(t * GT, GT)]).then_inc(s.ots, 1)
    dve.wait_ge(s.rows, t + 1)
    rows = g.ps[:, 0:4].rearrange("p k (h d) -> p (k h) d", d=PADV)
    nc.vector.reciprocal(s.rec[:], rows[:, :, DK]).then_inc(s.recip, 1)
    dve.wait_ge(s.recip, t + 1)
    nc.vector.tensor_tensor(s.AT[:].rearrange("p k (h d) -> p (k h) d", d=DK), rows[:, :, 0:DK],
                            s.rec[:].unsqueeze(2).to_broadcast([P, GT * H, DK]), ALU.mult).then_inc(s.at, 1)


def head_buffers(g, c, nc, tag):
    def sb(n, sh):
        return c.enter_context(nc.sbuf_tensor(tag + n, sh, F32))
    s = Shared()
    s.OTs, s.AT, s.ATT, s.rec = sb("OTs", [P, GT, NG, P]), sb("AT", [P, GT, D]), sb("ATT", [P, DC, GT * P]), sb("rec", [P, GT * H])
    s.ots, s.rows, s.recip, s.at, s.att, s.attc = (g.sem(tag + n) for n in ("ots", "rows", "recip", "at", "att", "attc"))
    return s


def project(nc, g, a):
    sem, ps = g.sem, g.ps
    (s_h, s_hs, s_var, s_rs, s_x, s_ms, s_r2, s_hn, s_ht, s_htc, s_q, s_hi, s_r1, s_mi, s_lo, s_moved, s_v, s_vk, s_dv, s_half, s_apart) = (
        sem("pj_" + n) for n in ("h hs var rs x ms r2 hn ht htc q hi r1 mid lo moved v vkept dve half apart").split())
    with ExitStack() as c:
        def sb(n, sh, dt):
            return c.enter_context(nc.sbuf_tensor("pj_" + n, sh, dt))
        s = head_buffers(g, c, nc, "pj_")
        st, mv, half = sb("st", [P, GT, 6], F32), sb("mv", [P, GT, 8], F32), sb("half", [P, GT], F32)
        hn, hT = sb("hn", [P, GT, D], F32), sb("hT", [P, DC, GT * P], F32)
        w1 = sb("w1", [P, D], F32)
        W = sb("W", [P, 3, DC, D], F32)
        r1 = sb("r1", [P, 2, DC, GT * P], F32)
        parts = sb("parts", [P, 2, 3, DC, GT * P], BF16)
        qd = g.qd.rearrange("k a (m p) t -> k p a m t", p=P)
        with nc.Block() as block:
            @block.sync
            def _(sp):
                for n, w in enumerate((a["wq"], a["wk"], a["wv"])):
                    sp.dma_start(W[:, n], w).then_inc(s_moved, 16)
                sp.dma_start(w1[:], a["w1"]).then_inc(s_moved, 16)
                with sp.Fori(0, GN) as t:
                    for k in range(2):
                        sp.wait_ge(s_lo, t * 2 + k + 1)
                        for part in range(3):
                            sp.dma_start(qd[k, :, part, :, bass.ds(t * (GT * P), GT * P)], parts[:, k, part]).then_inc(s_moved, 16)
                sp.wait_ge(s_moved, 64 + GN * 96)

            @block.gpsimd
            def _(pool):
                nc.gpsimd.memset(half[:], -0.5).then_inc(s_half, 1)
                pool.wait_ge(s_half, 1)
                with pool.Fori(0, GN) as t:
                    pool.wait_ge(s_var, t + 1)
                    nc.gpsimd.tensor_tensor(mv[:, :, 3], mv[:, :, 2], half[:], ALU.pow).then_inc(s_rs, 1)
                    pool.wait_ge(s_ms, t + 1)
                    nc.gpsimd.tensor_tensor(mv[:, :, 5], mv[:, :, 4], half[:], ALU.pow).then_inc(s_r2, 1)

            @block.tensor
            def _(pe):
                mm = nc.tensor.matmul
                pe.wait_ge(s_moved, 64)
                with pe.Fori(0, GN) as t:
                    pe_turn_heads(nc, pe, g, s, t)
                    pe.wait_ge(s.attc, t + 1)
                    for k in range(GT):
                        out = ps[:, k // 2, (k % 2) * D:(k % 2 + 1) * D]
                        for cc in range(DC):
                            mm(out, s.ATT[:, cc, k * P:(k + 1) * P], g.WoT[:, cc], start=cc == 0, stop=False)
                        last = mm(out, g.OH3[:, bass.ds(t * (GT * P) + k * P, P)], g.R3[:], start=False, stop=True)
                    last.then_inc(s_h, 1)
                    pe.wait_ge(s_hn, GT * (t + 1))
                    for k in range(GT):
                        for cc in range(DC):
                            last = nc.tensor.transpose(ps[:, 2 + cc, k * P:(k + 1) * P], hn[:, k, cc * P:(cc + 1) * P], g.identF[:])
                    last.then_inc(s_ht, 1)
                    pe.wait_ge(s_htc, t + 1)
                    for n in range(2):
                        for m in range(DC):
                            for cc in range(DC):
                                last = mm(ps[:, 4 + 2 * n + m], W[:, n, cc, m * P:(m + 1) * P], hT[:, cc], start=cc == 0, stop=cc == DC - 1)
                        last.then_inc(s_q, 1)
                    for k in range(GT):
                        for cc in range(DC):
                            last = mm(ps[:, k // 2, (k % 2) * D:(k % 2 + 1) * D], hT[:, cc, k * P:(k + 1) * P], W[:, 2, cc], start=cc == 0, stop=cc == DC - 1)
                    last.then_inc(s_v, 1)
                    pe.wait_ge(s_vk, t + 1)
                    pe.wait_ge(s_lo, 2 * t + 2)

            @block.scalar
            def _(act):
                def copy(out, in_):
                    return nc.scalar.activation(out, in_, ACT.Copy)

                with act.Fori(0, GN) as t:
                    act.wait_ge(s.att, t + 1)
                    copy(s.ATT[:], ps[:, 4:6]).then_inc(s.attc, 1)
                    act.wait_ge(s_h, t + 1)
                    copy(g.HS[:, bass.ds(t * GT, GT)], ps[:, 0:2].rearrange("p a (k d) -> p (a k) d", d=D)).then_inc(s_hs, 1)
                    act.wait_ge(s_ht, t + 1)
                    copy(hT[:], ps[:, 2:4]).then_inc(s_htc, 1)
                    act.wait_ge(s_moved, t * 96 + 64)
                    for n in range(2):
                        act.wait_ge(s_q, 2 * t + n + 1)
                        copy(parts[:, n, 0], ps[:, 4 + 2 * n:6 + 2 * n]).then_inc(s_hi, 1)
                    act.wait_ge(s_v, t + 1)
                    copy(g.V2[:, bass.ds(t * GT, GT), :, 0:DK], ps[:, 0:2].rearrange("p a (k h d) -> p (a k) h d", h=H, d=DK)).then_inc(s_vk, 1)
                    for n in range(2):
                        act.wait_ge(s_r1, 2 * t + n + 1)
                        copy(parts[:, n, 1], r1[:, n]).then_inc(s_mi, 1)

            @block.vector
            def _(dve):
                V = nc.vector
                do = Chain(dve, s_dv)
                with dve.Fori(0, GN) as t:
                    do.enter(t, 2 + 2 * GT)
                    dve_divide_heads(nc, dve, g, s, t)
                    dve.wait_ge(s_hs, t + 1)
                    for k in range(GT):
                        do(V.bn_stats(st[:, k], g.HS[:, bass.ds(t * GT + k, 1)].rearrange("p o d -> p (o d)")), s_apart)
                        do(V.bn_aggr(mv[:, k, 0:2], st[:, k]))
                    V.tensor_scalar(mv[:, :, 2], mv[:, :, 1], LN_EPS, None, ALU.add).then_inc(s_var, 1)
                    dve.wait_ge(s_rs, t + 1)
                    for k in range(GT):
                        V.tensor_scalar(g.XS[:, bass.ds(t * GT + k, 1)], g.HS[:, bass.ds(t * GT + k, 1)], mv[:, k, 0:1], mv[:, k, 3:4],
                                        ALU.subtract, ALU.mult).then_inc(s_x, 1)
                    do(V.tensor_tensor(mv[:, :, 6], mv[:, :, 3], mv[:, :, 3], ALU.mult))
                    do(V.tensor_tensor(mv[:, :, 6], mv[:, :, 6], mv[:, :, 1], ALU.mult))
                    V.tensor_scalar(mv[:, :, 4], mv[:, :, 6], RMS_EPS, None, ALU.add).then_inc(s_ms, 1)
                    dve.wait_ge(s_x, GT * (t + 1))
                    dve.wait_ge(s_r2, t + 1)
                    for k in range(GT):
                        V.scalar_tensor_tensor(hn[:, k:k + 1], g.XS[:, bass.ds(t * GT + k, 1)], mv[:, k, 5:6], w1[:].unsqueeze(1),
                                               ALU.mult, ALU.mult).then_inc(s_hn, 1)
                    for n in range(2):
                        dve.wait_ge(s_hi, 2 * t + n + 1)
                        V.tensor_tensor(r1[:, n], ps[:, 4 + 2 * n:6 + 2 * n], parts[:, n, 0], ALU.subtract).then_inc(s_r1, 1)
                    for n in range(2):
                        dve.wait_ge(s_mi, 2 * t + n + 1)
                        V.tensor_tensor(parts[:, n, 2], r1[:, n], parts[:, n, 1], ALU.subtract).then_inc(s_lo, 1)
                    do.leave(GN)


def full_attention(nc, g):
    sem, ps = g.sem, g.ps
    (s_sc, s_max, s_lg, s_exp, s_pv, s_ot, s_vs, s_pad) = (sem("fa_" + n) for n in "scores max less exp pv out values pad".split())
    s_ld = [sem("fa_load" + n) for n in names(2)]
    HP = H // 2
    with ExitStack() as c:
        def sb(n, sh, dt):
            return c.enter_context(nc.sbuf_tensor("fa_" + n, sh, dt))
        QK = sb("QK", [KP, 2, 2, H, S], BF16)
        m = sb("m", [P, 2, H, 2], BF16)
        PT = sb("PT", [P, 2, 4, 2, S], F32)
        Vs = sb("Vs", [P, 2, 2, H, PADV], F32)
        src = g.qd.rearrange("k a (h d) t -> k a d h t", d=DK)
        sides = (LEFT, RIGHT)
        with nc.Block() as block:
            @block.sync
            def _(sp):
                def load(b, par):
                    for k in range(2):
                        for n in range(SLOTS):
                            sp.dma_start(QK[n * DK:(n + 1) * DK, par, k], src[k, sides[k][n], :, :, bass.ds(b * S, S)]).then_inc(s_ld[par], 16)

                load(0, 0)
                load(1, 1)
                with sp.Fori(0, B // 2 - 1) as t:
                    for par in range(2):
                        sp.wait_ge(s_lg, (2 * t + par + 1) * HP)
                        load(2 * t + 2 + par, par)

            @block.tensor
            def _(pe):
                mm = nc.tensor.matmul

                def scores(b, par, h):
                    if h >= 2:
                        pe.wait_ge(s_max, b * H + h - 1)
                    for half in range(2):
                        last = mm(ps[:, h % 2, half * S:(half + 1) * S], QK[:, par, 0, h, half * P:(half + 1) * P], QK[:, par, 1, h],
                                  start=True, stop=True)
                    last.then_inc(s_sc, 1)

                def less_max(b, par, hp):
                    if hp >= 2:
                        pe.wait_ge(s_exp, b * HP + hp - 1)
                    pe.wait_ge(s_max, b * H + 2 * hp + 2)
                    for k in range(2):
                        h = 2 * hp + k
                        bank = ps[:, 2 + 2 * (hp % 2) + k]
                        for jh in range(2):
                            mm(bank[:, jh * S:(jh + 1) * S], QK[:, par, 1, h, jh * P:(jh + 1) * P], QK[:, par, 0, h],
                               start=jh == 0, stop=False, skip_group_check=True)
                        for jh in range(2):
                            for half in range(2):
                                at = jh * S + half * P
                                last = mm(bank[:, at:at + P], m[:, par, h, half:half + 1].to_broadcast([P, P]), g.negIB[:],
                                          start=False, stop=True, skip_group_check=True)
                    last.then_inc(s_lg, 1)

                def weigh(b, par, grp):
                    pe.wait_ge(s_exp, b * HP + 2 * grp + 2)
                    if grp % 2 == 0:
                        pe.wait_ge(s_ot, b * 2 + grp // 2 + 1)
                    for jh in range(2):
                        for k in range(4):
                            last = mm(ps[32 * k:32 * k + PADV, 6 + grp // 2, (grp % 2) * S:(grp % 2 + 1) * S],
                                      Vs[:, par, jh, 4 * grp + k], PT[:, grp % 2, k, jh], start=jh == 0, stop=jh == 1, skip_group_check=True)
                    last.then_inc(s_pv, 1)

                pe.wait_ge(s_pad, 2)
                with pe.Fori(0, B // 2) as t:
                    for par in range(2):
                        b = 2 * t + par
                        pe.wait_ge(s_ld[par], t * (2 * SLOTS * 16) + 2 * SLOTS * 16)
                        pe.wait_ge(s_vs, b + 1)
                        for h in range(4):
                            scores(b, par, h)
                        for hp in range(HP):
                            less_max(b, par, hp)
                            for h in (2 * hp + 4, 2 * hp + 5):
                                if h < H:
                                    scores(b, par, h)
                            if hp % 2 == 0 and hp:
                                weigh(b, par, hp // 2 - 1)
                        weigh(b, par, NG - 1)

            @block.gpsimd
            def _(pool):
                nc.gpsimd.memset(Vs[:, :, :, :, DK:PADV], 0.0).then_inc(s_pad, 1)
                pool.wait_ge(s_pad, 1)
                nc.gpsimd.memset(Vs[:, :, :, :, DK:DK + 1], 1.0).then_inc(s_pad, 1)

            @block.scalar
            def _(act):
                with act.Fori(0, B // 2) as t:
                    for par in range(2):
                        b = 2 * t + par
                        nc.scalar.activation(Vs[:, par, :, :, 0:DK], g.V2[:, bass.ds(2 * b, 2)], ACT.Copy).then_inc(s_vs, 1)
                        for hp in range(HP):
                            act.wait_ge(s_lg, b * HP + hp + 1)
                            if hp >= 4:
                                act.wait_ge(s_pv, b * NG + hp // 2 - 1)
                            grp, k = hp // 2, 2 * (hp % 2)
                            nc.scalar.activation(PT[:, grp % 2, k:k + 2], ps[:, 2 + 2 * (hp % 2):4 + 2 * (hp % 2)].rearrange("p k (j i) -> p k j i", j=2),
                                                 ACT.Exp, scale=QK_SCALE).then_inc(s_exp, 1)

            @block.vector
            def _(dve):
                def keep_out(b, x):
                    dve.wait_ge(s_pv, b * NG + 2 * x + 2)
                    nc.vector.tensor_copy(g.OT[:, bass.ds(2 * b, 2), 2 * x:2 * x + 2], ps[:, 6 + x].rearrange("p (g f i) -> p f g i", g=2, f=2)
                                          ).then_inc(s_ot, 1)

                for n in range(2):
                    nc.vector.memset(m[0:1, n, 0, 0:1], 0.0).then_inc(s_ot, 1)
                dve.wait_ge(s_ot, 2)
                with dve.Fori(0, B // 2) as t:
                    for par in range(2):
                        b = 2 * t + par
                        for h in range(H):
                            dve.wait_ge(s_sc, b * H + h + 1)
                            nc.vector.reduce_max(m[:, par, h], ps[:, h % 2].rearrange("p (f j) -> p f j", f=2), AX.X).then_inc(s_max, 1)
                            if h == 13:
                                keep_out(b, 0)
                        keep_out(b, 1)


def route(nc, g, a):
    sem, ps = g.sem, g.ps
    (s_in, s_h, s_x2, s_var, s_r2, s_hn, s_ht, s_htc, s_h2, s_lg, s_d, s_e, s_d2, s_e2, s_dv, s_half, s_done, s_kept, s_apart) = (
        sem("rt_" + n) for n in "in h x2 var r2 hn ht htc h2 logits diff exp diff2 exp2 dve half done kept apart".split())
    with ExitStack() as c:
        def sb(n, sh, dt):
            return c.enter_context(nc.sbuf_tensor("rt_" + n, sh, dt))
        s = head_buffers(g, c, nc, "rt_")
        st, mv, half = sb("st", [P, GT, 6], F32), sb("mv", [P, GT, 6], F32), sb("half", [P, GT], F32)
        X2, hn, hT = sb("X2", [P, GT, D], F32), sb("hn", [P, GT, D], F32), sb("hT", [P, DC, GT * P], F32)
        w2, W, rw, iota = sb("w2", [P, D], F32), sb("W", [P, DC, D], F32), sb("rw", [P, DC, E], F32), sb("iota", [P, E], F32)
        lg, v8, ix, es = sb("lg", [P, GT, E], F32), sb("v8", [P, GT, E], F32), sb("ix", [P, GT, E], U32), sb("es", [P, GT, E], F32)
        fx, p, ed = sb("fx", [P, GT, 2], F32), sb("p", [P, GT, 4], F32), sb("ed", [P, GT], F32)
        cw = sb("cw", [P, GT, 2], F32)
        with nc.Block() as block:
            @block.sync
            def _(sp):
                for o, i in ((W, a["wo"]), (w2, a["w2"]), (rw, a["rw"]), (iota, a["iota"])):
                    sp.dma_start(o[:], i).then_inc(s_in, 16)

            @block.gpsimd
            def _(pool):
                nc.gpsimd.memset(half[:], -0.5).then_inc(s_half, 1)
                pool.wait_ge(s_half, 1)
                with pool.Fori(0, GN) as t:
                    pool.wait_ge(s_var, t + 1)
                    nc.gpsimd.tensor_tensor(mv[:, :, 4], mv[:, :, 3], half[:], ALU.pow).then_inc(s_r2, 1)
                    pool.wait_ge(s_hn, GT * (t + 1))
                    nc.gpsimd.tensor_copy(g.XS[:, bass.ds(t * GT, GT)], hn[:]).then_inc(s_kept, 1)

            @block.tensor
            def _(pe):
                mm = nc.tensor.matmul
                pe.wait_ge(s_in, 64)
                with pe.Fori(0, GN) as t:
                    pe_turn_heads(nc, pe, g, s, t)
                    pe.wait_ge(s.attc, t + 1)
                    for k in range(GT):
                        for cc in range(DC):
                            last = mm(ps[:, k // 2, (k % 2) * D:(k % 2 + 1) * D], s.ATT[:, cc, k * P:(k + 1) * P], W[:, cc],
                                      start=cc == 0, stop=cc == DC - 1)
                    last.then_inc(s_h, 1)
                    pe.wait_ge(s_hn, GT * (t + 1))
                    for k in range(GT):
                        for cc in range(DC):
                            last = nc.tensor.transpose(ps[:, 2 + cc, k * P:(k + 1) * P], hn[:, k, cc * P:(cc + 1) * P], g.identF[:])
                    last.then_inc(s_ht, 1)
                    pe.wait_ge(s_htc, t + 1)
                    for k in range(GT):
                        for cc in range(DC):
                            last = mm(ps[:, 6, k * E:(k + 1) * E], hT[:, cc, k * P:(k + 1) * P], rw[:, cc], start=cc == 0, stop=cc == DC - 1)
                    last.then_inc(s_lg, 1)
                    pe.wait_ge(s_done, t + 1)

            @block.scalar
            def _(act):
                act.wait_ge(s_in, 64)
                with act.Fori(0, GN) as t:
                    act.wait_ge(s.att, t + 1)
                    nc.scalar.activation(s.ATT[:], ps[:, 4:6], ACT.Copy).then_inc(s.attc, 1)
                    act.wait_ge(s_ht, t + 1)
                    nc.scalar.activation(hT[:], ps[:, 2:4], ACT.Copy).then_inc(s_htc, 1)
                    act.wait_ge(s_htc, t + 1)
                    nc.scalar.activation(g.H2T[:, :, bass.ds(t * (GT * P), GT * P)], hT[:], ACT.Copy).then_inc(s_h2, 1)
                    act.wait_ge(s_d, t + 1)
                    nc.scalar.activation(es[:], es[:], ACT.Exp).then_inc(s_e, 1)
                    act.wait_ge(s_d2, t + 1)
                    nc.scalar.activation(ed[:], ed[:], ACT.Exp).then_inc(s_e2, 1)

            @block.vector
            def _(dve):
                V = nc.vector
                do = Chain(dve, s_dv)
                dve.wait_ge(s_in, 64)
                with dve.Fori(0, GN) as t:
                    do.enter(t, 11 + 6 * GT)
                    dve_divide_heads(nc, dve, g, s, t)
                    dve.wait_ge(s_h, t + 1)
                    V.tensor_tensor(X2[:], ps[:, 0:2].rearrange("p a (k d) -> p (a k) d", d=D), g.XS[:, bass.ds(t * GT, GT)], ALU.add).then_inc(s_x2, 1)
                    dve.wait_ge(s_x2, t + 1)
                    for k in range(GT):
                        do(V.bn_stats(st[:, k], X2[:, k]), s_apart)
                        do(V.bn_aggr(mv[:, k, 0:2], st[:, k]))
                    do(V.tensor_tensor(mv[:, :, 2], mv[:, :, 0], mv[:, :, 0], ALU.mult))
                    do(V.tensor_tensor(mv[:, :, 2], mv[:, :, 2], mv[:, :, 1], ALU.add))
                    V.tensor_scalar(mv[:, :, 3], mv[:, :, 2], RMS_EPS, None, ALU.add).then_inc(s_var, 1)
                    do(V.tensor_tensor(g.HS[:, bass.ds(t * GT, GT)], g.HS[:, bass.ds(t * GT, GT)], X2[:], ALU.add))
                    dve.wait_ge(s_r2, t + 1)
                    for k in range(GT):
                        V.scalar_tensor_tensor(hn[:, k], X2[:, k], mv[:, k, 4:5], w2[:], ALU.mult, ALU.mult).then_inc(s_hn, 1)
                    dve.wait_ge(s_lg, t + 1)
                    do(V.tensor_copy(lg[:], ps[:, 6, 0:GT * E].rearrange("p (k e) -> p k e", e=E)), s_apart)
                    for k in range(GT):
                        do(V.max(v8[:, k], lg[:, k]), s_apart)
                        do(V.max_index(ix[:, k], v8[:, k], lg[:, k]), s_apart)
                    V.tensor_tensor(es[:], v8[:], v8[:, :, 0:1].to_broadcast([P, GT, E]), ALU.subtract).then_inc(s_d, 1)
                    do(V.tensor_copy(fx[:], ix[:, :, 0:2]))
                    dve.wait_ge(s_e, t + 1)
                    do(V.reduce_sum(p[:, :, 0], es[:], AX.X))
                    do(V.reciprocal(p[:, :, 1], p[:, :, 0]))
                    do(V.tensor_tensor(p[:, :, 2], es[:, :, 1], p[:, :, 1], ALU.mult))
                    V.tensor_tensor(ed[:], p[:, :, 2], p[:, :, 1], ALU.subtract).then_inc(s_d2, 1)
                    dve.wait_ge(s_e2, t + 1)
                    do(V.tensor_scalar(p[:, :, 3], ed[:], 1.0, None, ALU.add))
                    do(V.reciprocal(cw[:, :, 0], p[:, :, 3]))
                    do(V.tensor_tensor(cw[:, :, 1], cw[:, :, 0], ed[:], ALU.mult))
                    for k in range(GT):
                        for n in range(2):
                            do(V.tensor_scalar(g.pick[:, n, bass.ds(t * GT + k, 1)], iota[:].unsqueeze(1), fx[:, k, n:n + 1], None, ALU.is_equal))
                    V.tensor_copy(g.share[:, bass.ds(t * GT, GT)], cw[:]).then_inc(s_done, 1)
                    dve.wait_ge(s_done, t + 1)
                    do.leave(GN)


def experts(nc, g, a, outs):
    sem, ps = g.sem, g.ps
    (s_hid, s_sil, s_act_, s_y, s_acc, s_out, s_c, s_m, s_cnt, s_dv, s_pos, s_sc, s_sw, s_half) = (
        sem("ex_" + n) for n in "hidden silu act y acc out consts member count dve places scattered shared_w half".split())
    (s_xT, s_xTc, s_g, s_u, s_si, s_h, s_hT, s_hTc, s_yd, s_yk, s_ys, s_fin, s_ot2) = (
        sem("slot_" + n) for n in "xT xTc gate up silu hid hidT hidTc down ykept pad sum pad2".split())
    s_w = [sem("ex_w" + n) for n in names(E)]
    s_x = [sem("slot_x" + n) for n in names(2)]
    s_yst = [sem("slot_stored" + n) for n in names(2)]
    s_ga = [sem("pick" + n) for n in names(2)]
    s_o = [sem("out" + n) for n in names(2)]
    NS = SLOTS_X
    with ExitStack() as c:
        def sb(n, sh, dt):
            return c.enter_context(nc.sbuf_tensor("ex_" + n, sh, dt))
        WG, WU, WD = sb("WG", [P, E, DC, F], F32), sb("WU", [P, E, DC, F], F32), sb("WD", [P, E, FC, D], F32)
        SG, SU, SD = sb("SG", [P, DC, F], F32), sb("SU", [P, DC, F], F32), sb("SD", [P, FC, D], F32)
        sil, hidS = sb("sil", [P, 2, 512], F32), sb("hidS", [P, FC, 512], F32)
        before, ones, place, tile_no = sb("before", [P, P], F32), sb("ones", [P, P], BF16), sb("place", [P, E, NT], F32), sb("tile_no", [1, NS, E], F32)
        befB, mem = sb("befB", [P, P], BF16), sb("mem", [P, E, NT], BF16)
        tot, run, cnt, base = sb("tot", [P, E, NT], F32), sb("run", [P, E, NT], F32), sb("cnt", [P, E], F32), sb("base", [P, E], F32)
        zer, tl, incl, cmp_ = sb("zer", [P, E * NT], F32), sb("tl", [P, E], F32), sb("incl", [P, E], F32), sb("cmp", [P, E, NT], F32)
        pos, pp, pf, pidx = sb("pos", [P, E, NT], F32), sb("pp", [P, NT, E], F32), sb("pf", [P, 2, NT], F32), sb("pidx", [P, 2, NT], U32)
        ce, ef, eid = sb("ce", [1, NS, E], F32), sb("ef", [1, NS], F32), sb("eid", [1, NS], I32)
        XR, xT = sb("XR", [P, 2, D], F32), sb("xT", [P, 2, DC, P], F32)
        sl, hd, hT, Y = sb("sl", [P, 2, F], F32), sb("hd", [P, 2, F], F32), sb("hT", [P, 2, FC, P], F32), sb("Y", [P, 2, D], F32)
        G, O = sb("G", [P, 2, 2, D], F32), sb("O", [P, 2, D], F32)
        ov = outs.rearrange("(t p) d -> t p d", p=P)
        with nc.Block() as block:
            @block.sync
            def _(sp):
                for o, i in ((before, "before"), (place, "place"), (tile_no, "tile_no")):
                    sp.dma_start(o[:], a[i]).then_inc(s_c, 16)
                for o, i in ((SG, "sh_gate"), (SU, "sh_up"), (SD, "sh_down")):
                    sp.dma_start(o[:], a[i].rearrange("(c p) f -> p c f", p=P)).then_inc(s_sw, 16)
                for e in range(E):
                    for o, i in ((WG, "e_gate"), (WU, "e_up"), (WD, "e_down")):
                        sp.dma_start(o[:, e], a[i][e].rearrange("(c p) f -> p c f", p=P)).then_inc(s_w[e], 16)
                sp.wait_ge(s_sc, NT * 2 * 16)
                for n in range(2):
                    sp.dma_start(XR[:, n], g.xs[n * P:(n + 1) * P]).then_inc(s_x[n], 16)

                def load_slot(s, n):
                    sp.wait_ge(s_xT, s - 1)
                    sp.dma_start(XR[:, n], g.xs[bass.ds(s * P, P)]).then_inc(s_x[n], 16)

                def store_slot(s, n):
                    sp.wait_ge(s_yk, s + 2)
                    sp.dma_start(g.ys[bass.ds(s * P, P)], Y[:, n]).then_inc(s_yst[n], 16)

                load_slot(2, 0)
                with sp.Fori(0, NS // 2 - 1) as t:
                    load_slot(2 * t + 3, 1)
                    store_slot(2 * t, 0)
                    load_slot(2 * t + 4, 0)
                    store_slot(2 * t + 1, 1)
                for k in range(NS - 3, NS):
                    store_slot(k, k % 2)
                for n in range(2):
                    sp.wait_ge(s_o[n], NT // 2 * 16)

            @block.gpsimd
            def _(pool):
                pool.wait_ge(s_pos, 1)
                for t in range(NT):
                    for n in range(2):
                        nc.gpsimd.indirect_dma_start(out=g.xs, out_offset=bass.IndirectOffsetOnAxis(ap=pidx[:, n, t:t + 1], axis=0),
                                                     in_=g.XS[:, t], in_offset=None).then_inc(s_sc, 16)
                for n in range(2):
                    pool.wait_ge(s_yst[n], (NS - n + 1) // 2 * 16 + 16)
                for t in range(NT):
                    if t >= 2:
                        pool.wait_ge(s_fin, 2 * (t - 1))
                    for n in range(2):
                        nc.gpsimd.indirect_dma_start(out=G[:, t % 2, n], out_offset=None, in_=g.ys,
                                                     in_offset=bass.IndirectOffsetOnAxis(ap=pidx[:, n, t:t + 1], axis=0)).then_inc(s_ga[t % 2], 16)

            @block.tensor
            def _(pe):
                mm = nc.tensor.matmul

                def up(tg):
                    for f in range(FC):
                        n = tg * FC + f
                        if n >= 2:
                            pe.wait_ge(s_act_, n - 1)
                        for w, bk in ((SG, 2 * (n % 2)), (SU, 2 * (n % 2) + 1)):
                            for cc in range(DC):
                                last = mm(ps[:, bk], w[:, cc, f * P:(f + 1) * P], g.H2T[:, cc, tg * 512:(tg + 1) * 512], start=cc == 0, stop=cc == 1)
                        last.then_inc(s_hid, 1)

                def down(tg):
                    pe.wait_ge(s_act_, FC * (tg + 1))
                    if tg:
                        pe.wait_ge(s_acc, tg)
                    for k in range(4):
                        for f in range(FC):
                            last = mm(ps[:, 4 + k // 2, (k % 2) * D:(k % 2 + 1) * D], hidS[:, f, k * P:(k + 1) * P], SD[:, f], start=f == 0, stop=f == 3)
                    last.then_inc(s_y, 1)

                pe.wait_ge(s_m, 2)
                memf = mem[:].rearrange("p e t -> p (e t)")
                mm(ps[:, 7, 0:P], befB[:], memf, start=True, stop=True)
                mm(ps[:, 7, P:2 * P], ones[:], memf, start=True, stop=True).then_inc(s_cnt, 1)
                pe.wait_ge(s_sw, 48)
                for tg in range(4):
                    up(tg)
                    down(tg)
                pe.wait_ge(s_acc, 4)
                for e in range(E):
                    pe.wait_ge(s_w[e], 48)
                pe.wait_ge(s_pos, 2)

                flatG, flatU, flatD = (w[:].rearrange("p e c f -> p (e c f)") for w in (WG, WU, WD))

                def turn_x(s, x_done):
                    pe.wait_ge(s_x[x_done[0]], x_done[1])
                    if x_done[2]:
                        pe.wait_ge(s_xTc, s)
                    for cc in range(DC):
                        last = nc.tensor.transpose(ps[:, 6, cc * P:(cc + 1) * P], XR[:, x_done[0], cc * P:(cc + 1) * P], g.identF[:])
                    last.then_inc(s_xT, 1)

                def gate_up(s, n, e):
                    pe.wait_ge(s_xTc, s + 1)
                    for w, bk, s_done in ((flatG, 0, s_g), (flatU, 2, s_u)):
                        for cc in range(DC):
                            last = mm(ps[:, bk + n], xT[:, n, cc], w[:, bass.ds(e + cc * F, F)], start=cc == 0, stop=cc == 1)
                        last.then_inc(s_done, 1)

                def turn_hidden(s, n):
                    pe.wait_ge(s_h, s + 1)
                    for f in range(FC):
                        last = nc.tensor.transpose(ps[:, 4, f * P:(f + 1) * P], hd[:, n, f * P:(f + 1) * P], g.identF[:])
                    last.then_inc(s_hT, 1)

                def down_slot(s, n, e):
                    pe.wait_ge(s_hTc, s + 1)
                    pe.wait_ge(s_yk, s + 1)
                    for f in range(FC):
                        last = mm(ps[:, 5, 0:D], hT[:, n, f], flatD[:, bass.ds(e + f * D, D)], start=f == 0, stop=f == FC - 1)
                    last.then_inc(s_yd, 1)

                def expert_of(s):
                    return pe.value_load(eid[0:1, bass.ds(s, 1)], min_val=0, max_val=(E - 1) * DC * F)

                e = expert_of(0)
                turn_x(0, (0, 16, False))
                gate_up(0, 0, e)
                with pe.Fori(0, NS // 2) as t:
                    es = [expert_of(2 * t + i) for i in range(3)]
                    turn_x(2 * t + 1, (1, t * 16 + 16, True))
                    turn_hidden(2 * t, 0)
                    gate_up(2 * t + 1, 1, es[1])
                    down_slot(2 * t, 0, es[0])
                    turn_x(2 * t + 2, (0, t * 16 + 32, True))
                    turn_hidden(2 * t + 1, 1)
                    gate_up(2 * t + 2, 0, es[2])
                    down_slot(2 * t + 1, 1, es[1])
                turn_hidden(NS - 1, 0)
                down_slot(NS - 1, 0, expert_of(NS - 1))

            @block.scalar
            def _(act):
                A = nc.scalar.activation
                for n in range(4 * FC):
                    act.wait_ge(s_hid, n + 1)
                    if n >= 2:
                        act.wait_ge(s_act_, n - 1)
                    A(sil[:, n % 2], ps[:, 2 * (n % 2)], ACT.Silu).then_inc(s_sil, 1)

                def rows_gate(s, n):
                    act.wait_ge(s_xT, s + 1)
                    A(xT[:, n], ps[:, 6, 0:D].rearrange("p (c i) -> p c i", c=DC), ACT.Copy).then_inc(s_xTc, 1)
                    act.wait_ge(s_g, s + 1)
                    A(sl[:, n], ps[:, n], ACT.Silu).then_inc(s_si, 1)

                rows_gate(0, 0)
                with act.Fori(0, NS // 2) as t:
                    rows_gate(2 * t + 1, 1)
                    rows_gate(2 * t + 2, 0)
                for t in range(NT):
                    act.wait_ge(s_fin, 2 * t + 2)
                    act.dma_start(ov[t], O[:, t % 2]).then_inc(s_o[t % 2], 16)

            @block.vector
            def _(dve):
                V = nc.vector
                do = Chain(dve, s_dv)

                def acc(tg):
                    dve.wait_ge(s_y, tg + 1)
                    V.tensor_tensor(g.HS[:, 4 * tg:4 * tg + 4], ps[:, 4:6].rearrange("p a (k d) -> p (a k) d", d=D),
                                    g.HS[:, 4 * tg:4 * tg + 4], ALU.add).then_inc(s_acc, 1)

                dve.wait_ge(s_c, 48)
                V.memset(ones[:], 1.0).then_inc(s_m, 1)
                do(V.memset(zer[:], 0.0))
                do(V.tensor_copy(befB[:], before[:]))
                V.tensor_tensor(mem[:].rearrange("p e t -> p t e"), g.pick[:, 0], g.pick[:, 1], ALU.add).then_inc(s_m, 1)
                dve.wait_ge(s_cnt, 1)
                flat = lambda x: x[:].rearrange("p e t -> p (e t)")
                per_e = lambda x: x[:].unsqueeze(2).to_broadcast([P, E, NT])
                do(V.tensor_copy(flat(tot), ps[:, 7, P:2 * P]))
                do(V.tensor_tensor_scan(flat(run), flat(tot), zer[:], 0.0, ALU.add, ALU.add))
                do(V.memset(base[:, 0:1], 0.0))
                do(V.tensor_copy(base[:, 1:E], run[:, 0:E - 1, NT - 1]))
                do(V.tensor_tensor(cnt[:], run[:, :, NT - 1], base[:], ALU.subtract))
                do(V.tensor_tensor(cmp_[:], per_e(cnt), place[:], ALU.is_gt))
                do(V.reduce_sum(tl[:], cmp_[:], AX.X))
                do(V.tensor_tensor_scan(incl[:], tl[:], zer[:, 0:E], 0.0, ALU.add, ALU.add))
                do(V.tensor_tensor(cnt[:], incl[:], tl[:], ALU.subtract))
                do(V.scalar_tensor_tensor(base[:], cnt[:], float(P), base[:], ALU.mult, ALU.subtract))
                do(V.tensor_tensor(pos[:], run[:], tot[:], ALU.subtract))
                do(V.tensor_tensor(flat(pos), flat(pos), ps[:, 7, 0:P], ALU.add))
                do(V.tensor_tensor(pos[:], pos[:], per_e(base), ALU.add))
                for n in range(2):
                    do(V.tensor_tensor(pp[:], pos[:].rearrange("p e t -> p t e"), g.pick[:, n], ALU.mult))
                    do(V.reduce_sum(pf[:, n], pp[:], AX.X))
                V.tensor_copy(pidx[:], pf[:]).then_inc(s_pos, 1)
                do(V.tensor_tensor(ce[:], tile_no[:], incl[0:1].unsqueeze(1).to_broadcast([1, NS, E]), ALU.is_ge))
                do(V.reduce_sum(ef[:], ce[:], AX.X))
                do(V.tensor_scalar(ef[:], ef[:], float(E - 1), None, ALU.min))
                do(V.tensor_scalar(ef[:], ef[:], float(DC * F), None, ALU.mult))
                V.tensor_copy(eid[:], ef[:]).then_inc(s_pos, 1)
                for n in range(2):
                    V.memset(Y[0:1, n, 0:1], 0.0).then_inc(s_yst[n], 16)
                V.memset(sl[0:1, 0, 0:1], 0.0).then_inc(s_yk, 1)
                for tg in range(4):
                    for f in range(FC):
                        n = tg * FC + f
                        dve.wait_ge(s_sil, n + 1)
                        if tg:
                            dve.wait_ge(s_y, tg)
                        V.tensor_tensor(hidS[:, f], ps[:, 2 * (n % 2) + 1], sil[:, n % 2], ALU.mult).then_inc(s_act_, 1)
                    acc(tg)

                def hidden(s, n):
                    dve.wait_ge(s_u, s + 1)
                    dve.wait_ge(s_si, s + 1)
                    V.tensor_tensor(hd[:, n], ps[:, 2 + n], sl[:, n], ALU.mult).then_inc(s_h, 1)

                def keep_turned(s, n):
                    dve.wait_ge(s_hT, s + 1)
                    V.tensor_copy(hT[:, n].rearrange("p f i -> p (f i)"), ps[:, 4]).then_inc(s_hTc, 1)

                def keep_y(s, n, stored):
                    dve.wait_ge(s_yd, s + 1)
                    dve.wait_ge(s_yst[n], stored)
                    V.tensor_copy(Y[:, n], ps[:, 5, 0:D]).then_inc(s_yk, 1)

                hidden(0, 0)
                with dve.Fori(0, NS // 2) as t:
                    keep_turned(2 * t, 0)
                    hidden(2 * t + 1, 1)
                    keep_y(2 * t, 0, t * 16 + 16)
                    keep_turned(2 * t + 1, 1)
                    hidden(2 * t + 2, 0)
                    keep_y(2 * t + 1, 1, t * 16 + 16)
                keep_turned(NS - 1, 0)
                keep_y(NS - 1, 0, NS // 2 * 16 + 16)
                for t in range(NT):
                    dve.wait_ge(s_ga[t % 2], (t // 2 + 1) * 32)
                    if t >= 2:
                        dve.wait_ge(s_o[t % 2], t // 2 * 16)
                    V.scalar_tensor_tensor(O[:, t % 2], G[:, t % 2, 0], g.share[:, t, 0:1], g.HS[:, t], ALU.mult, ALU.add).then_inc(s_fin, 1)
                    dve.wait_ge(s_fin, 2 * t + 1)
                    V.scalar_tensor_tensor(O[:, t % 2], G[:, t % 2, 1], g.share[:, t, 1:2], O[:, t % 2], ALU.mult, ALU.add).then_inc(s_fin, 1)


def kernel(**inputs):
    import numpy as np
    import concourse.bacc as bacc
    from concourse.bass_utils import run_bass_kernel_spmd

    def given(name):
        return np.asarray(inputs[name])

    def rows(w):
        return np.ascontiguousarray(w.reshape(DC, P, -1).transpose(1, 0, 2))

    sel = np.zeros((B, B, L3), np.float32)
    sel[np.arange(B), np.arange(B)] = 1
    arrays = dict(
        before=np.triu(np.ones((P, P), np.float32), 1),
        place=np.ascontiguousarray(np.broadcast_to(P * np.arange(NT, dtype=np.float32), (P, E, NT))),
        tile_no=np.repeat(np.arange(SLOTS_X, dtype=np.float32), E).reshape(1, SLOTS_X, E),
        x=given("x"), sel=sel, lvl=(np.arange(L3) % L).astype(np.float32)[:, None].copy(),
        iota=np.ascontiguousarray(np.broadcast_to(np.arange(E, dtype=np.float32), (P, E))),
        er=np.ascontiguousarray(given("L0_attn_Er")[::-1].reshape(4, P, DK).transpose(1, 0, 2)), emb=given("L0_tok_level_emb"),
        ident=np.eye(P, dtype=np.float32), bo=np.ascontiguousarray(np.broadcast_to(given("L0_attn_bo"), (L, D))),
        bias=np.ascontiguousarray(np.broadcast_to(np.stack([given("L0_attn_b" + k) for k in "qkv"]), (L, 3, D))),
        w1=np.ascontiguousarray(np.broadcast_to(given("L0_ffn_norm1_w"), (P, D))),
        w2=np.ascontiguousarray(np.broadcast_to(given("L0_ffn_norm2_w"), (P, D))),
        **{k + "T": rows(given("L0_attn_" + k).T) for k in ("Wq", "Wk", "Wv", "Wo")},
        **{k: rows(given("L0_ffn_" + k)) for k in ("wq", "wk", "wv", "wo")},
        rw=rows(given("L0_ffn_router_w")),
        **{k: given("L0_ffn_" + k) for k in ("sh_gate", "sh_up", "sh_down", "e_gate", "e_up", "e_down")})
    nc = bacc.Bacc("TRN2", target_bir_lowering=False, num_devices=1)
    aps = {n: nc.dram_tensor("in_" + n, v.shape, mybir.dt.from_np(v.dtype), kind="ExternalInput").ap() for n, v in arrays.items()}
    out = nc.dram_tensor("out", [T, D], F32, kind="ExternalOutput").ap()
    build_program(nc, aps, out)
    r = run_bass_kernel_spmd(nc, [{"in_" + n: v for n, v in arrays.items()}], core_ids=[0])
    return r.results[0]["out"].reshape(B, S, D)
```

```python
import concourse.bass as bass
from concourse import mybir
from contextlib import ExitStack

F32 = mybir.dt.float32
F32R = mybir.dt.float32r
BF16 = mybir.dt.bfloat16
I32 = mybir.dt.int32
U32 = mybir.dt.uint32
ALU = mybir.AluOpType
ACT = mybir.ActivationFunctionType
AX = mybir.AxisListType

B, S, D = 8, 256, 256
T = B * S
H, DK = 16, 16
L = 32
E, F = 8, 512
P = 128
NT = T // P
DC = D // P
FC = F // P
QK_SCALE = 1.0 / DK ** 0.5
EMB_SCALE = 0.15
LN_EPS, RMS_EPS = 1e-5, 1e-6

LEFT = (0, 0, 1, 0, 2, 1)
RIGHT = (0, 1, 0, 2, 0, 1)
SLOTS = len(LEFT)
KP = SLOTS * DK
L3 = 3 * L

BP = 2
NPAIR = B // BP
QI = 16
STEPS = P // QI
COLS = BP * H * QI
PADV = 32
SLOTS_X = (2 * T + E * (P - 1)) // P
RING = 4
NG = H // 4


class Shared:
    pass


def names(n):
    return [str(i) for i in range(n)]


def first(i):
    return isinstance(i, int) and i == 0


class Chain:

    def __init__(self, eng, sem):
        self.eng, self.sem, self.base, self.k, self.trip, self.per = eng, sem, 0, 0, None, 0

    def enter(self, trip, per):
        self.base, self.k, self.trip, self.per = self.base + self.k, 0, trip, per

    def leave(self, trips):
        assert self.k == self.per, self.k
        self.base, self.k, self.trip = self.base + trips * self.per, 0, None

    def __call__(self, ins, apart=None):
        ins.then_inc(self.sem, 1)
        self.k += 1
        done = self.base + self.k
        self.eng.wait_ge(self.sem, done if self.trip is None else self.trip * self.per + done)
        if apart is not None:
            self.eng.sem_inc(apart)


def build_program(nc, a, outs):
    ctx = ExitStack()
    with ctx:
        def sem(name):
            return ctx.enter_context(nc.semaphore(name))

        def kept(name, shape, dt):
            return ctx.enter_context(nc.sbuf_tensor(name, shape, dt))

        g = Shared()
        g.sem = sem
        g.ps = ctx.enter_context(nc.psum_tensor("ps", [P, 8, 512], F32))
        g.identF = kept("identF", [P, P], F32)
        g.identB = kept("identB", [P, P], BF16)
        g.negIB = kept("negIB", [P, P], BF16)
        g.xs = nc.dram_tensor("expert_in", [SLOTS_X * P, D], F32, kind="Internal").ap()
        g.ys = nc.dram_tensor("expert_out", [SLOTS_X * P, D], F32, kind="Internal").ap()
        g.qd = nc.dram_tensor("qk_parts", [2, 3, D, T], BF16, kind="Internal").ap()
        g.HS = kept("HS", [P, NT, D], F32)
        g.V2 = kept("V2", [P, NT, H, DK], F32)
        g.H2T = g.V2[:].rearrange("p t h d -> p (t h d)").rearrange("p (c t) -> p c t", c=DC)
        g.XS = kept("XS", [P, NT, D], F32)
        g.pick = kept("pick", [P, 2, NT, E], F32)
        g.share = kept("share", [P, NT, 2], F32)
        g.LG = kept("LG", [P, NT, E], F32)
        g.SG, g.SU = kept("SG", [P, DC, F], F32), kept("SU", [P, DC, F], F32)
        g.SD = kept("SD", [P, FC, D], F32)
        g.s_sw, g.s_zd = sem("shared_w"), sem("zeroed")
        g.s_ld = [sem("fa_load" + n) for n in names(2)]
        with ExitStack() as mid:
            g.QK = mid.enter_context(nc.sbuf_tensor("QK", [KP, 2, 2, H, S], BF16))
            g.OT = mid.enter_context(nc.sbuf_tensor("OT", [P, NT, NG, P], F32))
            with ExitStack() as low:
                def lo(name, shape, dt):
                    return low.enter_context(nc.sbuf_tensor(name, shape, dt))
                g.WoT = lo("WoT", [P, DC, D], F32)
                g.R3 = lo("R3", [L3, D], BF16)
                g.OH3 = lo("OH3", [L3, (NPAIR + 1) * BP * S], BF16)
                g.ErT = lo("ErT", [KP, 2 * S], BF16)
                g.QT = lo("QT", [L, H, KP], BF16)
                g.ACP = lo("ACP", [L, H, L3], BF16)
                g.V3 = lo("V3", [L3, D], BF16)
                tables(nc, g, a)
                level_attention(nc, g)
                project(nc, g, a)
            full_attention(nc, g)
            route(nc, g, a)
        experts(nc, g, a, outs)


def split(eng, do, src, rest, rest2, out):
    do(eng.tensor_copy(out[0], src))
    do(eng.tensor_tensor(rest, src, out[0], ALU.subtract))
    do(eng.tensor_copy(out[1], rest))
    do(eng.tensor_tensor(rest2, rest, out[1], ALU.subtract))
    do(eng.tensor_copy(out[2], rest2))


def tables(nc, g, a):
    sem, ps = g.sem, g.ps
    s_in = [sem("in_" + n) for n in ("tok", "tab", "w", "er", "id", "wo", "bias")]
    s_dve, s_act, s_pool = sem("tab_dve"), sem("tab_act"), sem("tab_pool")
    s_lv, s_lvp, s_ln, s_xt, s_xtc, s_proj, s_sp, s_qkT, s_qkTc, s_ac, s_er, s_erT, s_idb, s_rs, s_zero = (
        sem("tab_" + n) for n in "levels levelsB norm xT xTc proj split qkT qkTc ac er erT idb rstd zero".split())
    with ExitStack() as c:
        def sb(n, sh, dt):
            return c.enter_context(nc.sbuf_tensor("t_" + n, sh, dt))
        tok, tokf = sb("tok", [B, S], I32), sb("tokf", [B, S], F32)
        acc, Dl, nD, rD, zer, lev = (sb(n, [B, S], F32) for n in ("acc", "Dl", "nD", "rD", "zer", "lev"))
        sel, lvl = sb("sel", [B, B, L3], F32), sb("lvl", [L3, 1], F32)
        emb, xt, bo = sb("emb", [L, D], F32), sb("xt", [L, D], F32), sb("bo", [L, D], F32)
        st, mv, half = sb("st", [L, 6], F32), sb("mv", [L, 4], F32), sb("half", [L, 1], F32)
        xT = sb("xT", [P, DC, L], F32)
        W = sb("W", [P, 3, DC, D], F32)
        zfill = g.SG[:].rearrange("p c f -> p (c f)")[:, 0:3 * D]
        bias, tab = sb("bias", [L, 3, D], F32), sb("tab", [L, 3, D], F32)
        r1, r2 = sb("r1", [L, 3, D], F32), sb("r2", [L, 3, D], F32)
        parts = [sb("part" + i, [L, 3, D], BF16) for i in names(3)]
        KT = sb("KT", [L, H, KP], BF16)
        qkT = sb("qkT", [KP, 2, H, L], BF16)
        er, e1, e2 = sb("er", [P, 4, DK], F32), sb("e1", [P, 4, DK], F32), sb("e2", [P, 4, DK], F32)
        eparts = [sb("epart" + i, [P, 4, DK], BF16) for i in names(3)]
        EP = sb("EP", [P, 4, SLOTS, DK], BF16)
        ac, a1, a2 = sb("ac", [L, H, L], F32), sb("a1", [L, H, L], F32), sb("a2", [L, H, L], F32)
        rr, rr1, rr2 = sb("rr", [L, D], F32), sb("rr1", [L, D], F32), sb("rr2", [L, D], F32)
        rparts = sb("rparts", [L, 3, D], BF16)
        psf = ps[:].rearrange("p a b -> p (a b)")
        with nc.Block() as block:
            @block.sync
            def _(sp):
                sp.dma_start(emb[:], a["emb"]).then_inc(s_in[1], 16)
                sp.dma_start(g.identF[:], a["ident"]).then_inc(s_in[4], 16)
                sp.dma_start(tok[:], a["x"]).then_inc(s_in[0], 16)
                sp.dma_start(sel[:], a["sel"]).then_inc(s_in[0], 16)
                sp.dma_start(lvl[:], a["lvl"]).then_inc(s_in[0], 16)
                sp.dma_start(er[:], a["er"]).then_inc(s_in[3], 16)
                sp.dma_start(g.WoT[:], a["WoT"]).then_inc(s_in[5], 16)
                sp.wait_ge(s_zero, 1)
                sp.dma_start(g.xs.rearrange("(n p r) d -> p n (r d)", r=3, p=P), zfill.unsqueeze(1).to_broadcast([P, SLOTS_X // 3, 3 * D])
                             ).then_inc(g.s_zd, 16)
                sp.wait_ge(s_in[5], 16)

            @block.scalar
            def _(act):
                for n, w in enumerate((a["WqT"], a["WkT"], a["WvT"])):
                    act.dma_start(W[:, n], w).then_inc(s_in[2], 16)
                act.dma_start(bias[:], a["bias"]).then_inc(s_in[6], 16)
                act.dma_start(bo[:], a["bo"]).then_inc(s_in[6], 16)
                copy = lambda out, in_: nc.scalar.activation(out, in_, ACT.Copy)
                act.wait_ge(s_xt, 1)
                copy(xT[:], psf[:, 2048:2048 + DC * L].rearrange("p (c l) -> p c l", c=DC)).then_inc(s_xtc, 1)
                act.wait_ge(s_qkT, 1)
                for n in range(2):
                    copy(qkT[:, n].rearrange("p h l -> p (h l)"), ps[0:KP, 5 + n].bitcast(BF16)[:, 0:512]).then_inc(s_qkTc, 1)
                act.wait_ge(s_erT, 1)
                copy(g.ErT[:], ps[0:KP, 4].bitcast(BF16)[:, 0:512]).then_inc(s_act, 1)
                act.wait_ge(s_act, 1)

            @block.gpsimd
            def _(pool):
                G = nc.gpsimd
                do = Chain(pool, s_pool)
                do(G.memset(half[:], -0.5))
                pool.wait_ge(s_ln, 1)
                G.tensor_tensor(mv[:, 3:4], mv[:, 2:3], half[:], ALU.pow).then_inc(s_rs, 1)
                pool.wait_ge(s_in[3], 16)
                split(G, do, er[:], e1[:], e2[:], [x[:] for x in eparts])
                for n in range(SLOTS):
                    do(G.tensor_copy(EP[:, :, n], eparts[RIGHT[n]][:]))
                G.memset(half[:], -0.5).then_inc(s_er, 1)
                G.memset(zfill, 0.0).then_inc(s_zero, 1)
                pool.wait_ge(s_in[6], 32)
                pool.wait_ge(s_ln, 2)
                do(G.tensor_tensor(rr[:], emb[:], bo[:], ALU.add))
                split(G, do, rr[:], rr1[:], rr2[:], [rparts[:, n] for n in range(3)])
                for n in range(3):
                    do(G.tensor_copy(g.R3[n * L:(n + 1) * L], rparts[:, n]))

            @block.vector
            def _(dve):
                do = Chain(dve, s_dve)
                V = nc.vector

                do(V.memset(zer[:], 0.0))
                dve.wait_ge(s_in[1], 16)
                do(V.tensor_scalar(emb[:], emb[:], EMB_SCALE, None, ALU.mult))
                do(V.bn_stats(st[:], emb[:]))
                do(V.bn_aggr(mv[:, 0:2], st[:]))
                V.tensor_scalar(mv[:, 2:3], mv[:, 1:2], LN_EPS, None, ALU.add).then_inc(s_ln, 1)
                dve.wait_ge(s_in[4], 16)
                V.tensor_copy(g.identB[:], g.identF[:]).then_inc(s_idb, 1)
                V.tensor_scalar(g.negIB[:], g.identF[:], -1.0, None, ALU.mult).then_inc(s_idb, 1)
                dve.wait_ge(s_rs, 1)
                V.tensor_scalar(xt[:], emb[:], mv[:, 0:1], mv[:, 3:4], ALU.subtract, ALU.mult).then_inc(s_ln, 1)
                dve.wait_ge(s_in[0], 48)
                do(V.tensor_copy(tokf[:], tok[:]))
                do(V.tensor_scalar(acc[:], tokf[:], 41.0, None, ALU.is_equal))
                for close in (93.0, 125.0):
                    do(V.scalar_tensor_tensor(acc[:], tokf[:], close, acc[:], ALU.is_equal, ALU.add))
                do(V.scalar_tensor_tensor(acc[:], tokf[:], 40.0, acc[:], ALU.is_equal, ALU.subtract))
                for opened in (91.0, 123.0):
                    do(V.scalar_tensor_tensor(acc[:], tokf[:], opened, acc[:], ALU.is_equal, ALU.add))
                do(V.tensor_tensor_scan(Dl[:], acc[:], zer[:], 0.0, ALU.add, ALU.add))
                do(V.tensor_scalar(nD[:], Dl[:], -1.0, None, ALU.mult))
                do(V.tensor_scalar(rD[:], Dl[:], -1.0, float(L - 1), ALU.mult, ALU.add))
                do(V.tensor_tensor_scan(acc[:], nD[:], rD[:], 0.0, ALU.max, ALU.min))
                V.tensor_tensor(lev[:], acc[:], Dl[:], ALU.add).then_inc(s_lv, 1)
                dve.wait_ge(s_in[6], 32)
                for n in range(3):
                    dve.wait_ge(s_proj, n + 1)
                    do(V.tensor_tensor(tab[:, n], ps[0:L, 5 + n, 0:D], bias[:, n], ALU.add))
                split(V, do, tab[:], r1[:], r2[:], [x[:] for x in parts])
                heads = [[x[:, n].rearrange("p (h d) -> p h d", h=H) for x in parts] for n in range(2)]
                for n in range(SLOTS):
                    at = slice(n * DK, (n + 1) * DK)
                    do(V.tensor_copy(g.QT[:, :, at], heads[0][LEFT[n]]))
                    do(V.tensor_copy(KT[:, :, at], heads[1][RIGHT[n]]))
                V.memset(zer[0:1, 0:1], 0.0).then_inc(s_sp, 1)
                do(V.memset(g.OH3[:, T:], 0.0))
                for q in range(4):
                    dve.wait_ge(s_lvp, q + 1)
                    do(V.tensor_scalar(g.OH3[:, q * 512:(q + 1) * 512], ps[0:L3, q, :], lvl[:, 0:1], None, ALU.is_equal))
                dve.wait_ge(s_ac, 1)
                do(V.tensor_copy(ac[:], ps[0:L, 7].rearrange("p (h l) -> p h l", h=H)))
                split(V, do, ac[:], a1[:], a2[:], [g.ACP[:, :, n * L:(n + 1) * L] for n in range(3)])
                for n in range(3):
                    do(V.tensor_copy(g.V3[n * L:(n + 1) * L], parts[n][:, 2]))

            @block.tensor
            def _(pe):
                mm = nc.tensor.matmul
                pe.wait_ge(s_ln, 2)
                pe.wait_ge(s_in[4], 16)
                for n in range(DC):
                    last = nc.tensor.transpose(psf[:, 2048 + n * L:2048 + (n + 1) * L], xt[:, n * P:(n + 1) * P], g.identF[0:L, 0:L])
                last.then_inc(s_xt, 1)
                pe.wait_ge(s_xtc, 1)
                pe.wait_ge(s_in[2], 48)
                for n in range(3):
                    for c_ in range(DC):
                        last = mm(ps[0:L, 5 + n, 0:D], xT[:, c_], W[:, n, c_], start=c_ == 0, stop=c_ == DC - 1)
                    last.then_inc(s_proj, 1)
                pe.wait_ge(s_lv, 1)
                for b in range(B):
                    last = mm(ps[0:L3, b // 2, (b % 2) * S:(b % 2 + 1) * S], sel[:, b], lev[:], start=True, stop=True)
                    if b % 2:
                        last.then_inc(s_lvp, 1)
                pe.wait_ge(s_idb, 2)
                pe.wait_ge(s_sp, 1)
                for n, t in enumerate((g.QT, KT)):
                    for h in range(H):
                        last = nc.tensor.transpose(ps[0:KP, 5 + n].bitcast(BF16)[:, h * L:(h + 1) * L], t[:, h], g.identB[0:L, 0:L])
                last.then_inc(s_qkT, 1)
                pe.wait_ge(s_er, 1)
                for n in range(4):
                    last = nc.tensor.transpose(ps[0:KP, 4].bitcast(BF16)[:, n * P:(n + 1) * P], EP[:, n].rearrange("p s d -> p (s d)"), g.identB[:])
                last.then_inc(s_erT, 1)
                pe.wait_ge(s_qkTc, 2)
                for h in range(H):
                    last = mm(ps[0:L, 7, h * L:(h + 1) * L], qkT[:, 0, h], qkT[:, 1, h], start=True, stop=True)
                last.then_inc(s_ac, 1)


def level_attention(nc, g):
    sem, ps = g.sem, g.ps
    (s_evac, s_mx, s_tr, s_m, s_qp, s_qb, s_ap, s_ab, s_vp, s_vs, s_pv, s_ot, s_ms, s_apart) = (
        sem("la_" + n) for n in ("evac halfmax turned max q_made q_kept a_made a_kept "
                                 "v_made v_kept pv out init apart").split())
    s_built, s_ready, s_exp = ([sem("la_" + n + k) for k in names(2)] for n in ("built", "ready", "exp"))
    NS = 2 * STEPS
    UN = H // 2
    FIRST = ((6, 7), (2, 3))
    with ExitStack() as c:
        def sb(n, sh, dt):
            return c.enter_context(nc.sbuf_tensor("la_" + n, sh, dt))
        def flat(x, pattern):
            return x[:].rearrange(pattern)
        QB = flat(g.V2, "p t h d -> p (t h d)").bitcast(BF16)[0:KP].rearrange("p (f b h i) -> p f b h i", f=2, b=BP, h=H)
        AQ = flat(g.XS, "p t d -> p (t d)").bitcast(BF16)[0:L3].rearrange("p (f b h i) -> p f b h i", f=2, b=BP, h=H)
        rows = flat(g.HS, "p t d -> p (t d)")
        VW = BP * 2 * H * PADV
        Vs = rows[:, 0:VW].rearrange("p (b j h d) -> p b j h d", b=BP, j=2, h=H)
        SA, SM = (rows[:, VW + k * COLS:VW + (k + 1) * COLS].bitcast(BF16).rearrange("p (n c) -> p n c", n=2) for k in range(2))
        m = sb("m", [P, 2, 4], BF16)
        PT = sb("PT", [P, 2, 2, BP * H, P], F32)
        OHq = g.OH3[0:L].rearrange("p (q b f i) -> p q b f i", b=BP, f=2, i=P)
        XT = ps[:, 4].bitcast(BF16)[:, 0:512]
        with nc.Block() as block:
            @block.gpsimd
            def _(pool):
                nc.gpsimd.memset(Vs[:, :, :, :, DK:PADV], 0.0).then_inc(s_ms, 1)
                pool.wait_ge(s_ms, 1)
                nc.gpsimd.memset(Vs[:, :, :, :, DK:DK + 1], 1.0).then_inc(s_ms, 1)

            @block.tensor
            def _(pe):
                mm = nc.tensor.matmul

                def make_unit(pair, half, u, made, banks=(6, 7), kept=None):
                    kept = made + 1 if kept is None else kept
                    pe.wait_ge(s_qb, kept)
                    pe.sem_inc(s_apart)
                    rhs = OHq[:, bass.ds(pair, 1), :, half, :]
                    for k in range(2):
                        last = mm(ps[0:KP, banks[0], k * BP * P:(k + 1) * BP * P], g.QT[:, 2 * u + k], rhs, start=True, stop=True)
                    last.then_inc(s_qp, 1)
                    pe.wait_ge(s_ab, kept)
                    pe.sem_inc(s_apart)
                    for k in range(2):
                        last = mm(ps[0:L3, banks[1], k * BP * P:(k + 1) * BP * P], g.ACP[:, 2 * u + k], rhs, start=True, stop=True)
                    last.then_inc(s_ap, 1)

                def build(pair, n, jh):
                    half, k = divmod(n % NS, STEPS)
                    q0 = k * QI
                    if n >= 2:
                        pe.wait_ge(s_exp[jh], pair * NS + n - 1)
                    bank = ps[:, 2 * (n % 2) + jh]
                    for b in range(BP):
                        mm(bank[:, b * H * QI:(b + 1) * H * QI], g.OH3[:, bass.ds(pair * (BP * S) + (n // NS * BP + b) * S + jh * P, P)],
                           AQ[:, half, b, :, q0:q0 + QI], start=b == 0, stop=False, skip_group_check=True)
                    cols = bank.rearrange("p (h i) -> p h i", i=QI)
                    q = QB[:, half].rearrange("p b h i -> p (b h) i")
                    for i in range(QI):
                        w0 = S - (half * P + q0 + i) + jh * P
                        last = mm(cols[:, :, i], g.ErT[:, w0:w0 + P], q[:, :, q0 + i], start=False, stop=False,
                                  skip_group_check=True)
                    last.then_inc(s_built[jh], 1)

                def turn(pair, n):
                    pe.wait_ge(s_mx, pair * NS + n + 1)
                    for q in range(4):
                        last = nc.tensor.transpose(XT[:, q * P:(q + 1) * P], SM[:, n % 2, q * P:(q + 1) * P], g.identB[:])
                    last.then_inc(s_tr, 1)

                def subtract_max(pair, n):
                    pe.wait_ge(s_m, pair * NS + n + 1)
                    for jh in range(2):
                        for q in range(4):
                            last = mm(ps[:, 2 * (n % 2) + jh, q * P:(q + 1) * P], m[:, n % 2, q:q + 1].to_broadcast([P, P]), g.negIB[:],
                                      start=False, stop=True, skip_group_check=True)
                        last.then_inc(s_ready[jh], 1)

                def make_values(pair, b):
                    pe.wait_ge(s_vs, pair * BP + b + 1)
                    pe.wait_ge(s_ot, pair * 4 + 1)
                    for jh in range(2):
                        last = mm(ps[:, 5, jh * D:(jh + 1) * D], g.OH3[:, bass.ds(pair * (BP * S) + b * S + jh * P, P)], g.V3[:],
                                  start=True, stop=True)
                    last.then_inc(s_vp, 1)

                def weigh_values(pair, half, b, groups):
                    if groups[0] == 0:
                        for jh in range(2):
                            pe.wait_ge(s_exp[jh], pair * NS + (half + 1) * STEPS)
                        pe.wait_ge(s_vs, pair * BP + BP + 1)
                        pe.wait_ge(s_ot, pair * 4 + half * 2 + b + 1)
                    for grp in groups:
                        for jh in range(2):
                            for k in range(4):
                                h = 4 * grp + k
                                last = mm(ps[32 * k:32 * k + PADV, 5, grp * P:(grp + 1) * P], Vs[:, b, jh, h],
                                          PT[:, half, jh, b * H + h], start=jh == 0, stop=jh == 1, skip_group_check=True)
                    if groups[-1] == NG - 1:
                        last.then_inc(s_pv, 1)

                def kept_units(count):
                    pe.wait_ge(s_qb, count + 1)
                    pe.wait_ge(s_ab, count + 1)

                for u in range(UN):
                    make_unit(0, 0, u, u, FIRST[u % 2], max(u, 1))
                kept_units(UN)
                pe.wait_ge(s_ms, 2)
                for jh in range(2):
                    build(0, 0, jh)
                with pe.Fori(0, NPAIR) as pair:
                    for n in range(NS):
                        half, k = divmod(n, STEPS)
                        if k == STEPS - 1:
                            kept_units(pair * (2 * UN) + (2 + half) * UN)
                        build(pair, n + 1, 0)
                        turn(pair, n)
                        if k == 0:
                            make_unit(pair + half, 1 - half, 0, pair * (2 * UN) + UN + half * UN)
                        build(pair, n + 1, 1)
                        if n < BP:
                            make_values(pair, n)
                        subtract_max(pair, n)
                        if k < UN - 1:
                            make_unit(pair + half, 1 - half, k + 1, pair * (2 * UN) + UN + half * UN + k + 1)
                        if half and k < UN - 1:
                            for x in ((0, 1) if k == 0 else (k + 1,)):
                                weigh_values(pair, 0, x // NG, (x % NG,))
                    for b in range(BP):
                        weigh_values(pair, 1, b, range(NG))

            @block.scalar
            def _(act):
                def keep_unit(half, u, made, bank=7):
                    act.wait_ge(s_ap, made)
                    nc.scalar.activation(AQ[:, half, :, 2 * u:2 * u + 2], ps[0:L3, bank].rearrange("p (h b i) -> p b h i", h=2, b=BP),
                                         ACT.Copy).then_inc(s_ab, 1)

                def copy_half(pair, n):
                    act.wait_ge(s_built[0], pair * NS + n + 1)
                    nc.scalar.activation(SA[:, n % 2], ps[:, 2 * (n % 2)], ACT.Copy).then_inc(s_evac, 1)

                nc.scalar.activation(AQ[0:1, 0, 0, 0, 0:1], g.identF[0:1, 0:1], ACT.Copy).then_inc(s_ab, 1)
                nc.scalar.activation(Vs[0:1, 0, 0, 0, 0:1], g.identF[0:1, 0:1], ACT.Copy).then_inc(s_vs, 1)
                act.wait_ge(s_vs, 1)
                act.wait_ge(s_ab, 1)
                for u in range(UN):
                    keep_unit(0, u, u + 1, FIRST[u % 2][1])
                copy_half(0, 0)
                with act.Fori(0, NPAIR) as pair:
                    for n in range(NS):
                        half, k = divmod(n, STEPS)
                        copy_half(pair, n + 1)
                        if k == 0:
                            keep_unit(1 - half, 0, pair * (2 * UN) + UN + half * UN + 1)
                        if n < BP:
                            act.wait_ge(s_vp, pair * BP + n + 1)
                            nc.scalar.activation(Vs[:, n, :, :, 0:DK], ps[:, 5].rearrange("p (j h d) -> p j h d", j=2, h=H),
                                                 ACT.Copy).then_inc(s_vs, 1)
                        for jh in range(2):
                            act.wait_ge(s_ready[jh], pair * NS + n + 1)
                            nc.scalar.activation(PT[:, half, jh, :, k * QI:(k + 1) * QI],
                                                 ps[:, 2 * (n % 2) + jh].rearrange("p (h i) -> p h i", i=QI),
                                                 ACT.Exp, scale=QK_SCALE).then_inc(s_exp[jh], 1)
                        if k < UN - 1:
                            keep_unit(1 - half, k + 1, pair * (2 * UN) + UN + half * UN + k + 2)

            @block.vector
            def _(dve):
                def keep_unit(half, u, made, bank=6):
                    dve.wait_ge(s_qp, made)
                    nc.vector.tensor_copy(QB[:, half, :, 2 * u:2 * u + 2], ps[0:KP, bank].rearrange("p (h b i) -> p b h i", h=2, b=BP)
                                          ).then_inc(s_qb, 1)

                def keep_out(pair, half, b):
                    dve.wait_ge(s_pv, pair * 4 + half * 2 + b + 1)
                    nc.vector.tensor_copy(g.OT[:, bass.ds(pair * 4 + b * 2 + half, 1)], ps[:, 5].rearrange("p (o g i) -> p o g i", o=1, g=NG)
                                          ).then_inc(s_ot, 1)

                nc.vector.memset(QB[0:1, 0, 0, 0, 0:1], 0.0).then_inc(s_qb, 1)
                nc.vector.memset(g.OT[0:1, 0, 0, 0:1], 0.0).then_inc(s_ot, 1)
                dve.wait_ge(s_qb, 1)
                dve.wait_ge(s_ot, 1)
                for u in range(UN):
                    keep_unit(0, u, u + 1, FIRST[u % 2][0])
                def halves_max(pair, n):
                    dve.wait_ge(s_built[1], pair * NS + n + 1)
                    dve.wait_ge(s_evac, pair * NS + n + 1)
                    nc.vector.tensor_tensor(SM[:, n % 2], ps[:, 2 * (n % 2) + 1], SA[:, n % 2], ALU.max).then_inc(s_mx, 1)

                halves_max(0, 0)
                with dve.Fori(0, NPAIR) as pair:
                    for n in range(NS):
                        half, k = divmod(n, STEPS)
                        dve.wait_ge(s_tr, pair * NS + n + 1)
                        nc.vector.reduce_max(m[:, n % 2], XT.rearrange("p (q j) -> p q j", q=4), AX.X).then_inc(s_m, 1)
                        if k == 0:
                            keep_unit(1 - half, 0, pair * (2 * UN) + UN + half * UN + 1)
                        if n in (NS - 5, NS - 1):
                            keep_out(pair, 0, int(n == NS - 1))
                        halves_max(pair, n + 1)
                        if k < UN - 1:
                            keep_unit(1 - half, k + 1, pair * (2 * UN) + UN + half * UN + k + 2)
                    for b in range(BP):
                        keep_out(pair, 1, b)


GT = 2
GN = NT // GT
GC = GT * P


def pe_turn_rows(nc, pe, g, s, i):
    pe.wait_ge(s.ots, i + 1)
    if not first(i):
        pe.wait_ge(s.at, i)
    for k in range(GT):
        for grp in range(NG):
            last = nc.tensor.transpose(g.ps[:, k, grp * P:(grp + 1) * P], s.OTs[:, k, grp], g.identF[:])
    last.then_inc(s.rows, 1)


def pe_turn_att(nc, pe, g, s, i):
    pe.wait_ge(s.at, i + 1)
    if not first(i):
        pe.wait_ge(s.attc, i)
    for k in range(GT):
        for c in range(DC):
            last = nc.tensor.transpose(g.ps[:, 2, c * GC + k * P:c * GC + (k + 1) * P], s.AT[:, k, c * P:(c + 1) * P], g.identF[:])
    last.then_inc(s.att, 1)


def act_keep_att(nc, act, g, s, i, s_h):
    act.wait_ge(s.att, i + 1)
    if not first(i):
        act.wait_ge(s_h, i)
    nc.scalar.activation(s.ATT[:], g.ps[:, 2].rearrange("p (c t) -> p c t", c=DC), ACT.Copy).then_inc(s.attc, 1)


def dve_fetch_sums(nc, dve, g, s, i):
    nc.vector.tensor_copy(s.OTs[:], g.OT[:, bass.ds(i * GT, GT)]).then_inc(s.ots, 1)


def dve_divide_heads(nc, dve, g, s, i):
    dve.wait_ge(s.rows, i + 1)
    if not first(i):
        dve.wait_ge(s.at, i)
    rows = g.ps[:, 0:GT].rearrange("p k (h d) -> p (k h) d", d=PADV)
    nc.vector.reciprocal(s.rec[:], rows[:, :, DK]).then_inc(s.recip, 1)
    dve.wait_ge(s.recip, i + 1)
    if not first(i):
        dve.wait_ge(s.att, i)
    nc.vector.tensor_tensor(s.AT[:].rearrange("p k (h d) -> p (k h) d", d=DK), rows[:, :, 0:DK],
                            s.rec[:].unsqueeze(2).to_broadcast([P, GT * H, DK]), ALU.mult).then_inc(s.at, 1)


def head_buffers(g, c, nc, tag):
    def sb(n, sh):
        return c.enter_context(nc.sbuf_tensor(tag + n, sh, F32))
    s = Shared()
    s.OTs, s.AT, s.ATT, s.rec = sb("OTs", [P, GT, NG, P]), sb("AT", [P, GT, D]), sb("ATT", [P, DC, GC]), sb("rec", [P, GT * H])
    s.ots, s.rows, s.recip, s.at, s.att, s.attc = (g.sem(tag + n) for n in ("ots", "rows", "recip", "at", "att", "attc"))
    return s


def project(nc, g, a):
    sem, ps = g.sem, g.ps
    (s_h, s_hs, s_var, s_rs, s_x, s_ms, s_r2, s_hn, s_ht, s_htc, s_moved, s_v, s_vk, s_dv, s_half, s_apart) = (
        sem("pj_" + n) for n in "h hs var rs x ms r2 hn ht htc moved v vkept dve half apart".split())
    s_q, s_hi, s_r1, s_mi, s_lo = ([sem("pj_" + n + k) for k in "qk"] for n in ("made_", "high_", "rest_", "mid_", "low_"))
    with ExitStack() as c:
        def sb(n, sh, dt):
            return c.enter_context(nc.sbuf_tensor("pj_" + n, sh, dt))
        s = head_buffers(g, c, nc, "pj_")
        st, mv, half = sb("st", [P, GT, 6], F32), sb("mv", [P, GT, 8], F32), sb("half", [P, GT], F32)
        hn, hT = sb("hn", [P, GT, D], F32), sb("hT", [P, DC, GC], F32)
        w1 = sb("w1", [P, D], F32)
        W = sb("W", [P, 3, DC, D], F32)
        r1 = sb("r1", [P, 2, DC * GC], F32)
        parts = sb("parts", [P, 2, 3, DC * GC], BF16)
        qd = g.qd.rearrange("k a (m p) t -> k p (a m) t", p=P)
        with nc.Block() as block:
            @block.sync
            def _(sp):
                sp.dma_start(w1[:], a["w1"]).then_inc(s_moved, 16)
                for n, w in enumerate((a["wq"], a["wk"], a["wv"])):
                    sp.dma_start(W[:, n], w).then_inc(s_moved, 16)

                def store(t):
                    for k in range(2):
                        sp.wait_ge(s_lo[k], t + 1)
                        sp.dma_start(qd[k, :, :, bass.ds(t * GC, GC)], parts[:, k].rearrange("p a (m t) -> p (a m) t", m=DC)).then_inc(s_moved, 16)

                for t in range(2):
                    store(t)
                sp.wait_ge(s_moved, 64 + 2 * 32)
                for b in range(2):
                    load_packed(g, sp, b, b)
                with sp.Fori(2, GN) as t:
                    store(t)
                sp.wait_ge(s_moved, 64 + GN * 32)

            @block.gpsimd
            def _(pool):
                nc.gpsimd.memset(half[:], -0.5).then_inc(s_half, 1)
                pool.wait_ge(s_half, 1)

                def powers(t):
                    pool.wait_ge(s_var, t + 1)
                    nc.gpsimd.tensor_tensor(mv[:, :, 3], mv[:, :, 2], half[:], ALU.pow).then_inc(s_rs, 1)
                    pool.wait_ge(s_ms, t + 1)
                    nc.gpsimd.tensor_tensor(mv[:, :, 5], mv[:, :, 4], half[:], ALU.pow).then_inc(s_r2, 1)

                def low(i, n):
                    pool.wait_ge(s_mi[n], i + 1)
                    nc.gpsimd.tensor_tensor(parts[:, n, 2], r1[:, n], parts[:, n, 1], ALU.subtract).then_inc(s_lo[n], 1)

                powers(0)
                with pool.Fori(0, GN - 1) as t:
                    powers(t + 1)
                    for n in range(2):
                        low(t, n)
                for n in range(2):
                    low(GN - 1, n)

            @block.tensor
            def _(pe):
                mm = nc.tensor.matmul

                def output(i):
                    pe.wait_ge(s.attc, i + 1)
                    if not first(i):
                        pe.wait_ge(s_hs, i)
                    for k in range(GT):
                        out = ps[:, 3, k * D:(k + 1) * D]
                        for cc in range(DC):
                            mm(out, s.ATT[:, cc, k * P:(k + 1) * P], g.WoT[:, cc], start=cc == 0, stop=False)
                        last = mm(out, g.OH3[:, bass.ds(i * GC + k * P, P)], g.R3[:], start=False, stop=True)
                    last.then_inc(s_h, 1)

                def turn_normed(i):
                    pe.wait_ge(s_hn, i * GT + GT)
                    for k in range(GT):
                        for cc in range(DC):
                            last = nc.tensor.transpose(ps[:, 4, cc * GC + k * P:cc * GC + (k + 1) * P], hn[:, k, cc * P:(cc + 1) * P], g.identF[:])
                    last.then_inc(s_ht, 1)

                def query_key(i, n):
                    pe.wait_ge(s_htc, i + 1)
                    pe.wait_ge(s_r1[n], i + 1)
                    for m in range(DC):
                        for cc in range(DC):
                            last = mm(ps[:, 5 + n, m * GC:(m + 1) * GC], W[:, n, cc, m * P:(m + 1) * P], hT[:, cc], start=cc == 0, stop=cc == DC - 1)
                    last.then_inc(s_q[n], 1)

                def value(i):
                    pe.wait_ge(s_vk, i + 1)
                    for k in range(GT):
                        for cc in range(DC):
                            last = mm(ps[:, 7, k * D:(k + 1) * D], hT[:, cc, k * P:(k + 1) * P], W[:, 2, cc], start=cc == 0, stop=cc == DC - 1)
                    last.then_inc(s_v, 1)

                for i in range(2):
                    pe_turn_rows(nc, pe, g, s, i)
                    if i == 1:
                        output(0)
                    pe_turn_att(nc, pe, g, s, i)
                pe.wait_ge(s_moved, 64)

                def trip(t, ahead):
                    if ahead:
                        pe_turn_rows(nc, pe, g, s, t + 2)
                    output(t + 1)
                    turn_normed(t)
                    if ahead:
                        pe_turn_att(nc, pe, g, s, t + 2)
                    for n in range(2):
                        query_key(t, n)
                    value(t)

                with pe.Fori(0, GN - 2) as t:
                    trip(t, True)
                trip(GN - 2, False)
                turn_normed(GN - 1)
                query_key(GN - 1, 0)
                query_key(GN - 1, 1)
                value(GN - 1)

            @block.scalar
            def _(act):
                def copy(out, in_):
                    return nc.scalar.activation(out, in_, ACT.Copy)

                def residual(i):
                    act.wait_ge(s_h, i + 1)
                    copy(g.HS[:, bass.ds(i * GT, GT)], ps[:, 3].rearrange("p (k d) -> p k d", d=D)).then_inc(s_hs, 1)

                def turned(i):
                    act.wait_ge(s_ht, i + 1)
                    copy(hT[:], ps[:, 4].rearrange("p (c t) -> p c t", c=DC)).then_inc(s_htc, 1)

                def high(i, n):
                    act.wait_ge(s_q[n], i + 1)
                    act.wait_ge(s_moved, i * 32 + 64)
                    copy(parts[:, n, 0], ps[:, 5 + n]).then_inc(s_hi[n], 1)

                def mid(i, n):
                    act.wait_ge(s_r1[n], i + 2)
                    copy(parts[:, n, 1], r1[:, n]).then_inc(s_mi[n], 1)

                def value(i):
                    act.wait_ge(s_v, i + 1)
                    copy(g.V2[:, bass.ds(i * GT, GT)], ps[:, 7].rearrange("p (k h d) -> p k h d", h=H, d=DK)).then_inc(s_vk, 1)

                copy(hT[0:1, 0, 0:1], g.identF[0:1, 0:1]).then_inc(s_vk, 1)
                act.wait_ge(s_vk, 1)
                act_keep_att(nc, act, g, s, 0, s_h)
                residual(0)
                act_keep_att(nc, act, g, s, 1, s_h)

                def trip(t, ahead):
                    residual(t + 1)
                    turned(t)
                    if ahead:
                        act_keep_att(nc, act, g, s, t + 2, s_h)
                    for n in range(2):
                        high(t, n)
                    mid(t, 0)
                    value(t)
                    mid(t, 1)

                with act.Fori(0, GN - 2) as t:
                    trip(t, True)
                trip(GN - 2, False)
                turned(GN - 1)
                for n in range(2):
                    high(GN - 1, n)
                value(GN - 1)
                for n in range(2):
                    mid(GN - 1, n)

            @block.vector
            def _(dve):
                V = nc.vector
                do = Chain(dve, s_dv)

                def rest(i, n):
                    dve.wait_ge(s_hi[n], i + 1)
                    V.tensor_tensor(r1[:, n], ps[:, 5 + n], parts[:, n, 0], ALU.subtract).then_inc(s_r1[n], 1)

                def moments(i):
                    dve.wait_ge(s_hs, i + 1)
                    for k in range(GT):
                        do(V.bn_stats(st[:, k], g.HS[:, bass.ds(i * GT + k, 1)].rearrange("p o d -> p (o d)")), s_apart)
                        do(V.bn_aggr(mv[:, k, 0:2], st[:, k]))
                    V.tensor_scalar(mv[:, :, 2], mv[:, :, 1], LN_EPS, None, ALU.add).then_inc(s_var, 1)

                def layer_norm(i):
                    dve.wait_ge(s_rs, i + 1)
                    do(V.tensor_tensor(mv[:, :, 6], mv[:, :, 3], mv[:, :, 3], ALU.mult))
                    do(V.tensor_tensor(mv[:, :, 6], mv[:, :, 6], mv[:, :, 1], ALU.mult))
                    V.tensor_scalar(mv[:, :, 4], mv[:, :, 6], RMS_EPS, None, ALU.add).then_inc(s_ms, 1)
                    for k in range(GT):
                        V.tensor_scalar(g.XS[:, bass.ds(i * GT + k, 1)], g.HS[:, bass.ds(i * GT + k, 1)], mv[:, k, 0:1], mv[:, k, 3:4],
                                        ALU.subtract, ALU.mult).then_inc(s_x, 1)

                def rms_norm(i):
                    dve.wait_ge(s_x, i * GT + GT)
                    dve.wait_ge(s_r2, i + 1)
                    if not first(i):
                        dve.wait_ge(s_ht, i)
                    for k in range(GT):
                        V.scalar_tensor_tensor(hn[:, k:k + 1], g.XS[:, bass.ds(i * GT + k, 1)], mv[:, k, 5:6], w1[:].unsqueeze(1),
                                               ALU.mult, ALU.mult).then_inc(s_hn, 1)

                for n in range(2):
                    V.memset(parts[0:1, n, 0, 0:1], 0.0).then_inc(s_r1[n], 1)
                    dve.wait_ge(s_r1[n], 1)
                dve_fetch_sums(nc, dve, g, s, 0)
                for i in range(2):
                    dve_divide_heads(nc, dve, g, s, i)
                    dve_fetch_sums(nc, dve, g, s, i + 1)
                moments(0)
                layer_norm(0)
                dve.wait_ge(s_moved, 64)
                rms_norm(0)

                def trip(t, ahead, fetch):
                    if ahead:
                        dve_divide_heads(nc, dve, g, s, t + 2)
                    if fetch:
                        dve_fetch_sums(nc, dve, g, s, t + 3)
                    moments(t + 1)
                    layer_norm(t + 1)
                    rest(t, 0)
                    rms_norm(t + 1)
                    rest(t, 1)

                with dve.Fori(0, GN - 3) as t:
                    do.enter(t, 2 + 2 * GT)
                    trip(t, True, True)
                do.leave(GN - 3)
                trip(GN - 3, True, False)
                trip(GN - 2, False, False)
                for n in range(2):
                    rest(GN - 1, n)


def load_packed(g, sp, b, par):
    src = g.qd.rearrange("k a (h d) t -> k a d h t", d=DK)
    for k, side in enumerate((LEFT, RIGHT)):
        for n in range(SLOTS):
            sp.dma_start(g.QK[n * DK:(n + 1) * DK, par, k], src[k, side[n], :, :, bass.ds(b * S, S)]).then_inc(g.s_ld[par], 16)


def full_attention(nc, g):
    sem, ps = g.sem, g.ps
    (s_sc, s_max, s_lg, s_exp, s_pv, s_ot, s_vs, s_pad) = (sem("fa_" + n) for n in "scores max less exp pv out values pad".split())
    s_ld, QK = g.s_ld, g.QK
    HP = H // 2
    with ExitStack() as c:
        def sb(n, sh, dt):
            return c.enter_context(nc.sbuf_tensor("fa_" + n, sh, dt))
        m = sb("m", [P, 2, H, 2], BF16)
        PT = sb("PT", [P, 2, 4, 2, S], F32)
        Vs = sb("Vs", [P, 2, 2, H, PADV], F32)
        with nc.Block() as block:
            @block.sync
            def _(sp):
                with sp.Fori(0, B // 2 - 1) as t:
                    for par in range(2):
                        sp.wait_ge(s_lg, (2 * t + par + 1) * HP)
                        load_packed(g, sp, 2 * t + 2 + par, par)

            @block.tensor
            def _(pe):
                mm = nc.tensor.matmul

                def scores(b, par, h):
                    if h >= 2:
                        pe.wait_ge(s_max, b * H + h - 1)
                    for half in range(2):
                        last = mm(ps[:, h % 2, half * S:(half + 1) * S], QK[:, par, 0, h, half * P:(half + 1) * P], QK[:, par, 1, h],
                                  start=True, stop=True)
                    last.then_inc(s_sc, 1)

                def less_max(b, par, hp):
                    if hp >= 2:
                        pe.wait_ge(s_exp, b * HP + hp - 1)
                    pe.wait_ge(s_max, b * H + 2 * hp + 2)
                    for k in range(2):
                        h = 2 * hp + k
                        bank = ps[:, 2 + 2 * (hp % 2) + k]
                        for jh in range(2):
                            mm(bank[:, jh * S:(jh + 1) * S], QK[:, par, 1, h, jh * P:(jh + 1) * P], QK[:, par, 0, h],
                               start=jh == 0, stop=False, skip_group_check=True)
                        for jh in range(2):
                            for half in range(2):
                                at = jh * S + half * P
                                last = mm(bank[:, at:at + P], m[:, par, h, half:half + 1].to_broadcast([P, P]), g.negIB[:],
                                          start=False, stop=True, skip_group_check=True)
                    last.then_inc(s_lg, 1)

                def weigh(b, par, grp):
                    pe.wait_ge(s_exp, b * HP + 2 * grp + 2)
                    if grp % 2 == 0:
                        pe.wait_ge(s_ot, b * 2 + grp // 2 + 1)
                    for jh in range(2):
                        for k in range(4):
                            last = mm(ps[32 * k:32 * k + PADV, 6 + grp // 2, (grp % 2) * S:(grp % 2 + 1) * S],
                                      Vs[:, par, jh, 4 * grp + k], PT[:, grp % 2, k, jh], start=jh == 0, stop=jh == 1, skip_group_check=True)
                    last.then_inc(s_pv, 1)

                def begin(b, par, loaded):
                    pe.wait_ge(s_ld[par], loaded)
                    for h in range(2):
                        scores(b, par, h)

                LOADED = 2 * SLOTS * 16

                def sequence(t, par, more):
                    b = 2 * t + par
                    for h in (2, 3):
                        scores(b, par, h)
                    pe.wait_ge(s_vs, b + 1)
                    for hp in range(HP):
                        less_max(b, par, hp)
                        for h in (2 * hp + 4, 2 * hp + 5):
                            if h < H:
                                scores(b, par, h)
                        if hp % 2 == 0 and hp:
                            weigh(b, par, hp // 2 - 1)
                    if more:
                        begin(b + 1, 1 - par, (t + 1 + par) * LOADED)
                    weigh(b, par, NG - 1)

                begin(0, 0, LOADED)
                pe.wait_ge(s_pad, 2)
                with pe.Fori(0, B // 2 - 1) as t:
                    for par in range(2):
                        sequence(t, par, True)
                sequence(B // 2 - 1, 0, True)
                sequence(B // 2 - 1, 1, False)

            @block.gpsimd
            def _(pool):
                nc.gpsimd.memset(Vs[:, :, :, :, DK:PADV], 0.0).then_inc(s_pad, 1)
                pool.wait_ge(s_pad, 1)
                nc.gpsimd.memset(Vs[:, :, :, :, DK:DK + 1], 1.0).then_inc(s_pad, 1)

            @block.scalar
            def _(act):
                with act.Fori(0, B // 2) as t:
                    for par in range(2):
                        b = 2 * t + par
                        nc.scalar.activation(Vs[:, par, :, :, 0:DK], g.V2[:, bass.ds(2 * b, 2)], ACT.Copy).then_inc(s_vs, 1)
                        for hp in range(HP):
                            act.wait_ge(s_lg, b * HP + hp + 1)
                            if hp >= 4:
                                act.wait_ge(s_pv, b * NG + hp // 2 - 1)
                            grp, k = hp // 2, 2 * (hp % 2)
                            nc.scalar.activation(PT[:, grp % 2, k:k + 2], ps[:, 2 + 2 * (hp % 2):4 + 2 * (hp % 2)].rearrange("p k (j i) -> p k j i", j=2),
                                                 ACT.Exp, scale=QK_SCALE).then_inc(s_exp, 1)

            @block.vector
            def _(dve):
                def keep_out(b, x):
                    dve.wait_ge(s_pv, b * NG + 2 * x + 2)
                    nc.vector.tensor_copy(g.OT[:, bass.ds(2 * b, 2), 2 * x:2 * x + 2], ps[:, 6 + x].rearrange("p (g f i) -> p f g i", g=2, f=2)
                                          ).then_inc(s_ot, 1)

                for n in range(2):
                    nc.vector.memset(m[0:1, n, 0, 0:1], 0.0).then_inc(s_ot, 1)
                dve.wait_ge(s_ot, 2)

                def sequence(t, par, before):
                    b = 2 * t + par
                    for h in range(H):
                        dve.wait_ge(s_sc, b * H + h + 1)
                        nc.vector.reduce_max(m[:, par, h], ps[:, h % 2].rearrange("p (f j) -> p f j", f=2), AX.X).then_inc(s_max, 1)
                        if h == 1 and before:
                            keep_out(b - 1, 1)
                        if h == 13:
                            keep_out(b, 0)

                sequence(0, 0, False)
                sequence(0, 1, True)
                with dve.Fori(1, B // 2) as t:
                    for par in range(2):
                        sequence(t, par, True)
                keep_out(B - 1, 1)


def route(nc, g, a):
    sem, ps = g.sem, g.ps
    (s_in, s_h, s_x2, s_var, s_r2, s_hn, s_ht, s_htc, s_h2, s_lg, s_lgk, s_dv, s_half, s_kept, s_apart) = (
        sem("rt_" + n) for n in "in h x2 var r2 hn ht htc h2 logits lkept dve half kept apart".split())
    with ExitStack() as c:
        def sb(n, sh, dt):
            return c.enter_context(nc.sbuf_tensor("rt_" + n, sh, dt))
        s = head_buffers(g, c, nc, "rt_")
        st, mv, half = sb("st", [P, GT, 6], F32), sb("mv", [P, GT, 6], F32), sb("half", [P, GT], F32)
        X2, hn, hT = sb("X2", [P, GT, D], F32), sb("hn", [P, GT, D], F32), sb("hT", [P, DC, GC], F32)
        w2, W, rw = sb("w2", [P, D], F32), sb("W", [P, DC, D], F32), sb("rw", [P, DC, E], F32)
        with nc.Block() as block:
            @block.sync
            def _(sp):
                for o, i in ((W, a["wo"]), (w2, a["w2"]), (rw, a["rw"])):
                    sp.dma_start(o[:], i).then_inc(s_in, 16)
                sp.wait_ge(g.s_zd, 16)
                for o, i in ((g.SG, "sh_gate"), (g.SU, "sh_up"), (g.SD, "sh_down")):
                    sp.dma_start(o[:], a[i].rearrange("(c p) f -> p c f", p=P)).then_inc(g.s_sw, 16)

            @block.gpsimd
            def _(pool):
                nc.gpsimd.memset(half[:], -0.5).then_inc(s_half, 1)
                pool.wait_ge(s_half, 1)
                with pool.Fori(0, GN) as t:
                    pool.wait_ge(s_var, t + 1)
                    nc.gpsimd.tensor_tensor(mv[:, :, 4], mv[:, :, 3], half[:], ALU.pow).then_inc(s_r2, 1)
                    pool.wait_ge(s_hn, t * GT + GT)
                    nc.gpsimd.tensor_copy(g.XS[:, bass.ds(t * GT, GT)], hn[:]).then_inc(s_kept, 1)

            @block.tensor
            def _(pe):
                mm = nc.tensor.matmul

                def output(i):
                    pe.wait_ge(s.attc, i + 1)
                    if not first(i):
                        pe.wait_ge(s_x2, i)
                    for k in range(GT):
                        for cc in range(DC):
                            last = mm(ps[:, 3, k * D:(k + 1) * D], s.ATT[:, cc, k * P:(k + 1) * P], W[:, cc], start=cc == 0, stop=cc == DC - 1)
                    last.then_inc(s_h, 1)

                def turn_normed(i):
                    pe.wait_ge(s_hn, i * GT + GT)
                    for k in range(GT):
                        for cc in range(DC):
                            last = nc.tensor.transpose(ps[:, 4, cc * GC + k * P:cc * GC + (k + 1) * P], hn[:, k, cc * P:(cc + 1) * P], g.identF[:])
                    last.then_inc(s_ht, 1)

                def logits(i):
                    pe.wait_ge(s_htc, i + 1)
                    pe.wait_ge(s_lgk, i + 1)
                    for k in range(GT):
                        for cc in range(DC):
                            last = mm(ps[:, 5, k * E:(k + 1) * E], hT[:, cc, k * P:(k + 1) * P], rw[:, cc], start=cc == 0, stop=cc == DC - 1)
                    last.then_inc(s_lg, 1)

                for i in range(2):
                    pe_turn_rows(nc, pe, g, s, i)
                    if i == 1:
                        pe.wait_ge(s_in, 48)
                        output(0)
                    pe_turn_att(nc, pe, g, s, i)

                def trip(t, ahead):
                    if ahead:
                        pe_turn_rows(nc, pe, g, s, t + 2)
                    output(t + 1)
                    turn_normed(t)
                    if ahead:
                        pe_turn_att(nc, pe, g, s, t + 2)
                    logits(t)

                with pe.Fori(0, GN - 2) as t:
                    trip(t, True)
                trip(GN - 2, False)
                turn_normed(GN - 1)
                logits(GN - 1)

            @block.scalar
            def _(act):
                def turned(i):
                    act.wait_ge(s_ht, i + 1)
                    nc.scalar.activation(hT[:], ps[:, 4].rearrange("p (c t) -> p c t", c=DC), ACT.Copy).then_inc(s_htc, 1)
                    act.wait_ge(s_htc, i + 1)
                    nc.scalar.activation(g.H2T[:, :, bass.ds(i * GC, GC)], hT[:], ACT.Copy).then_inc(s_h2, 1)
                    act.wait_ge(s_h2, i + 1)

                for i in range(2):
                    act_keep_att(nc, act, g, s, i, s_h)
                with act.Fori(0, GN - 2) as t:
                    turned(t)
                    act_keep_att(nc, act, g, s, t + 2, s_h)
                for i in range(GN - 2, GN):
                    turned(i)

            @block.vector
            def _(dve):
                V = nc.vector
                do = Chain(dve, s_dv)

                def moments(i):
                    dve.wait_ge(s_h, i + 1)
                    if not first(i):
                        dve.wait_ge(s_hn, i * GT)
                    V.tensor_tensor(X2[:], ps[:, 3].rearrange("p (k d) -> p k d", d=D), g.XS[:, bass.ds(i * GT, GT)], ALU.add).then_inc(s_x2, 1)
                    dve.wait_ge(s_x2, i + 1)
                    for k in range(GT):
                        do(V.bn_stats(st[:, k], X2[:, k]), s_apart)
                        do(V.bn_aggr(mv[:, k, 0:2], st[:, k]))
                    do(V.tensor_tensor(mv[:, :, 2], mv[:, :, 0], mv[:, :, 0], ALU.mult))
                    do(V.tensor_tensor(mv[:, :, 2], mv[:, :, 2], mv[:, :, 1], ALU.add))
                    V.tensor_scalar(mv[:, :, 3], mv[:, :, 2], RMS_EPS, None, ALU.add).then_inc(s_var, 1)
                    do(V.tensor_tensor(g.HS[:, bass.ds(i * GT, GT)], g.HS[:, bass.ds(i * GT, GT)], X2[:], ALU.add))

                def rms_norm(i):
                    dve.wait_ge(s_r2, i + 1)
                    if not first(i):
                        dve.wait_ge(s_kept, i)
                        dve.wait_ge(s_ht, i)
                    for k in range(GT):
                        V.scalar_tensor_tensor(hn[:, k], X2[:, k], mv[:, k, 4:5], w2[:], ALU.mult, ALU.mult).then_inc(s_hn, 1)

                def keep_logits(i):
                    dve.wait_ge(s_lg, i + 1)
                    V.tensor_copy(g.LG[:, bass.ds(i * GT, GT)], ps[:, 5, 0:GT * E].rearrange("p (k e) -> p k e", e=E)).then_inc(s_lgk, 1)

                V.memset(g.LG[0:1, 0, 0:1], 0.0).then_inc(s_lgk, 1)
                dve.wait_ge(s_lgk, 1)
                dve_fetch_sums(nc, dve, g, s, 0)
                for i in range(2):
                    dve_divide_heads(nc, dve, g, s, i)
                    dve_fetch_sums(nc, dve, g, s, i + 1)
                moments(0)
                dve.wait_ge(s_in, 48)
                rms_norm(0)

                def trip(t, ahead, fetch):
                    if ahead:
                        dve_divide_heads(nc, dve, g, s, t + 2)
                    if fetch:
                        dve_fetch_sums(nc, dve, g, s, t + 3)
                    moments(t + 1)
                    rms_norm(t + 1)
                    keep_logits(t)

                with dve.Fori(0, GN - 3) as t:
                    do.enter(t, 3 + 2 * GT)
                    trip(t, True, True)
                do.leave(GN - 3)
                trip(GN - 3, True, False)
                trip(GN - 2, False, False)
                keep_logits(GN - 1)


def experts(nc, g, a, outs):
    sem, ps = g.sem, g.ps
    (s_hid, s_sil, s_act_, s_y, s_acc, s_out, s_c, s_m, s_cnt, s_dv, s_pos, s_sc) = (
        sem("ex_" + n) for n in "hidden silu act y acc out consts member count dve places scattered".split())
    (s_xT, s_xTc, s_g, s_u, s_si, s_h, s_hT, s_hTc, s_yd, s_yk, s_fin) = (
        sem("slot_" + n) for n in "xT xTc gate up silu hid hidT hidTc down ykept sum".split())
    s_d, s_e, s_dd, s_ee = (sem("top_" + n) for n in "diff exp diff2 exp2".split())
    s_w = [sem("ex_w" + n) for n in names(E)]
    s_x = [sem("slot_x" + n) for n in names(2)]
    s_yst = [sem("slot_stored" + n) for n in names(2)]
    s_ga = [sem("pick" + n) for n in names(RING)]
    s_o = [sem("out" + n) for n in names(2)]
    NS = SLOTS_X
    with ExitStack() as c:
        def sb(n, sh, dt):
            return c.enter_context(nc.sbuf_tensor("ex_" + n, sh, dt))
        WG, WU, WD = sb("WG", [P, E, DC, F], F32), sb("WU", [P, E, DC, F], F32), sb("WD", [P, E, FC, D], F32)
        SG, SU, SD = g.SG, g.SU, g.SD
        sil, hidS = sb("sil", [P, 2, 512], F32), sb("hidS", [P, FC, 512], F32)
        v8, ix, es = sb("v8", [P, NT, E], F32), sb("ix", [P, NT, E], U32), sb("es", [P, NT, E], F32)
        fx, p, ed, iota = sb("fx", [P, NT, 2], F32), sb("p", [P, NT, 4], F32), sb("ed", [P, NT], F32), sb("iota", [P, E], F32)
        before, ones, place, tile_no = sb("before", [P, P], F32), sb("ones", [P, P], BF16), sb("place", [P, E, NT], F32), sb("tile_no", [1, NS, E], F32)
        befB, mem = sb("befB", [P, P], BF16), sb("mem", [P, E, NT], BF16)
        tot, run, cnt, base = sb("tot", [P, E, NT], F32), sb("run", [P, E, NT], F32), sb("cnt", [P, E], F32), sb("base", [P, E], F32)
        zer, tl, incl, cmp_ = sb("zer", [P, E * NT], F32), sb("tl", [P, E], F32), sb("incl", [P, E], F32), sb("cmp", [P, E, NT], F32)
        pos, pp, pf, pidx = sb("pos", [P, E, NT], F32), sb("pp", [P, NT, E], F32), sb("pf", [P, 2, NT], F32), sb("pidx", [P, 2, NT], U32)
        ce, ef, eid = sb("ce", [1, NS, E], F32), sb("ef", [1, NS], F32), sb("eid", [1, NS], I32)
        XR, xT = sb("XR", [P, 2, D], F32), sb("xT", [P, 2, DC, P], F32)
        sl, hd, hT, Y = sb("sl", [P, 2, F], F32), sb("hd", [P, 2, F], F32), sb("hT", [P, 2, FC, P], F32), sb("Y", [P, 2, D], F32)
        O = sb("O", [P, 2, D], F32)
        G = hidS[:].rearrange("p r (n d) -> p r n d", n=2)
        ov = outs.rearrange("(t p) d -> t p d", p=P)
        with nc.Block() as block:
            @block.sync
            def _(sp):
                for o, i in ((before, "before"), (place, "place"), (tile_no, "tile_no"), (iota, "iota")):
                    sp.dma_start(o[:], a[i]).then_inc(s_c, 16)
                for e in range(E):
                    for o, i in ((WG, "e_gate"), (WU, "e_up"), (WD, "e_down")):
                        sp.dma_start(o[:, e], a[i][e].rearrange("(c p) f -> p c f", p=P)).then_inc(s_w[e], 16)
                sp.wait_ge(s_sc, NT * 2 * 16)
                for n in range(2):
                    sp.dma_start(XR[:, n], g.xs[n * P:(n + 1) * P]).then_inc(s_x[n], 16)

                def load_slot(s, n):
                    sp.wait_ge(s_xT, s - 1)
                    sp.dma_start(XR[:, n], g.xs[bass.ds(s * P, P)]).then_inc(s_x[n], 16)

                def store_slot(s, n):
                    sp.wait_ge(s_yk, s + 2)
                    sp.dma_start(g.ys[bass.ds(s * P, P)], Y[:, n]).then_inc(s_yst[n], 16)

                load_slot(2, 0)
                with sp.Fori(0, NS // 2 - 1) as t:
                    load_slot(2 * t + 3, 1)
                    store_slot(2 * t, 0)
                    load_slot(2 * t + 4, 0)
                    store_slot(2 * t + 1, 1)
                for k in range(NS - 3, NS):
                    store_slot(k, k % 2)
                for n in range(2):
                    sp.wait_ge(s_o[n], NT // 2 * 16)

            @block.gpsimd
            def _(pool):
                pool.wait_ge(s_pos, 1)
                for t in range(NT):
                    for n in range(2):
                        nc.gpsimd.indirect_dma_start(out=g.xs, out_offset=bass.IndirectOffsetOnAxis(ap=pidx[:, n, t:t + 1], axis=0),
                                                     in_=g.XS[:, t], in_offset=None).then_inc(s_sc, 16)
                for n in range(2):
                    pool.wait_ge(s_yst[n], (NS - n + 1) // 2 * 16 + 16)
                for t in range(NT):
                    if t >= RING:
                        pool.wait_ge(s_fin, 2 * (t - RING + 1))
                    for n in range(2):
                        nc.gpsimd.indirect_dma_start(out=G[:, t % RING, n], out_offset=None, in_=g.ys,
                                                     in_offset=bass.IndirectOffsetOnAxis(ap=pidx[:, n, t:t + 1], axis=0)).then_inc(s_ga[t % RING], 16)

            @block.tensor
            def _(pe):
                mm = nc.tensor.matmul

                def up(tg, fs):
                    for f in fs:
                        n = tg * FC + f
                        if n >= 2:
                            pe.wait_ge(s_act_, n - 1)
                        for w, bk in ((SG, 2 * (n % 2)), (SU, 2 * (n % 2) + 1)):
                            for cc in range(DC):
                                last = mm(ps[:, bk], w[:, cc, f * P:(f + 1) * P], g.H2T[:, cc, tg * 512:(tg + 1) * 512], start=cc == 0, stop=cc == 1)
                        last.then_inc(s_hid, 1)

                def down(tg):
                    pe.wait_ge(s_act_, FC * (tg + 1))
                    if tg:
                        pe.wait_ge(s_acc, tg)
                    for k in range(4):
                        for f in range(FC):
                            last = mm(ps[:, 4 + k // 2, (k % 2) * D:(k % 2 + 1) * D], hidS[:, f, k * P:(k + 1) * P], SD[:, f], start=f == 0, stop=f == 3)
                    last.then_inc(s_y, 1)

                pe.wait_ge(g.s_sw, 48)
                up(0, range(FC))
                for tg in range(4):
                    if tg < 3:
                        up(tg + 1, (0,))
                    down(tg)
                    if tg == 0:
                        pe.wait_ge(s_m, 2)
                        memf = mem[:].rearrange("p e t -> p (e t)")
                        mm(ps[:, 7, 0:P], befB[:], memf, start=True, stop=True)
                        mm(ps[:, 7, P:2 * P], ones[:], memf, start=True, stop=True).then_inc(s_cnt, 1)
                    if tg < 3:
                        up(tg + 1, range(1, FC))
                pe.wait_ge(s_acc, 4)
                for e in range(E):
                    pe.wait_ge(s_w[e], 48)
                pe.wait_ge(s_pos, 2)

                flatG, flatU, flatD = (w[:].rearrange("p e c f -> p (e c f)") for w in (WG, WU, WD))

                def turn_x(s, x_done):
                    pe.wait_ge(s_x[x_done[0]], x_done[1])
                    if x_done[2]:
                        pe.wait_ge(s_xTc, s)
                    for cc in range(DC):
                        last = nc.tensor.transpose(ps[:, 6, cc * P:(cc + 1) * P], XR[:, x_done[0], cc * P:(cc + 1) * P], g.identF[:])
                    last.then_inc(s_xT, 1)

                def gate_up(s, n, e):
                    pe.wait_ge(s_xTc, s + 1)
                    for w, bk, s_done in ((flatG, 0, s_g), (flatU, 2, s_u)):
                        for cc in range(DC):
                            last = mm(ps[:, bk + n], xT[:, n, cc], w[:, bass.ds(e + cc * F, F)], start=cc == 0, stop=cc == 1)
                        last.then_inc(s_done, 1)

                def turn_hidden(s, n):
                    pe.wait_ge(s_h, s + 1)
                    for f in range(FC):
                        last = nc.tensor.transpose(ps[:, 4, f * P:(f + 1) * P], hd[:, n, f * P:(f + 1) * P], g.identF[:])
                    last.then_inc(s_hT, 1)

                def down_slot(s, n, e):
                    pe.wait_ge(s_hTc, s + 1)
                    pe.wait_ge(s_yk, s + 1)
                    for f in range(FC):
                        last = mm(ps[:, 5, 0:D], hT[:, n, f], flatD[:, bass.ds(e + f * D, D)], start=f == 0, stop=f == FC - 1)
                    last.then_inc(s_yd, 1)

                def expert_of(s):
                    return pe.value_load(eid[0:1, bass.ds(s, 1)], min_val=0, max_val=(E - 1) * DC * F)

                e = expert_of(0)
                turn_x(0, (0, 16, False))
                gate_up(0, 0, e)
                with pe.Fori(0, NS // 2) as t:
                    es = [expert_of(2 * t + i) for i in range(3)]
                    turn_x(2 * t + 1, (1, t * 16 + 16, True))
                    turn_hidden(2 * t, 0)
                    gate_up(2 * t + 1, 1, es[1])
                    down_slot(2 * t, 0, es[0])
                    turn_x(2 * t + 2, (0, t * 16 + 32, True))
                    turn_hidden(2 * t + 1, 1)
                    gate_up(2 * t + 2, 0, es[2])
                    down_slot(2 * t + 1, 1, es[1])
                turn_hidden(NS - 1, 0)
                down_slot(NS - 1, 0, expert_of(NS - 1))

            @block.scalar
            def _(act):
                A = nc.scalar.activation
                for n in range(4 * FC):
                    if n == FC:
                        act.wait_ge(s_d, 1)
                        A(es[:], es[:], ACT.Exp).then_inc(s_e, 1)
                        act.wait_ge(s_dd, 1)
                        A(ed[:], ed[:], ACT.Exp).then_inc(s_ee, 1)
                    act.wait_ge(s_hid, n + 1)
                    if n >= 2:
                        act.wait_ge(s_act_, n - 1)
                    A(sil[:, n % 2], ps[:, 2 * (n % 2)], ACT.Silu).then_inc(s_sil, 1)

                def rows_gate(s, n):
                    act.wait_ge(s_xT, s + 1)
                    A(xT[:, n], ps[:, 6, 0:D].rearrange("p (c i) -> p c i", c=DC), ACT.Copy).then_inc(s_xTc, 1)
                    act.wait_ge(s_g, s + 1)
                    A(sl[:, n], ps[:, n], ACT.Silu).then_inc(s_si, 1)

                rows_gate(0, 0)
                with act.Fori(0, NS // 2) as t:
                    rows_gate(2 * t + 1, 1)
                    rows_gate(2 * t + 2, 0)
                for t in range(NT):
                    act.wait_ge(s_fin, 2 * t + 2)
                    act.dma_start(ov[t], O[:, t % 2]).then_inc(s_o[t % 2], 16)

            @block.vector
            def _(dve):
                V = nc.vector
                do = Chain(dve, s_dv)

                def acc(tg):
                    dve.wait_ge(s_y, tg + 1)
                    V.tensor_tensor(g.HS[:, 4 * tg:4 * tg + 4], ps[:, 4:6].rearrange("p a (k d) -> p (a k) d", d=D),
                                    g.HS[:, 4 * tg:4 * tg + 4], ALU.add).then_inc(s_acc, 1)

                for n in range(2):
                    V.memset(Y[0:1, n, 0:1], 0.0).then_inc(s_yst[n], 16)
                V.memset(sl[0:1, 0, 0:1], 0.0).then_inc(s_yk, 1)
                flat = lambda x: x[:].rearrange("p e t -> p (e t)")
                per_e = lambda x: x[:].unsqueeze(2).to_broadcast([P, E, NT])

                def largest(f):
                    for t in range(f * NT // FC, (f + 1) * NT // FC):
                        do(V.max(v8[:, t], g.LG[:, t]))
                        do(V.max_index(ix[:, t], v8[:, t], g.LG[:, t]))

                def picks():
                    V.tensor_tensor(es[:], v8[:], v8[:, :, 0:1].to_broadcast([P, NT, E]), ALU.subtract).then_inc(s_d, 1)
                    do(V.tensor_copy(fx[:], ix[:, :, 0:2]))
                    dve.wait_ge(s_c, 64)
                    for n in range(2):
                        do(V.tensor_tensor(g.pick[:, n], iota[:].unsqueeze(1).to_broadcast([P, NT, E]),
                                           fx[:, :, n:n + 1].to_broadcast([P, NT, E]), ALU.is_equal))
                    V.memset(ones[:], 1.0).then_inc(s_m, 1)
                    do(V.memset(zer[:], 0.0))
                    do(V.tensor_copy(befB[:], before[:]))
                    V.tensor_tensor(mem[:].rearrange("p e t -> p t e"), g.pick[:, 0], g.pick[:, 1], ALU.add).then_inc(s_m, 1)
                    dve.wait_ge(s_e, 1)
                    do(V.reduce_sum(p[:, :, 0], es[:], AX.X))
                    do(V.reciprocal(p[:, :, 1], p[:, :, 0]))
                    do(V.tensor_tensor(p[:, :, 2], es[:, :, 1], p[:, :, 1], ALU.mult))
                    V.tensor_tensor(ed[:], p[:, :, 2], p[:, :, 1], ALU.subtract).then_inc(s_dd, 1)
                    dve.wait_ge(s_ee, 1)
                    do(V.tensor_scalar(p[:, :, 3], ed[:], 1.0, None, ALU.add))
                    do(V.reciprocal(g.share[:, :, 0], p[:, :, 3]))
                    do(V.tensor_tensor(g.share[:, :, 1], g.share[:, :, 0], ed[:], ALU.mult))

                def places():
                    dve.wait_ge(s_cnt, 1)
                    do(V.tensor_copy(flat(tot), ps[:, 7, P:2 * P]))
                    do(V.tensor_tensor_scan(flat(run), flat(tot), zer[:], 0.0, ALU.add, ALU.add))
                    do(V.memset(base[:, 0:1], 0.0))
                    do(V.tensor_copy(base[:, 1:E], run[:, 0:E - 1, NT - 1]))
                    do(V.tensor_tensor(cnt[:], run[:, :, NT - 1], base[:], ALU.subtract))
                    do(V.tensor_tensor(cmp_[:], per_e(cnt), place[:], ALU.is_gt))
                    do(V.reduce_sum(tl[:], cmp_[:], AX.X))
                    do(V.tensor_tensor_scan(incl[:], tl[:], zer[:, 0:E], 0.0, ALU.add, ALU.add))
                    do(V.tensor_tensor(cnt[:], incl[:], tl[:], ALU.subtract))
                    do(V.scalar_tensor_tensor(base[:], cnt[:], float(P), base[:], ALU.mult, ALU.subtract))
                    do(V.tensor_tensor(pos[:], run[:], tot[:], ALU.subtract))
                    do(V.tensor_tensor(flat(pos), flat(pos), ps[:, 7, 0:P], ALU.add))
                    do(V.tensor_tensor(pos[:], pos[:], per_e(base), ALU.add))
                    for n in range(2):
                        do(V.tensor_tensor(pp[:], pos[:].rearrange("p e t -> p t e"), g.pick[:, n], ALU.mult))
                        do(V.reduce_sum(pf[:, n], pp[:], AX.X))
                    V.tensor_copy(pidx[:], pf[:]).then_inc(s_pos, 1)
                    do(V.tensor_tensor(ce[:], tile_no[:], incl[0:1].unsqueeze(1).to_broadcast([1, NS, E]), ALU.is_ge))
                    do(V.reduce_sum(ef[:], ce[:], AX.X))
                    do(V.tensor_scalar(ef[:], ef[:], float(E - 1), None, ALU.min))
                    do(V.tensor_scalar(ef[:], ef[:], float(DC * F), None, ALU.mult))
                    V.tensor_copy(eid[:], ef[:]).then_inc(s_pos, 1)

                for tg in range(4):
                    for f in range(FC):
                        n = tg * FC + f
                        dve.wait_ge(s_sil, n + 1)
                        if tg:
                            dve.wait_ge(s_y, tg)
                        V.tensor_tensor(hidS[:, f], ps[:, 2 * (n % 2) + 1], sil[:, n % 2], ALU.mult).then_inc(s_act_, 1)
                        if tg == 0:
                            largest(f)
                        elif n == FC:
                            places()
                    if tg == 0:
                        picks()
                    acc(tg)

                def hidden(s, n):
                    dve.wait_ge(s_u, s + 1)
                    dve.wait_ge(s_si, s + 1)
                    V.tensor_tensor(hd[:, n], ps[:, 2 + n], sl[:, n], ALU.mult).then_inc(s_h, 1)

                def keep_turned(s, n):
                    dve.wait_ge(s_hT, s + 1)
                    V.tensor_copy(hT[:, n].rearrange("p f i -> p (f i)"), ps[:, 4]).then_inc(s_hTc, 1)

                def keep_y(s, n, stored):
                    dve.wait_ge(s_yd, s + 1)
                    dve.wait_ge(s_yst[n], stored)
                    V.tensor_copy(Y[:, n], ps[:, 5, 0:D]).then_inc(s_yk, 1)

                hidden(0, 0)
                with dve.Fori(0, NS // 2) as t:
                    keep_turned(2 * t, 0)
                    hidden(2 * t + 1, 1)
                    keep_y(2 * t, 0, t * 16 + 16)
                    keep_turned(2 * t + 1, 1)
                    hidden(2 * t + 2, 0)
                    keep_y(2 * t + 1, 1, t * 16 + 16)
                keep_turned(NS - 1, 0)
                keep_y(NS - 1, 0, NS // 2 * 16 + 16)
                for t in range(NT):
                    dve.wait_ge(s_ga[t % RING], (t // RING + 1) * 32)
                    if t >= 2:
                        dve.wait_ge(s_o[t % 2], t // 2 * 16)
                    V.scalar_tensor_tensor(O[:, t % 2], G[:, t % RING, 0], g.share[:, t, 0:1], g.HS[:, t], ALU.mult, ALU.add).then_inc(s_fin, 1)
                    dve.wait_ge(s_fin, 2 * t + 1)
                    V.scalar_tensor_tensor(O[:, t % 2], G[:, t % RING, 1], g.share[:, t, 1:2], O[:, t % 2], ALU.mult, ALU.add).then_inc(s_fin, 1)


def kernel(**inputs):
    import numpy as np
    import concourse.bacc as bacc
    from concourse.bass_utils import run_bass_kernel_spmd

    def given(name):
        return np.asarray(inputs[name])

    def rows(w):
        return np.ascontiguousarray(w.reshape(DC, P, -1).transpose(1, 0, 2))

    sel = np.zeros((B, B, L3), np.float32)
    sel[np.arange(B), np.arange(B)] = 1
    arrays = dict(
        before=np.triu(np.ones((P, P), np.float32), 1),
        place=np.ascontiguousarray(np.broadcast_to(P * np.arange(NT, dtype=np.float32), (P, E, NT))),
        tile_no=np.repeat(np.arange(SLOTS_X, dtype=np.float32), E).reshape(1, SLOTS_X, E),
        x=given("x"), sel=sel, lvl=(np.arange(L3) % L).astype(np.float32)[:, None].copy(),
        iota=np.ascontiguousarray(np.broadcast_to(np.arange(E, dtype=np.float32), (P, E))),
        er=np.ascontiguousarray(given("L0_attn_Er")[::-1].reshape(4, P, DK).transpose(1, 0, 2)), emb=given("L0_tok_level_emb"),
        ident=np.eye(P, dtype=np.float32), bo=np.ascontiguousarray(np.broadcast_to(given("L0_attn_bo"), (L, D))),
        bias=np.ascontiguousarray(np.broadcast_to(np.stack([given("L0_attn_b" + k) for k in "qkv"]), (L, 3, D))),
        w1=np.ascontiguousarray(np.broadcast_to(given("L0_ffn_norm1_w"), (P, D))),
        w2=np.ascontiguousarray(np.broadcast_to(given("L0_ffn_norm2_w"), (P, D))),
        **{k + "T": rows(given("L0_attn_" + k).T) for k in ("Wq", "Wk", "Wv", "Wo")},
        **{k: rows(given("L0_ffn_" + k)) for k in ("wq", "wk", "wv", "wo")},
        rw=rows(given("L0_ffn_router_w")),
        **{k: given("L0_ffn_" + k) for k in ("sh_gate", "sh_up", "sh_down", "e_gate", "e_up", "e_down")})
    nc = bacc.Bacc("TRN2", target_bir_lowering=False, num_devices=1)
    aps = {n: nc.dram_tensor("in_" + n, v.shape, mybir.dt.from_np(v.dtype), kind="ExternalInput").ap() for n, v in arrays.items()}
    out = nc.dram_tensor("out", [T, D], F32, kind="ExternalOutput").ap()
    build_program(nc, aps, out)
    r = run_bass_kernel_spmd(nc, [{"in_" + n: v for n, v in arrays.items()}], core_ids=[0])
    return r.results[0]["out"].reshape(B, S, D)
```
